# Optimizing a Trainium2 kernel written in Bass

```python
import numpy as np
import jax
import jax.numpy as jnp

def _softmax(x, axis=-1):
    return jax.nn.softmax(x, axis=axis)

def _gelu(x):
    return jax.nn.gelu(x, approximate=True)

def _silu(x):
    return jax.nn.silu(x)

def _sigmoid(x):
    return jax.nn.sigmoid(x)

def _layernorm(x, axis=-1, eps=1e-05):
    m = jnp.mean(x, axis=axis, keepdims=True)
    v = jnp.var(x, axis=axis, keepdims=True)
    return (x - m) / jnp.sqrt(v + eps)

def _scatter_add(tgt, idx, src, axis=0):
    return tgt.at[idx].add(src)

def _segment_sum(src, seg, n):
    return jax.ops.segment_sum(src, seg, n)
kernel_name = 'mk_adj_preln_d4_adj_r2_d4ff24'

def setup_inputs(seed: int=0):
    np.random.seed(seed)
    _w = jnp.asarray

    def _rec_inputs():
        import jax
        import jax.numpy as jnp
        _gk = jax.random.key(seed)
        x = -0.0005207 + 1.001 * jax.random.normal(jax.random.fold_in(_gk, 1), (16, 512, 128), jnp.float32)
        _a = jax.random.bernoulli(jax.random.fold_in(_gk, 2), 0.00390625, (512, 512))
        _a = jnp.logical_or(_a, jnp.eye(512, dtype=bool))
        _af = _a.astype(jnp.float32)
        _af = _af * jax.random.uniform(jax.random.fold_in(_gk, 3), (512, 512), jnp.float32, 0.05, 1.99371)
        adj = _af
        return (x, adj)
    x, adj = _rec_inputs()

    def _L0_gnn_setup():
        import jax, jax.numpy as jnp
        import numpy as np
        B, M, IN, HID, OUT = (8, 1024, 128, 128, 128)
        LN_EPS = 1e-05

        def _layernorm(x, g, b):
            mu = jnp.mean(x, axis=-1, keepdims=True)
            var = jnp.mean((x - mu) ** 2, axis=-1, keepdims=True)
            return (x - mu) * jax.lax.rsqrt(var + LN_EPS) * g + b
        key = jax.random.key(seed)
        ks = jax.random.split(key, 10)
        x = jax.random.normal(ks[0], (B, M, IN), dtype=jnp.float32)
        vals = jax.random.uniform(ks[1], (M, M), dtype=jnp.float32)
        keep = jax.random.uniform(ks[2], (M, M)) < 0.03
        A_final = jnp.where(keep, vals, 0.0) + jnp.eye(M, dtype=jnp.float32)
        s = 0.02
        return {'x': x, 'A_final': A_final, 'Wp': jax.random.normal(ks[3], (IN, HID), jnp.float32) * s, 'bp': jnp.zeros((HID,), jnp.float32), 'a_src': jax.random.normal(ks[4], (HID,), jnp.float32) * s, 'a_dst': jax.random.normal(ks[5], (HID,), jnp.float32) * s, 'gat_g': jnp.ones((HID,), jnp.float32), 'gat_b': jnp.zeros((HID,), jnp.float32), 'eps': jnp.zeros((1,), jnp.float32), 'W1': jax.random.normal(ks[6], (HID, HID), jnp.float32) * s, 'b1': jnp.zeros((HID,), jnp.float32), 'mlp_g': jnp.ones((HID,), jnp.float32), 'mlp_b': jnp.zeros((HID,), jnp.float32), 'W2': jax.random.normal(ks[7], (HID, OUT), jnp.float32) * s, 'b2': jnp.zeros((OUT,), jnp.float32)}
    _L0_gnn_all = _L0_gnn_setup()
    _L0_gnn_in = {k: v for k, v in _L0_gnn_all.items() if k in ('Wp', 'bp', 'a_src', 'a_dst', 'gat_g', 'gat_b', 'eps', 'W1', 'b1', 'mlp_g', 'mlp_b', 'W2', 'b2')}
    del _L0_gnn_all

    def _L1_gnn_setup():
        import jax, jax.numpy as jnp
        import numpy as np
        NEG = -9000000000000000.0
        key = jax.random.key(seed)
        k1, k2, k3, k4 = jax.random.split(key, 4)
        B, N, F_in, F_out, MAX_E = (8192, 16, 128, 128, 128)
        inp = jax.random.normal(k1, (B, N, F_in), dtype=jnp.float32)
        adj = jax.random.uniform(k2, (N, N), dtype=jnp.float32)
        limit = 1.414 * np.sqrt(6.0 / (F_in + F_out))
        W = jax.random.uniform(k3, (2, F_in, F_out), dtype=jnp.float32, minval=-limit, maxval=limit)
        e = jnp.ones((1, MAX_E), dtype=jnp.float32)
        stdv = 1.0 / np.sqrt(F_out)
        bias = jax.random.uniform(k4, (F_out,), dtype=jnp.float32, minval=-stdv, maxval=stdv)
        return {'input': inp, 'adj': adj, 'W': W, 'e': e, 'bias': bias}
    _L1_gnn_all = _L1_gnn_setup()
    _L1_gnn_in = {k: v for k, v in _L1_gnn_all.items() if k in ('W', 'e', 'bias')}
    del _L1_gnn_all

    def _L2_gnn_setup():
        import jax, jax.numpy as jnp
        import numpy as np
        B, N, CIN, COUT, K = (8192, 17, 128, 128, 3)

        def _cheb_basis(adj):
            n = adj.shape[0]
            d_inv_sqrt = jnp.sum(adj, axis=-1) ** (-0.5)
            eye = jnp.eye(n, dtype=adj.dtype)
            L = eye - d_inv_sqrt[:, None] * adj * d_inv_sqrt[None, :]
            T2 = 2.0 * (L @ L) - eye
            return jnp.stack([eye, L, T2])
        key = jax.random.key(seed)
        kx, ka, kw = jax.random.split(key, 3)
        x = jax.random.normal(kx, (B, N, CIN), dtype=jnp.float32)
        adj = jax.random.uniform(ka, (N, N), dtype=jnp.float32)
        weight = jax.random.normal(kw, (K, 1, CIN, COUT), dtype=jnp.float32) * 0.05
        bias = jnp.zeros((1, 1, COUT), dtype=jnp.float32)
        return {'x': x, 'adj': adj, 'weight': weight, 'bias': bias}
    _L2_gnn_all = _L2_gnn_setup()
    _L2_gnn_in = {k: v for k, v in _L2_gnn_all.items() if k in ('weight', 'bias')}
    del _L2_gnn_all

    def _L3_gnn_setup():
        import jax, jax.numpy as jnp
        import numpy as np
        B, N, F_IN, F_OUT = (8, 1024, 128, 128)
        ALPHA = 0.1
        NEG_BIG = -9000000000000000.0

        def _pair_indices(n):
            m = jnp.arange(n)[:, None] * n + jnp.arange(n)[None, :]
            nn = n * n
            k1, k2 = (2 * m, 2 * m + 1)
            idx1 = jnp.where(k1 < nn, k1 // n, k1 % n)
            idx2 = jnp.where(k2 < nn, k2 // n, k2 % n)
            return (idx1, idx2)
        key = jax.random.key(seed)
        k1, k2, k3, k4 = jax.random.split(key, 4)
        x = jax.random.normal(k1, (B, N, F_IN), dtype=jnp.float32)
        adj = jnp.ones((N, N), dtype=jnp.float32) - jnp.eye(N, dtype=jnp.float32)
        others_weight = jax.random.normal(k2, (F_IN, F_OUT), dtype=jnp.float32) * (1.0 / np.sqrt(F_OUT))
        self_weight = jax.random.normal(k3, (F_IN, F_OUT), dtype=jnp.float32) * (1.0 / np.sqrt(F_OUT))
        att_weight = jax.random.normal(k4, (2 * F_OUT, 1), dtype=jnp.float32)
        return {'x': x, 'adj': adj, 'others_weight': others_weight, 'self_weight': self_weight, 'att_weight': att_weight}
    _L3_gnn_all = _L3_gnn_setup()
    _L3_gnn_in = {k: v for k, v in _L3_gnn_all.items() if k in ('others_weight', 'self_weight', 'att_weight')}
    del _L3_gnn_all
    return {'x': x, 'adj': adj, 'L0_gnn_Wp': _L0_gnn_in['Wp'], 'L0_gnn_bp': _L0_gnn_in['bp'], 'L0_gnn_a_src': _L0_gnn_in['a_src'], 'L0_gnn_a_dst': _L0_gnn_in['a_dst'], 'L0_gnn_gat_g': _L0_gnn_in['gat_g'], 'L0_gnn_gat_b': _L0_gnn_in['gat_b'], 'L0_gnn_eps': _L0_gnn_in['eps'], 'L0_gnn_W1': _L0_gnn_in['W1'], 'L0_gnn_b1': _L0_gnn_in['b1'], 'L0_gnn_mlp_g': _L0_gnn_in['mlp_g'], 'L0_gnn_mlp_b': _L0_gnn_in['mlp_b'], 'L0_gnn_W2': _L0_gnn_in['W2'], 'L0_gnn_b2': _L0_gnn_in['b2'], 'L1_gnn_W': _L1_gnn_in['W'], 'L1_gnn_e': _L1_gnn_in['e'], 'L1_gnn_bias': _L1_gnn_in['bias'], 'L2_gnn_weight': _L2_gnn_in['weight'], 'L2_gnn_bias': _L2_gnn_in['bias'], 'L3_gnn_others_weight': _L3_gnn_in['others_weight'], 'L3_gnn_self_weight': _L3_gnn_in['self_weight'], 'L3_gnn_att_weight': _L3_gnn_in['att_weight']}

def reference(x, adj, L0_gnn_Wp, L0_gnn_bp, L0_gnn_a_src, L0_gnn_a_dst, L0_gnn_gat_g, L0_gnn_gat_b, L0_gnn_eps, L0_gnn_W1, L0_gnn_b1, L0_gnn_mlp_g, L0_gnn_mlp_b, L0_gnn_W2, L0_gnn_b2, L1_gnn_W, L1_gnn_e, L1_gnn_bias, L2_gnn_weight, L2_gnn_bias, L3_gnn_others_weight, L3_gnn_self_weight, L3_gnn_att_weight):
    import jax
    import jax.numpy as jnp

    def _L0_gnn_ref(x, A_final, Wp, bp, a_src, a_dst, gat_g, gat_b, eps, W1, b1, mlp_g, mlp_b, W2, b2):
        import jax, jax.numpy as jnp
        import numpy as np
        B, M, IN, HID, OUT = (8, 1024, 128, 128, 128)
        LN_EPS = 1e-05

        def _layernorm(x, g, b):
            mu = jnp.mean(x, axis=-1, keepdims=True)
            var = jnp.mean((x - mu) ** 2, axis=-1, keepdims=True)
            return (x - mu) * jax.lax.rsqrt(var + LN_EPS) * g + b
        h = jnp.einsum('bmi,ih->bmh', x, Wp) + bp
        s_src = jnp.einsum('bmh,h->bm', h, a_src)
        s_dst = jnp.einsum('bmh,h->bm', h, a_dst)
        scores = s_src[:, :, None] + s_dst[:, None, :]
        scores = jnp.where(scores >= 0, scores, 0.2 * scores)
        fill = jnp.finfo(scores.dtype).min
        scores = jnp.where((A_final <= 0)[None], fill, scores)
        attn = jax.nn.softmax(scores, axis=-1)
        weighted_adj = attn * A_final[None]
        h_gat = jnp.einsum('bmn,bnh->bmh', weighted_adj, h)
        h_gat = jax.nn.relu(_layernorm(h_gat, gat_g, gat_b))
        h_agg = jnp.einsum('mn,bnh->bmh', A_final, h_gat)
        h_gin = (1.0 + eps) * h_gat + h_agg
        z = jnp.einsum('bmh,hk->bmk', h_gin, W1) + b1
        z = jax.nn.relu(_layernorm(z, mlp_g, mlp_b))
        x_gin = jnp.einsum('bmk,ko->bmo', z, W2) + b2
        return jax.nn.relu(x_gin + h_gat)

    def _L1_gnn_ref(input, adj, W, e, bias):
        import jax, jax.numpy as jnp
        import numpy as np
        NEG = -9000000000000000.0
        h0 = jnp.einsum('bnf,fg->bng', input, W[0])
        h1 = jnp.einsum('bnf,fg->bng', input, W[1])
        m = adj > 0
        idx = jnp.cumsum(m.reshape(-1).astype(jnp.int32)) - 1
        vals = e[0][idx].reshape(adj.shape)
        A = jnp.where(m, vals, jnp.float32(NEG))
        A = jax.nn.softmax(A, axis=1)
        M = jnp.eye(adj.shape[0], dtype=A.dtype)
        out = jnp.einsum('ij,bjg->big', A * M, h0) + jnp.einsum('ij,bjg->big', A * (1.0 - M), h1)
        return out + bias[None, None, :]

    def _L2_gnn_ref(x, adj, weight, bias):
        import jax, jax.numpy as jnp
        import numpy as np
        B, N, CIN, COUT, K = (8192, 17, 128, 128, 3)

        def _cheb_basis(adj):
            n = adj.shape[0]
            d_inv_sqrt = jnp.sum(adj, axis=-1) ** (-0.5)
            eye = jnp.eye(n, dtype=adj.dtype)
            L = eye - d_inv_sqrt[:, None] * adj * d_inv_sqrt[None, :]
            T2 = 2.0 * (L @ L) - eye
            return jnp.stack([eye, L, T2])
        mul_L = _cheb_basis(adj)
        h = jnp.einsum('knm,bmc->kbnc', mul_L, x)
        h = jnp.einsum('kbnc,kcd->kbnd', h, weight[:, 0])
        out = jnp.sum(h, axis=0) + bias
        return jax.nn.relu(out)

    def _L3_gnn_ref(x, adj, others_weight, self_weight, att_weight):
        import jax, jax.numpy as jnp
        import numpy as np
        B, N, F_IN, F_OUT = (8, 1024, 128, 128)
        ALPHA = 0.1
        NEG_BIG = -9000000000000000.0

        def _pair_indices(n):
            m = jnp.arange(n)[:, None] * n + jnp.arange(n)[None, :]
            nn = n * n
            k1, k2 = (2 * m, 2 * m + 1)
            idx1 = jnp.where(k1 < nn, k1 // n, k1 % n)
            idx2 = jnp.where(k2 < nn, k2 // n, k2 % n)
            return (idx1, idx2)
        b, n, _ = x.shape
        f_out = others_weight.shape[1]
        h = x @ others_weight
        a1 = att_weight[:f_out, 0]
        a2 = att_weight[f_out:, 0]
        u1 = h @ a1
        u2 = h @ a2
        idx1, idx2 = _pair_indices(n)
        e = u1[:, idx1] + u2[:, idx2]
        e = jnp.where(e >= 0, e, ALPHA * e)
        att = jnp.where(adj > 0, e, NEG_BIG)
        att = jax.nn.softmax(att, axis=1)
        out = jnp.einsum('bik,bkl->bil', att, h)
        out = out + x @ self_weight
        return out
    h = jnp.maximum(_layernorm(x, axis=-1), 0.0)
    x = x + _L0_gnn_ref(h, adj, L0_gnn_Wp, L0_gnn_bp, L0_gnn_a_src, L0_gnn_a_dst, L0_gnn_gat_g, L0_gnn_gat_b, L0_gnn_eps, L0_gnn_W1, L0_gnn_b1, L0_gnn_mlp_g, L0_gnn_mlp_b, L0_gnn_W2, L0_gnn_b2)
    h = jnp.maximum(_layernorm(x, axis=-1), 0.0)
    x = x + _L1_gnn_ref(h, adj, L1_gnn_W, L1_gnn_e, L1_gnn_bias)
    h = jnp.maximum(_layernorm(x, axis=-1), 0.0)
    x = x + _L2_gnn_ref(h, adj, L2_gnn_weight, L2_gnn_bias)
    h = jnp.maximum(_layernorm(x, axis=-1), 0.0)
    x = x + _L3_gnn_ref(h, adj, L3_gnn_others_weight, L3_gnn_self_weight, L3_gnn_att_weight)
    return x

_drawn_inputs = setup_inputs


def setup_inputs(seed=0):
    import zlib

    import numpy as np

    out = dict(_drawn_inputs(seed))
    spreads = {'L0_gnn_bp': (0.0, 0.1),
     'L0_gnn_gat_g': (1.0, 0.2),
     'L0_gnn_gat_b': (0.0, 0.1),
     'L0_gnn_b1': (0.0, 0.315),
     'L0_gnn_mlp_g': (1.0, 0.573),
     'L0_gnn_mlp_b': (0.0, 0.683),
     'L0_gnn_b2': (0.0, 0.1),
     'L1_gnn_e': (1.0, 0.6),
     'L2_gnn_bias': (0.0, 0.1)}
    factors = {'L0_gnn_a_src': 64.0, 'L0_gnn_a_dst': 31.759}
    for name, (base, spread) in spreads.items():
        noise = np.random.default_rng([zlib.crc32(name.encode()), seed]).standard_normal(out[name].shape)
        drawn = base * np.exp(spread * noise) if base else spread * noise
        out[name] = jnp.asarray(drawn.astype(out[name].dtype))
    for name, factor in factors.items():
        out[name] = (out[name] * factor).astype(out[name].dtype)
    return out
```

```python
from contextlib import ExitStack

import concourse.bass as bass
from concourse import mybir

P = 128
ALU = mybir.AluOpType
ACT = mybir.ActivationFunctionType
F32 = mybir.dt.float32
F16 = mybir.dt.float16
AX_X = mybir.AxisListType.X

FLOAT_MIN = -3.4028234663852886e38
NEG_BIG = -9.0e15
LN_EPS = 1e-5
WS = 64.0


def build(nc, x, adj, Wp, bp, a_src, a_dst, gat_g, gat_b, eps, W1, b1, mlp_g, mlp_b, W2, b2,
          L1_W, L1_e, L1_bias, L2_weight, L2_bias, L3_others, L3_self, L3_att, out):
    B, N, D = x.shape
    T = N // P
    H = N // 2
    TH = T // 2
    assert D == P and N == 512 and L1_e.shape[1] == P

    WP, WZ, WO2, L1A, L1B, L2A, L2B, L2C, L3O, L3S = range(10)
    (R_BP, R_ASRC, R_ADST, R_GG, R_GB, R_B1, R_MG, R_MB, R_B2, R_L1, R_L2, R_A1, R_A2) = range(13)

    with ExitStack() as ctx:
        def sb(name, shape, dt=F32):
            return ctx.enter_context(nc.sbuf_tensor(name, shape, dt))

        def ps(name, shape=(P, 512), dt=F32):
            return ctx.enter_context(nc.psum_tensor(name, list(shape), dt))

        x_all = sb("x_all", [P, B, T, P])
        adj_n = sb("adj_n", [P, T, N])
        adj_t = sb("adj_t", [P, T, N])
        gat_mask = sb("gat_mask", [P, T, N])
        pair_mask = sb("pair_mask", [P, T, H])
        late_mask = sb("late_mask", [P, T, H], F16)
        late_neg = sb("late_neg", [P, T])
        late_cnt = sb("late_cnt", [P, T])
        gin_t = sb("gin_t", [P, 2, T, N], F16)
        att_t = sb("att_t", [P, 2, T, N], F16)
        att_d = sb("att_d", [P, 2, T, P], F16)
        lap_t = sb("lap_t", [P, 2, T, N], F16)
        cheb_t = sb("cheb_t", [P, 2, T, N], F16)
        w_raw = sb("w_raw", [P, 10, P])
        w_hl = sb("w_hl", [P, 2, 10, P], F16)
        rows = sb("rows", [P, 13, P])
        e_col = sb("e_col", [P, 1])
        e_last = sb("e_last", [P, 1])
        eps1 = sb("eps1", [P, 1])
        ident = sb("ident", [P, P])
        ident16 = sb("ident16", [P, P], F16)
        ones = sb("ones", [P, P])
        mhalf = sb("mhalf", [P, T])
        score_w = sb("score_w", [P, 6])
        col_hl = sb("col_hl", [P, 2, 4], F16)
        dst_hl = sb("dst_hl", [P, 2, P], F16)
        pair_hl = sb("pair_hl", [P, 2, P], F16)
        work = sb("work", [P, 3 * T * N])

        def area(at, per_part, inner):
            return work[:, at:at + per_part * inner].rearrange("p (a b) -> p a b", b=inner)

        wk1, wk2, wk3 = (area(k * T * N, T, N) for k in range(3))
        x2, x3, x4, xb, b_t, b_g, b_g2 = (area(k * T * P, T, P) for k in range(7))
        b_te, b_e = (area(7 * T * P + k * T * H, T, H) for k in range(2))
        tri = sb("tri", [P, P])
        kcol = sb("kcol", [P, 1])
        krow = sb("krow", [P, P])
        small = sb("small", [P, 16, T])
        pick_t = sb("pick_t", [P, T, P], F16)
        q16 = sb("q16", [P, T, N], F16)

        a_stats = sb("a_stats", [P, T, 6])
        a_mv = sb("a_mv", [P, T, 2])
        a_rstd = sb("a_rstd", [P, 4, T])
        a_y = sb("a_y", [P, T, P])
        a_y2 = sb("a_y2", [P, T, P])
        a_fT = sb("a_fT", [P, 2, N], F16)
        a_h1 = sb("a_h1", [P, T, P])
        a_s = sb("a_s", [P, 8, T])
        a_t = sb("a_t", [P, T, N])
        a_e = sb("a_e", [P, T, N])
        a_pt = sb("a_pt", [P, T, N])
        a_hg = sb("a_hg", [P, T, P])
        a_hghl = sb("a_hghl", [P, 2, T, P], F16)
        a_hb = sb("a_hb", [P, T, P])
        a_z = sb("a_z", [P, T, P])
        x1 = sb("x1", [P, T, P])
        b_stats = sb("b_stats", [P, T, 6])
        b_mv = sb("b_mv", [P, T, 2])
        b_rstd = sb("b_rstd", [P, 2, T])
        b_y = sb("b_y", [P, T, P])
        b_h = sb("b_h", [P, 2, T, P], F16)
        b_hT = sb("b_hT", [P, 2, N], F16)
        b_m1 = sb("b_m1", [P, 2, N], F16)
        b_m2 = sb("b_m2", [P, 2, N], F16)
        b_lv = sb("b_lv", [P, 2, H])
        b_lw = sb("b_lw", [P, 2])
        b_s = sb("b_s", [P, 12, T])
        b_g2hl = sb("b_g2hl", [P, 2, T, P], F16)

        pa = [ps(f"pa{i}") for i in range(4)]
        pb = [ps(f"pb{i}") for i in range(4)]
        pb3h = pb[3][:, :].bitcast(F16).rearrange("p (h n) -> p h n", h=2)

        pair_view = pb[0][:].rearrange("p (i c) -> p c i", c=2)

        names = """adj_loaded w_loaded rows_loaded x0_loaded x_loaded consts waits_passed
            pool_chain dve_chain adj_turned w_hi score_weights row_counts row_starts pick_ready picked
            edge_values spread edge_max edge_exp att_rows att_turned degrees degree_roots d_diag d_spread
            lap_rows lap_turned lap_cols lap_squared prepared
            a_stats a_mv a_var a_rstd a_y a_turned a_hi a_lo a_proj a_h1 a_max a_negmax a_relu a_lrelu a_exp
            a_eturned a_weighed a_heads a_recip a_r2 a_v1 a_v2 a_v3 a_norm a_scaled a_g1 a_g2 a_hg a_hghi
            a_hglo a_hb a_agg a_ghi a_glo a_z a_z1 a_zg1 a_zg2 a_zturned a_zhi a_zlo a_out a_t1 x1_done
            b_stats b_mv b_var b_rstd b_y b_hi b_lo b_xb b_agg b_agghi b_agglo b_mixed x2_done
            b_turned b_hT b_cheb b_chebhi b_cheblo b_mixed2 b_t x3_done
            b_turned3 b_hT3 b_proj b_tenth b_lv b_lw b_m2 b_pmax b_nmx b_exp b_sc b_den b_rc b_gs b_gs2 b_g2hi b_g2lo
            b_final x4_done out_stored""".split()
        S = {n: ctx.enter_context(nc.semaphore(n)) for n in names}

        block = ctx.enter_context(nc.Block())

        def flat(ap):
            return ap.rearrange("p t d -> p (t d)")

        def row4(r):
            return rows[:, r:r + 1, :].broadcast_to([P, T, P])

        def node_view(dram):
            return dram.rearrange("(t p) d -> p t d", p=P)

        def since(eng, sem, q, per, k):
            if isinstance(q, int) and per * q + k <= 0:
                return
            eng.wait_ge(sem, per * q + k)

        def since_apart(eng, sem, q, per, k):
            since(eng, sem, q, per, k)
            if not isinstance(q, int):
                eng.sem_inc(S["waits_passed"], 1)

        ORDER = [("a", 0), ("b", 0), ("a", 1), ("b", 1), ("a", 2), ("b", 2), ("a", 3), ("b", 3), ("b", 4),
                 ("a", 4), ("b", 5), ("b", 6), ("a", 5), ("b", 7), ("a", 6), ("b", 8), ("b", 9), ("a", 7), ("b", 10)]

        def run(eng, stream_a, stream_b, prepare):
            for s, i in ORDER:
                if s == "a":
                    stream_a(0, i)
                    prepare(i)
                    if i == 6:
                        prepare(i + 1)
                        break
            stream_a(0, 7)
            with eng.Fori(0, B - 1) as q:
                for s, i in ORDER:
                    if s == "a":
                        stream_a(q + 1, i)
                    else:
                        stream_b(q, i)
            for s, i in ORDER:
                if s == "b":
                    stream_b(B - 1, i)

        @block.sync
        def _(sp):
            sp.sem_inc(S["out_stored"], 16)
            sp.dma_start(adj_n[:], adj.rearrange("(t p) n -> p t n", p=P)).then_inc(S["adj_loaded"], 16)
            sp.dma_start(x_all[:, 0], node_view(x[0])).then_inc(S["x0_loaded"], 16)
            for k, w in enumerate((Wp, W1, W2, L1_W[0], L1_W[1], L2_weight[0, 0], L2_weight[1, 0],
                                   L2_weight[2, 0], L3_others, L3_self)):
                sp.dma_start(w_raw[:, k, :], w).then_inc(S["w_loaded"], 16)
            sp.dma_start(x_all[:, 1:B].rearrange("p b t d -> p (b t) d"),
                         x[1:B].rearrange("b (t p) d -> p (b t) d", p=P)).then_inc(S["x_loaded"], 16)
            out_v = out.rearrange("b (t p) d -> b p t d", p=P)
            with sp.Fori(0, B) as q:
                sp.wait_ge(S["x4_done"], q + 1)
                sp.dma_start(out_v[q], x4).then_inc(S["out_stored"], 16)
            sp.wait_ge(S["out_stored"], 16 * (B + 1))

        @block.gpsimd
        def _(pool):
            def bcast(v):
                return v.rearrange("(o d) -> o d", o=1).broadcast_to([P, v.shape[0]])

            att_flat = L3_att.rearrange("k o -> (k o)")
            vecs = [bp, a_src, a_dst, gat_g, gat_b, b1, mlp_g, mlp_b, b2, L1_bias,
                    L2_bias.rearrange("a b d -> (a b d)"), att_flat[0:P], att_flat[P:2 * P]]
            for k, v in enumerate(vecs):
                pool.dma_start(rows[:, k, :], bcast(v)).then_inc(S["rows_loaded"], 16)
            pool.dma_start(e_col[:], L1_e.rearrange("o k -> k o")).then_inc(S["rows_loaded"], 16)
            pool.dma_start(e_last[:], L1_e[0:1, P - 1:P].broadcast_to([P, 1])).then_inc(S["rows_loaded"], 16)
            pool.dma_start(eps1[:], eps.rearrange("(o d) -> o d", o=1).broadcast_to([P, 1])).then_inc(
                S["rows_loaded"], 16)

            n = 0

            def link(ins):
                nonlocal n
                n += 1
                ins.then_inc(S["pool_chain"], 1)
                pool.wait_ge(S["pool_chain"], n)

            link(pool.memset(ones[:], 1.0))
            pool.memset(mhalf[:], -0.5)
            link(pool.affine_select(out=ident[:], in_=ones[:], pattern=[[-1, P]], compare_op=ALU.is_equal,
                                    fill=0.0, base=0, channel_multiplier=1))
            pool.affine_select(out=tri[:], in_=ones[:], pattern=[[1, P]], compare_op=ALU.is_gt,
                               fill=0.0, base=0, channel_multiplier=-1)
            pool.iota(kcol[:], pattern=[[0, 1]], base=0, channel_multiplier=1,
                      allow_small_or_imprecise_dtypes=True)
            pool.iota(krow[:], pattern=[[1, P]], base=0, channel_multiplier=0,
                      allow_small_or_imprecise_dtypes=True)
            pool.tensor_copy(ident16[:], ident[:]).then_inc(S["consts"], 1)

            def rstd(q, per, k, mv, var, out_, s_mv, s_var, s_rstd):
                since_apart(pool, s_mv, q, per, k + 1)
                pool.tensor_scalar(var, mv[:, :, 1], LN_EPS, None, ALU.add).then_inc(s_var, 1)
                pool.wait_ge(s_var, per * q + k + 1)
                pool.tensor_tensor(out_, var, mhalf[:], ALU.pow).then_inc(s_rstd, 1)

            def a_rstd_of(q, k):
                rstd(q, 3, k, a_mv, a_rstd[:, 0], a_rstd[:, 1], S["a_mv"], S["a_var"], S["a_rstd"])

            def a_gat_norm(q):
                pool.wait_ge(S["a_recip"], q + 1)
                pool.tensor_tensor(a_s[:, 7], a_s[:, 6], a_s[:, 6], ALU.mult).then_inc(S["a_r2"], 1)
                pool.wait_ge(S["a_r2"], q + 1)
                pool.wait_ge(S["a_mv"], 3 * q + 2)
                pool.tensor_tensor(a_rstd[:, 2], a_mv[:, :, 1], a_s[:, 7], ALU.mult).then_inc(S["a_v1"], 1)
                since_apart(pool, S["a_v1"], q, 1, 1)
                pool.tensor_scalar(a_rstd[:, 0], a_rstd[:, 2], LN_EPS, None, ALU.add).then_inc(S["a_var"], 1)
                pool.wait_ge(S["a_var"], 3 * q + 2)
                pool.tensor_tensor(a_rstd[:, 3], a_rstd[:, 0], mhalf[:], ALU.pow).then_inc(S["a_v2"], 1)
                pool.wait_ge(S["a_v2"], q + 1)
                pool.tensor_tensor(a_rstd[:, 1], a_rstd[:, 3], a_s[:, 6], ALU.mult).then_inc(S["a_rstd"], 1)

            def affine(q, k, g, b):
                pool.wait_ge(S["a_y"], 3 * q + k + 1)
                pool.tensor_tensor(a_y2[:], a_y[:], row4(g), ALU.mult).then_inc(S["a_g1"], 1)
                pool.wait_ge(S["a_g1"], 2 * q + k)
                pool.tensor_tensor(a_y2[:], a_y2[:], row4(b), ALU.add).then_inc(S["a_g2"], 1)

            def a_residual(q):
                pool.wait_ge(S["a_hg"], q + 1)
                pool.tensor_tensor(a_hb[:], a_hg[:], row4(R_B2), ALU.add).then_inc(S["a_hb"], 1)

            def b_rstd_of(q, k):
                rstd(q, 3, k, b_mv, b_rstd[:, 0], b_rstd[:, 1], S["b_mv"], S["b_var"], S["b_rstd"])

            def b_bias(q):
                pool.wait_ge(S["x1_done"], q + 1)
                pool.tensor_tensor(xb, x1[:], row4(R_L1), ALU.add).then_inc(S["b_xb"], 1)

            def b_late(q):
                pool.wait_ge(S["b_gs"], q + 1)
                pool.tensor_tensor(b_g2, b_g, b_s[:, 5].unsqueeze(2).broadcast_to([P, T, P]),
                                   ALU.mult).then_inc(S["b_gs2"], 1)
                pool.wait_ge(S["b_g2hi"], q + 1)
                pool.tensor_tensor(b_g2hl[:, 1], b_g2, b_g2hl[:, 0], ALU.subtract).then_inc(S["b_g2lo"], 1)

            def stream_a(q, i):
                if i == 0:
                    a_rstd_of(q, 0)
                if i == 2:
                    for t in range(T):
                        since(pool, S["a_relu"], q, T, t + 1)
                        pool.tensor_tensor(a_e[:, t], a_e[:, t], a_t[:, t], ALU.add).then_inc(S["a_lrelu"], 1)
                if i == 4:
                    a_gat_norm(q)
                    affine(q, 1, R_GG, R_GB)
                    a_residual(q)
                if i == 6:
                    a_rstd_of(q, 2)
                    affine(q, 2, R_MG, R_MB)

            def stream_b(q, i):
                if i == 0:
                    b_rstd_of(q, 0)
                    b_bias(q)
                if i == 3:
                    b_rstd_of(q, 1)
                if i == 6:
                    b_rstd_of(q, 2)
                if i == 9:
                    b_late(q)

            run(pool, stream_a, stream_b, lambda i: None)

        @block.scalar
        def _(act):
            act.wait_ge(S["w_loaded"], 160)
            act.activation(w_hl[:, 0], w_raw[:], ACT.Copy, scale=WS).then_inc(S["w_hi"], 1)

            def prepare(i):
                if i == 3:
                    act.wait_ge(S["edge_max"], 1)
                    for t in range(T):
                        ins = act.activation(wk1[:, t], wk2[:, t], ACT.Exp, bias=small[:, 6, t:t + 1],
                                             accum_out=small[:, 7, t:t + 1])
                    ins.then_inc(S["edge_exp"], 1)
                if i == 5:
                    act.wait_ge(S["degrees"], 1)
                    act.activation(small[:, 1], small[:, 0], ACT.Sqrt).then_inc(S["degree_roots"], 1)

            def stream_a(q, i):
                if i == 0:
                    since(act, S["a_turned"], q, 1, 1)
                    act.activation(a_fT[:, 0], pa[0][:], ACT.Relu).then_inc(S["a_hi"], 1)
                if i == 2:
                    for t in range(T):
                        since(act, S["a_max"], q, T, t + 1)
                        act.activation(a_e[:, t], a_t[:, t], ACT.Relu, bias=a_s[:, 0, t:t + 1],
                                       scale=4.0).then_inc(S["a_relu"], 1)
                    since(act, S["a_negmax"], q, 1, 1)
                    for t in range(T):
                        since(act, S["a_lrelu"], q, T, t + 1)
                        act.activation(a_e[:, t], a_e[:, t], ACT.Exp, bias=a_s[:, 4, t:t + 1],
                                       accum_out=a_s[:, 5, t:t + 1]).then_inc(S["a_exp"], 1)
                if i == 4:
                    since(act, S["a_g2"], q, 2, 1)
                    act.activation(a_hg[:], a_y2[:], ACT.Relu).then_inc(S["a_hg"], 1)
                    act.activation(a_hghl[:, 0], a_y2[:], ACT.Relu).then_inc(S["a_hghi"], 1)
                if i == 5:
                    since(act, S["a_agg"], q, 1, 1)
                    act.activation(a_fT[:, 0], pa[1][:], ACT.Copy).then_inc(S["a_ghi"], 1)
                if i == 6:
                    since(act, S["a_zturned"], q, 1, 1)
                    act.activation(a_fT[:, 0], pa[2][:], ACT.Relu).then_inc(S["a_zhi"], 1)

            def stream_b(q, i):
                if i in (0, 3, 6):
                    k = i // 3
                    since(act, S["b_y"], q, 3, k + 1)
                    act.activation(b_h[:, 0], b_y[:], ACT.Relu).then_inc(S["b_hi"], 1)
                if i == 1:
                    since(act, S["b_agg"], q, 1, 1)
                    act.activation(b_m1[:, 0], pb[0][:], ACT.Copy).then_inc(S["b_agghi"], 1)
                    act.activation(b_m2[:, 0], pb[1][:], ACT.Copy).then_inc(S["b_agghi"], 1)
                if i == 4:
                    since(act, S["b_turned"], q, 1, 1)
                    act.activation(b_hT[:], pb3h, ACT.Copy).then_inc(S["b_hT"], 1)
                    since(act, S["b_cheb"], q, 1, 1)
                    act.activation(b_m1[:, 0], pb[0][:], ACT.Copy).then_inc(S["b_chebhi"], 1)
                    act.activation(b_m2[:, 0], pb[1][:], ACT.Copy).then_inc(S["b_chebhi"], 1)
                if i == 7:
                    since(act, S["b_turned3"], q, 1, 1)
                    act.activation(b_hT[:], pb3h, ACT.Copy).then_inc(S["b_hT3"], 1)
                if i == 8:
                    since(act, S["b_proj"], q, 1, 1)
                    act.activation(b_lv[:], pair_view, ACT.Copy, scale=0.1).then_inc(S["b_tenth"], 1)
                    act.activation(b_lw[:], pb[1][:, 0:2], ACT.Copy, scale=0.1).then_inc(S["b_tenth"], 1)
                if i == 9:
                    since(act, S["b_nmx"], q, 1, 1)
                    act.activation(b_s[:, 5], b_s[:, 4], ACT.Exp).then_inc(S["b_sc"], 1)
                    for t in range(T):
                        ins = act.activation(b_e[:, t], b_te[:, t], ACT.Exp, bias=b_s[:, 3, t:t + 1],
                                             accum_out=b_s[:, 7, t:t + 1])
                    ins.then_inc(S["b_exp"], 1)
                    since(act, S["b_gs2"], q, 1, 1)
                    act.activation(b_g2hl[:, 0], b_g2, ACT.Copy).then_inc(S["b_g2hi"], 1)

            run(act, stream_a, stream_b, prepare)

        @block.vector
        def _(dve):
            n = 0

            def link(ins, named=None):
                nonlocal n
                if named:
                    ins.then_inc(S[named], 1)
                    dve.wait_ge(S[named], 1)
                else:
                    n += 1
                    ins.then_inc(S["dve_chain"], 1)
                    dve.wait_ge(S["dve_chain"], n)

            dve.wait_ge(S["consts"], 1)
            for t in range(T):
                dve.wait_ge(S["adj_turned"], t + 1)
                ins = dve.tensor_copy(adj_t[:, t], pa[t][:])
            link(ins)
            link(dve.tensor_scalar(gat_mask[:], adj_n[:], 0.0, FLOAT_MIN, ALU.is_le, ALU.mult))
            dve.wait_ge(S["w_hi"], 1)
            dve.wait_ge(S["rows_loaded"], 16 * 16)
            link(dve.scalar_tensor_tensor(out=w_hl[:, 1].rearrange("p a b -> p (a b)"),
                                          in0=w_raw[:].rearrange("p a b -> p (a b)"), scalar=WS,
                                          in1=w_hl[:, 0].rearrange("p a b -> p (a b)"),
                                          op0=ALU.mult, op1=ALU.subtract))
            for k, (w, r) in enumerate(((WP, R_ASRC), (WP, R_ADST), (L3O, R_A1), (L3O, R_A2))):
                link(dve.tensor_tensor_reduce(out=wk2[:, 0, 0:P], in0=w_raw[:, w], in1=rows[:, r], scale=1.0,
                                              scalar=0.0, op0=ALU.mult, op1=ALU.add,
                                              accum_out=score_w[:, k:k + 1]))
            link(dve.tensor_tensor(score_w[:, 4:5], score_w[:, 2:3], score_w[:, 3:4], ALU.add))
            link(dve.tensor_tensor(wk2[:, 1, 0:P], rows[:, R_ASRC], rows[:, R_ADST], ALU.add))
            link(dve.tensor_tensor_reduce(out=wk2[:, 0, 0:P], in0=wk2[:, 1, 0:P], in1=rows[:, R_BP], scale=1.0,
                                          scalar=0.0, op0=ALU.mult, op1=ALU.add, accum_out=score_w[:, 5:6]))
            link(dve.tensor_copy(col_hl[:, 0], score_w[:, 0:4]))
            link(dve.tensor_tensor(col_hl[:, 1], score_w[:, 0:4], col_hl[:, 0], ALU.subtract))
            for o, k in ((dst_hl, 1), (pair_hl, 4)):
                link(dve.tensor_scalar(wk2[:, 0, 0:P], ones[:], score_w[:, k:k + 1], None, ALU.mult))
                link(dve.tensor_copy(o[:, 0], wk2[:, 0, 0:P]))
                link(dve.tensor_tensor(o[:, 1], wk2[:, 0, 0:P], o[:, 0], ALU.subtract))
            link(dve.memset(small[:, 14], 0.0), "score_weights")

            def split(o, src):
                link(dve.tensor_copy(o[:, 0], src))
                link(dve.tensor_tensor(o[:, 1], src, o[:, 0], ALU.subtract))

            def diag_block(m, t):
                return m[:, t, t * P:(t + 1) * P]

            def prepare(i):
                if i == 0:
                    link(dve.tensor_scalar(eps1[:], eps1[:], 1.0, None, ALU.add))
                    link(dve.tensor_copy(wk3, adj_t[:]))
                    for t in range(T):
                        dg = diag_block(wk3, t)
                        ins = dve.scalar_tensor_tensor(out=dg, in0=ident[:], scalar=eps1[:], in1=dg,
                                                       op0=ALU.mult, op1=ALU.add)
                    link(ins)
                    split(gin_t, wk3)
                    link(dve.tensor_scalar(pair_mask[:], adj_t[:, :, 0:H], 0.0, NEG_BIG, ALU.is_le, ALU.mult))
                    link(dve.tensor_scalar(wk1, adj_t[:], 0.0, None, ALU.is_gt))
                    link(dve.tensor_reduce(small[:, 8], wk1, AX_X, ALU.add))
                    link(dve.tensor_reduce(small[:, 9], wk1[:, :, H:N], AX_X, ALU.add))
                    link(dve.tensor_scalar(small[:, 10], small[:, 8], 0.0, None, ALU.is_equal))
                    link(dve.tensor_scalar(late_neg[:], small[:, 9], 0.0, NEG_BIG, ALU.is_equal, ALU.mult))
                    link(dve.scalar_tensor_tensor(out=late_cnt[:], in0=small[:, 10], scalar=float(H),
                                                  in1=small[:, 9], op0=ALU.mult, op1=ALU.add))
                    link(dve.tensor_tensor(late_mask[:], wk1[:, :, H:N],
                                           small[:, 10].unsqueeze(2).broadcast_to([P, T, H]), ALU.add))
                if i == 1:
                    for t in range(T):
                        link(dve.tensor_scalar(wk1[:, t], adj_n[:, t], 0.0, None, ALU.is_gt))
                        link(dve.tensor_tensor_scan(wk2[:, t], wk1[:, t], wk1[:, t], 0.0, ALU.add, ALU.max))
                    link(dve.tensor_copy(small[:, 2], wk2[:, :, N - 1]), "row_counts")
                if i == 2:
                    dve.wait_ge(S["row_starts"], 1)
                    link(dve.tensor_copy(small[:, 3], pb[0][:, 0:T]))
                    link(dve.tensor_tensor(small[:, 4], small[:, 3], small[:, 2], ALU.add))
                    for t in range(T):
                        link(dve.tensor_scalar(wk3[:, t, 0:P], krow[:], small[:, 3, t:t + 1], None, ALU.is_ge))
                        link(dve.scalar_tensor_tensor(out=pick_t[:, t], in0=krow[:], scalar=small[:, 4, t:t + 1],
                                                      in1=wk3[:, t, 0:P], op0=ALU.is_lt, op1=ALU.mult))
                        link(dve.scalar_tensor_tensor(out=wk2[:, t], in0=wk2[:, t], scalar=small[:, 3, t:t + 1],
                                                      in1=wk1[:, t], op0=ALU.add, op1=ALU.mult))
                    link(dve.tensor_scalar(q16[:], wk2, float(N), None, ALU.min), "pick_ready")
                    for t in range(T):
                        link(dve.tensor_scalar(wk1[:, t], wk2[:, t], float(P), e_last[:], ALU.is_gt, ALU.mult))
                    link(dve.tensor_scalar(small[:, 5, 0:1], kcol[:], 1.0, None, ALU.add))
                    dve.wait_ge(S["picked"], 1)
                    link(dve.tensor_scalar(wk3[:, 0], pb[1][:], small[:, 5, 0:1], None, ALU.is_equal))
                    link(dve.tensor_scalar(wk3[:, 1], pb[2][:], e_col[:], None, ALU.mult), "edge_values")
                if i == 3:
                    for t in range(T):
                        dve.wait_ge(S["spread"], t + 1)
                        link(dve.tensor_tensor(wk1[:, t], wk1[:, t], pb[t][:], ALU.add))
                    link(dve.tensor_scalar(wk2, adj_n[:], 0.0, NEG_BIG, ALU.is_le, ALU.mult))
                    link(dve.tensor_tensor(wk2, wk2, wk1, ALU.add))
                    link(dve.tensor_reduce(small[:, 6], wk2, AX_X, ALU.max, negate=True), "edge_max")
                if i == 4:
                    dve.wait_ge(S["edge_exp"], 1)
                    link(dve.reciprocal(small[:, 11], small[:, 7]))
                    for t in range(T):
                        ins = dve.tensor_scalar(wk2[:, t], wk1[:, t], small[:, 11, t:t + 1], None, ALU.mult)
                    link(ins, "att_rows")
                    for t in range(T):
                        dve.wait_ge(S["att_turned"], t + 1)
                        link(dve.tensor_copy(wk1[:, t], pb[t][:]))
                        dg, own = diag_block(wk1, t), wk3[:, 0, t * P:(t + 1) * P]
                        link(dve.tensor_tensor(own, dg, ident[:], ALU.mult))
                        link(dve.tensor_tensor(dg, dg, own, ALU.subtract))
                    split(att_d, wk3[:, 0].rearrange("p (t n) -> p t n", t=T))
                    split(att_t, wk1)
                if i == 5:
                    link(dve.tensor_reduce(small[:, 0], adj_n[:], AX_X, ALU.add), "degrees")
                    dve.wait_ge(S["degree_roots"], 1)
                    link(dve.reciprocal(small[:, 12], small[:, 1]))
                    for t in range(T):
                        ins = dve.tensor_scalar(wk3[:, 1, t * P:(t + 1) * P], ident[:], small[:, 12, t:t + 1], None,
                                                ALU.mult)
                    link(ins, "d_diag")
                    dve.wait_ge(S["d_spread"], 1)
                    for t in range(T):
                        ins = dve.scalar_tensor_tensor(out=wk1[:, t], in0=adj_n[:, t], scalar=small[:, 12, t:t + 1],
                                                       in1=pb[0][:], op0=ALU.mult, op1=ALU.mult)
                    link(ins)
                    link(dve.tensor_scalar(wk1, wk1, -1.0, None, ALU.mult))
                    for t in range(T):
                        ins = dve.tensor_tensor(diag_block(wk1, t), diag_block(wk1, t), ident[:], ALU.add)
                    link(ins, "lap_rows")
                if i == 6:
                    for t in range(T):
                        dve.wait_ge(S["lap_turned"], t + 1)
                        ins = dve.tensor_copy(wk2[:, t], pb[t][:])
                    link(ins, "lap_cols")
                    split(lap_t, wk2)
                if i == 7:
                    for t in range(T):
                        dve.wait_ge(S["lap_squared"], t + 1)
                        link(dve.tensor_scalar(wk3[:, t], pb[t][:], 2.0, None, ALU.mult))
                        link(dve.tensor_tensor(diag_block(wk3, t), diag_block(wk3, t), ident[:], ALU.subtract))
                    split(cheb_t, wk3)
                    link(dve.memset(small[:, 15], 0.0), "prepared")

            def stats(q, k, src, st, mv, s_st, s_mv):
                for t in range(T):
                    ins = dve.bn_stats(st[:, t], src(t))
                ins.then_inc(s_st, 1)
                since_apart(dve, s_st, q, 3, k + 1)
                for t in range(T):
                    ins = dve.bn_aggr(mv[:, t], st[:, t])
                ins.then_inc(s_mv, 1)

            def normalise(q, k, src, y, mv, rs, s_rstd, s_y):
                since(dve, s_rstd, q, 3, k + 1)
                for t in range(T):
                    ins = dve.tensor_scalar(y[:, t], src(t), mv[:, t, 0:1], rs[:, 1, t:t + 1],
                                            ALU.subtract, ALU.mult)
                ins.then_inc(s_y, 1)

            def low(out_, src, hi, floor=None):
                op = ALU.max if floor is not None else ALU.mult
                return dve.scalar_tensor_tensor(out=out_, in0=src, scalar=0.0 if floor is not None else 1.0,
                                                in1=hi, op0=op, op1=ALU.subtract)

            def stream_a(q, i):
                if i == 0:
                    if isinstance(q, int):
                        dve.wait_ge(S["x0_loaded"], 16)
                    else:
                        dve.wait_ge(S["x_loaded"], 16)
                    stats(q, 0, lambda t: x_all[:, q, t], a_stats, a_mv, S["a_stats"], S["a_mv"])
                    normalise(q, 0, lambda t: x_all[:, q, t], a_y, a_mv, a_rstd, S["a_rstd"], S["a_y"])
                    since(dve, S["a_hi"], q, 1, 1)
                    low(a_fT[:, 1], pa[0][:], a_fT[:, 0], 0.0).then_inc(S["a_lo"], 1)
                if i == 1:
                    since(dve, S["a_proj"], q, 1, 1)
                    dve.tensor_scalar(a_s[:, 0], pa[2][:, 0:T], score_w[:, 5:6], 0.8, ALU.add,
                                      ALU.mult).then_inc(S["a_h1"], 1)
                    dve.scalar_tensor_tensor(out=a_h1[:], in0=pa[3][:].rearrange("p (t d) -> p t d", t=T),
                                             scalar=1.0 / WS, in1=row4(R_BP), op0=ALU.mult,
                                             op1=ALU.add).then_inc(S["a_h1"], 1)
                if i == 2:
                    since_apart(dve, S["a_proj"], q, 1, 1)
                    for t in range(T):
                        dve.tensor_tensor_reduce(out=a_t[:, t], in0=pa[1][:], in1=gat_mask[:, t], scale=0.2,
                                                 scalar=FLOAT_MIN, op0=ALU.add, op1=ALU.max,
                                                 accum_out=a_s[:, 1, t:t + 1]).then_inc(S["a_max"], 1)
                    since(dve, S["a_max"], q, T, T)
                    dve.scalar_tensor_tensor(out=a_s[:, 2], in0=a_s[:, 1], scalar=4.0, in1=a_s[:, 0],
                                             op0=ALU.mult, op1=ALU.add).then_inc(S["a_t1"], 1)
                    since(dve, S["a_t1"], q, 3, 1)
                    dve.scalar_tensor_tensor(out=a_s[:, 3], in0=a_s[:, 2], scalar=0.0, in1=a_s[:, 1],
                                             op0=ALU.max, op1=ALU.add).then_inc(S["a_t1"], 1)
                    since(dve, S["a_t1"], q, 3, 2)
                    dve.tensor_scalar(a_s[:, 4], a_s[:, 3], -1.0, None, ALU.mult).then_inc(S["a_negmax"], 1)
                if i == 3:
                    for t in range(T):
                        since(dve, S["a_eturned"], q, T, t + 1)
                        dve.tensor_tensor(a_pt[:, :, t * P:(t + 1) * P],
                                          pa[2 * (t % 2)][:].rearrange("p (j m) -> p j m", j=T),
                                          adj_t[:, :, t * P:(t + 1) * P], ALU.mult).then_inc(S["a_weighed"], 1)
                    dve.reciprocal(a_s[:, 6], a_s[:, 5]).then_inc(S["a_recip"], 1)
                if i == 4:
                    since(dve, S["a_heads"], q, 1, 1)
                    src = lambda t: pa[3][:, t * P:(t + 1) * P]
                    stats(q, 1, src, a_stats, a_mv, S["a_stats"], S["a_mv"])
                    normalise(q, 1, src, a_y, a_mv, a_rstd, S["a_rstd"], S["a_y"])
                    since(dve, S["a_hghi"], q, 1, 1)
                    low(flat(a_hghl[:, 1]), flat(a_y2[:]), flat(a_hghl[:, 0]), 0.0).then_inc(S["a_hglo"], 1)
                if i == 5:
                    since(dve, S["a_ghi"], q, 1, 1)
                    low(a_fT[:, 1], pa[1][:], a_fT[:, 0]).then_inc(S["a_glo"], 1)
                if i == 6:
                    since(dve, S["a_z"], q, 1, 1)
                    dve.scalar_tensor_tensor(out=a_z[:], in0=pa[0][:].rearrange("p (t d) -> p t d", t=T),
                                             scalar=1.0 / WS, in1=row4(R_B1), op0=ALU.mult,
                                             op1=ALU.add).then_inc(S["a_z1"], 1)
                    since(dve, S["a_z1"], q, 1, 1)
                    stats(q, 2, lambda t: a_z[:, t], a_stats, a_mv, S["a_stats"], S["a_mv"])
                    normalise(q, 2, lambda t: a_z[:, t], a_y, a_mv, a_rstd, S["a_rstd"], S["a_y"])
                    since(dve, S["a_zhi"], q, 1, 1)
                    low(a_fT[:, 1], pa[2][:], a_fT[:, 0], 0.0).then_inc(S["a_zlo"], 1)
                if i == 7:
                    since(dve, S["a_out"], q, 1, 1)
                    since(dve, S["a_hb"], q, 1, 1)
                    dve.scalar_tensor_tensor(out=flat(a_z[:]), in0=pa[3][:], scalar=1.0 / WS, in1=flat(a_hb[:]),
                                             op0=ALU.mult, op1=ALU.add).then_inc(S["a_t1"], 1)
                    since(dve, S["a_t1"], q, 3, 3)
                    since(dve, S["b_xb"], q, 1, 0)
                    dve.scalar_tensor_tensor(out=x1[:], in0=a_z[:], scalar=0.0, in1=x_all[:, q],
                                             op0=ALU.max, op1=ALU.add).then_inc(S["x1_done"], 1)

            def stream_b(q, i):
                if i in (0, 3, 6):
                    k = i // 3
                    xin, done = ((x1, "x1_done"), (x2, "x2_done"), (x3, "x3_done"))[k]
                    since(dve, S[done], q, 1, 1)
                    stats(q, k, lambda t: xin[:, t], b_stats, b_mv, S["b_stats"], S["b_mv"])
                    normalise(q, k, lambda t: xin[:, t], b_y, b_mv, b_rstd, S["b_rstd"], S["b_y"])
                    since(dve, S["b_hi"], q, 3, k + 1)
                    low(flat(b_h[:, 1]), flat(b_y[:]), flat(b_h[:, 0]), 0.0).then_inc(S["b_lo"], 1)
                if i == 1:
                    since(dve, S["b_agghi"], q, 2, 1)
                    low(b_m1[:, 1], pb[0][:], b_m1[:, 0]).then_inc(S["b_agglo"], 1)
                    since(dve, S["b_agghi"], q, 2, 2)
                    low(b_m2[:, 1], pb[1][:], b_m2[:, 0]).then_inc(S["b_agglo"], 1)
                if i == 2:
                    since(dve, S["b_mixed"], q, 1, 1)
                    since(dve, S["b_xb"], q, 1, 1)
                    dve.scalar_tensor_tensor(out=flat(x2), in0=pb[2][:], scalar=1.0 / WS, in1=flat(xb),
                                             op0=ALU.mult, op1=ALU.add).then_inc(S["x2_done"], 1)
                if i == 4:
                    since(dve, S["b_chebhi"], q, 2, 1)
                    low(b_m1[:, 1], pb[0][:], b_m1[:, 0]).then_inc(S["b_cheblo"], 1)
                    since(dve, S["b_chebhi"], q, 2, 2)
                    low(b_m2[:, 1], pb[1][:], b_m2[:, 0]).then_inc(S["b_cheblo"], 1)
                if i == 5:
                    since(dve, S["b_mixed2"], q, 1, 1)
                    dve.scalar_tensor_tensor(out=b_t, in0=pb[2][:].rearrange("p (t d) -> p t d", t=T),
                                             scalar=1.0 / WS, in1=row4(R_L2), op0=ALU.mult,
                                             op1=ALU.add).then_inc(S["b_t"], 1)
                    since(dve, S["b_t"], q, 1, 1)
                    dve.scalar_tensor_tensor(out=flat(x3), in0=flat(b_t), scalar=0.0, in1=flat(x2),
                                             op0=ALU.max, op1=ALU.add).then_inc(S["x3_done"], 1)
                if i == 8:
                    since(dve, S["b_tenth"], q, 2, 2)
                    dve.tensor_tensor(b_lv[:], b_lv[:], pair_view, ALU.max).then_inc(S["b_lv"], 1)
                    dve.tensor_tensor(b_lw[:], b_lw[:], pb[1][:, 0:2], ALU.max).then_inc(S["b_lw"], 1)
                    since_apart(dve, S["b_lv"], q, 1, 1)
                    for t in range(T):
                        dve.tensor_tensor_reduce(out=b_te[:, t], in0=b_lv[:, t // TH], in1=pair_mask[:, t],
                                                 scale=1.0, scalar=FLOAT_MIN, op0=ALU.add, op1=ALU.max,
                                                 accum_out=b_s[:, 0, t:t + 1]).then_inc(S["b_pmax"], 1)
                    since(dve, S["b_lw"], q, 1, 1)
                    dve.tensor_tensor(b_s[:, 1].rearrange("p (r c) -> p r c", c=2),
                                      b_lw[:].unsqueeze(1).broadcast_to([P, T // 2, 2]),
                                      late_neg[:].rearrange("p (r c) -> p r c", c=2),
                                      ALU.add).then_inc(S["b_m2"], 1)
                    since(dve, S["b_m2"], q, 4, 1)
                    since(dve, S["b_pmax"], q, T, T)
                    dve.tensor_tensor(b_s[:, 2], b_s[:, 0], b_s[:, 1], ALU.max).then_inc(S["b_m2"], 1)
                    since(dve, S["b_m2"], q, 4, 2)
                    dve.tensor_scalar(b_s[:, 3], b_s[:, 2], -1.0, None, ALU.mult)
                    dve.tensor_tensor(b_s[:, 4], b_s[:, 1], b_s[:, 2], ALU.subtract).then_inc(S["b_nmx"], 1)
                if i == 9:
                    since(dve, S["b_sc"], q, 1, 1)
                    dve.tensor_tensor(b_s[:, 8], b_s[:, 5], late_cnt[:], ALU.mult).then_inc(S["b_m2"], 1)
                    since(dve, S["b_exp"], q, 1, 1)
                    since(dve, S["b_m2"], q, 4, 3)
                    dve.tensor_tensor(b_s[:, 9], b_s[:, 8], b_s[:, 7], ALU.add).then_inc(S["b_m2"], 1)
                    since(dve, S["b_m2"], q, 4, 4)
                    dve.reciprocal(b_s[:, 10], b_s[:, 9]).then_inc(S["b_rc"], 1)
                    since(dve, S["b_rc"], q, 1, 1)
                    dve.tensor_tensor(b_g, pb[2][:].rearrange("p (t d) -> p t d", t=T),
                                      b_s[:, 10].unsqueeze(2).broadcast_to([P, T, P]),
                                      ALU.mult).then_inc(S["b_gs"], 1)
                if i == 10:
                    since(dve, S["b_final"], q, 1, 1)
                    since(dve, S["out_stored"], q, 16, 16)
                    dve.scalar_tensor_tensor(out=flat(x4), in0=pb[3][:], scalar=1.0 / WS, in1=flat(x3),
                                             op0=ALU.mult, op1=ALU.add).then_inc(S["x4_done"], 1)

            run(dve, stream_a, stream_b, prepare)

        @block.tensor
        def _(pe):
            def turn_all(banks, src, sem):
                for j in range(T):
                    for t in range(T):
                        ins = pe.transpose(banks[j][:, t * P:(t + 1) * P], src[:, t, j * P:(j + 1) * P], ident[:])
                    ins.then_inc(sem, 1)

            pe.wait_ge(S["consts"], 1)
            pe.wait_ge(S["adj_loaded"], 16)
            turn_all(pa, adj_n, S["adj_turned"])

            def prepare(i):
                if i == 1:
                    pe.wait_ge(S["row_counts"], 1)
                    for t in range(T):
                        for k in range(t):
                            pe.matmul(pb[0][:, t:t + 1], ones[:], small[:, 2, k:k + 1], start=(k == 0), stop=False)
                        ins = pe.matmul(pb[0][:, t:t + 1], tri[:], small[:, 2, t:t + 1], start=(t == 0), stop=True)
                    ins.then_inc(S["row_starts"], 1)
                if i == 2:
                    pe.wait_ge(S["pick_ready"], 1)
                    for t in range(T):
                        pe.matmul(pb[1][:], pick_t[:, t], q16[:, t], start=(t == 0), stop=(t == T - 1))
                    for t in range(T):
                        ins = pe.matmul(pb[2][:, t * P:(t + 1) * P], pick_t[:, t], ident16[:], start=True, stop=True)
                    ins.then_inc(S["picked"], 1)
                    pe.wait_ge(S["edge_values"], 1)
                    for t in range(T):
                        pe.matmul(pb[t][:], wk3[:, 1, t * P:(t + 1) * P], wk3[:, 0], start=True,
                                  stop=True).then_inc(S["spread"], 1)
                if i == 4:
                    pe.wait_ge(S["att_rows"], 1)
                    turn_all(pb, wk2, S["att_turned"])
                if i == 5:
                    pe.wait_ge(S["d_diag"], 1)
                    pe.matmul(pb[0][:], ones[:], wk3[:, 1], start=True, stop=True).then_inc(S["d_spread"], 1)
                if i == 6:
                    pe.wait_ge(S["lap_rows"], 1)
                    turn_all(pb, wk1, S["lap_turned"])
                if i == 7:
                    pe.wait_ge(S["lap_cols"], 1)
                    for j in range(T):
                        for k in range(T):
                            ins = pe.matmul(pb[j][:], wk1[:, k, j * P:(j + 1) * P], wk2[:, k], start=(k == 0),
                                            stop=(k == T - 1))
                        ins.then_inc(S["lap_squared"], 1)
                    pe.wait_ge(S["prepared"], 1)

            def mm3(o, lh, ll, rh, rl, first, last):
                pe.matmul(o, lh, rh, start=first, stop=False)
                pe.matmul(o, lh, rl, start=False, stop=False)
                return pe.matmul(o, ll, rh, start=False, stop=last)

            def by_weight(bank, parts):
                for t in range(T):
                    c = slice(t * P, (t + 1) * P)
                    for n, (f, w) in enumerate(parts):
                        ins = mm3(bank[:, c], f[:, 0, c], f[:, 1, c], w_hl[:, 0, w], w_hl[:, 1, w],
                                  n == 0, n == len(parts) - 1)
                return ins

            def over_nodes(bank, h, m):
                for t in range(T):
                    ins = mm3(bank[:], h[:, 0, t], h[:, 1, t], m[:, 0, t], m[:, 1, t], t == 0, t == T - 1)
                return ins

            def stream_a(q, i):
                if i == 0:
                    since(pe, S["a_y"], q, 3, 1)
                    since(pe, S["a_z1"], q, 1, 0)
                    for t in range(T):
                        ins = pe.transpose(pa[0][:, t * P:(t + 1) * P], a_y[:, t], ident[:])
                    ins.then_inc(S["a_turned"], 1)
                if i == 1:
                    since(pe, S["a_lo"], q, 1, 1)
                    since(pe, S["x1_done"], q, 1, 0)
                    mm3(pa[1][:], dst_hl[:, 0], dst_hl[:, 1], a_fT[:, 0], a_fT[:, 1], True, True)
                    for t in range(T):
                        c = slice(t * P, (t + 1) * P)
                        mm3(pa[2][:, t:t + 1], a_fT[:, 0, c], a_fT[:, 1, c], col_hl[:, 0, 0:1], col_hl[:, 1, 0:1],
                            True, True)
                    by_weight(pa[3], [(a_fT, WP)]).then_inc(S["a_proj"], 1)
                if i == 3:
                    for t in range(T):
                        since(pe, S["a_exp"], q, T, t + 1)
                        if t < 2:
                            since(pe, S["a_h1"], q, 2, 2)
                        else:
                            since(pe, S["a_weighed"], q, T, t - 1)
                        for j in range(T):
                            ins = pe.transpose(pa[2 * (t % 2)][:, j * P:(j + 1) * P], a_e[:, t, j * P:(j + 1) * P], ident[:])
                        ins.then_inc(S["a_eturned"], 1)
                    for t in range(T):
                        since(pe, S["a_weighed"], q, T, t + 1)
                        for j in range(T):
                            ins = pe.matmul(pa[3][:, t * P:(t + 1) * P], a_pt[:, j, t * P:(t + 1) * P], a_h1[:, j],
                                            start=(j == 0), stop=(j == T - 1))
                    ins.then_inc(S["a_heads"], 1)
                if i == 5:
                    since(pe, S["a_hglo"], q, 1, 1)
                    over_nodes(pa[1], a_hghl, gin_t).then_inc(S["a_agg"], 1)
                if i == 6:
                    since(pe, S["a_glo"], q, 1, 1)
                    by_weight(pa[0], [(a_fT, WZ)]).then_inc(S["a_z"], 1)
                    since(pe, S["a_g2"], q, 2, 2)
                    for t in range(T):
                        ins = pe.transpose(pa[2][:, t * P:(t + 1) * P], a_y2[:, t], ident[:])
                    ins.then_inc(S["a_zturned"], 1)
                if i == 7:
                    since(pe, S["a_zlo"], q, 1, 1)
                    by_weight(pa[3], [(a_fT, WO2)]).then_inc(S["a_out"], 1)

            def stream_b(q, i):
                if i == 1:
                    since(pe, S["b_lo"], q, 3, 1)
                    over_nodes(pb[0], b_h, att_t)
                    for t in range(T):
                        ins = mm3(pb[1][:, t * P:(t + 1) * P], b_h[:, 0, t], b_h[:, 1, t], att_d[:, 0, t],
                                  att_d[:, 1, t], True, True)
                    ins.then_inc(S["b_agg"], 1)
                if i == 2:
                    since(pe, S["b_agglo"], q, 2, 2)
                    by_weight(pb[2], [(b_m2, L1A), (b_m1, L1B)]).then_inc(S["b_mixed"], 1)
                if i == 4:
                    since(pe, S["b_lo"], q, 3, 2)
                    for h in range(2):
                        for t in range(T):
                            ins = pe.transpose(pb3h[:, h, t * P:(t + 1) * P], b_h[:, h, t], ident16[:])
                    ins.then_inc(S["b_turned"], 1)
                    over_nodes(pb[0], b_h, lap_t)
                    over_nodes(pb[1], b_h, cheb_t).then_inc(S["b_cheb"], 1)
                if i == 5:
                    since(pe, S["b_hT"], q, 1, 1)
                    since(pe, S["b_cheblo"], q, 2, 2)
                    by_weight(pb[2], [(b_hT, L2A), (b_m1, L2B), (b_m2, L2C)]).then_inc(S["b_mixed2"], 1)
                if i == 7:
                    since(pe, S["b_lo"], q, 3, 3)
                    for h in range(2):
                        for t in range(T):
                            ins = pe.transpose(pb3h[:, h, t * P:(t + 1) * P], b_h[:, h, t], ident16[:])
                    ins.then_inc(S["b_turned3"], 1)
                if i == 8:
                    since(pe, S["b_hT3"], q, 1, 1)
                    mm3(pb[0][:], pair_hl[:, 0], pair_hl[:, 1], b_hT[:, 0], b_hT[:, 1], True, True)
                    for c in range(2):
                        ev = slice(c * H, (c + 1) * H, 2)
                        od = slice(c * H + 1, (c + 1) * H, 2)
                        mm3(pb[1][:, c:c + 1], b_hT[:, 0, ev], b_hT[:, 1, ev], col_hl[:, 0, 2:3], col_hl[:, 1, 2:3],
                            True, False)
                        mm3(pb[1][:, c:c + 1], b_hT[:, 0, od], b_hT[:, 1, od], col_hl[:, 0, 3:4], col_hl[:, 1, 3:4],
                            False, True)
                    by_weight(pb[2], [(b_hT, L3O)]).then_inc(S["b_proj"], 1)
                if i == 10:
                    since(pe, S["b_exp"], q, 1, 1)
                    since(pe, S["b_gs"], q, 1, 1)
                    since(pe, S["b_g2lo"], q, 1, 1)
                    for t in range(T):
                        c = slice(t * P, (t + 1) * P)
                        mm3(pb[3][:, c], b_hT[:, 0, c], b_hT[:, 1, c], w_hl[:, 0, L3S], w_hl[:, 1, L3S], True, False)
                        for j in range(T):
                            if t < TH:
                                ins = pe.matmul(pb[3][:, c], b_e[:, j, c], b_g[:, j], start=False, stop=(j == T - 1))
                            else:
                                r = slice((t - TH) * P, (t - TH + 1) * P)
                                pe.matmul(pb[3][:, c], late_mask[:, j, r], b_g2hl[:, 0, j], start=False, stop=False)
                                ins = pe.matmul(pb[3][:, c], late_mask[:, j, r], b_g2hl[:, 1, j], start=False,
                                                stop=(j == T - 1))
                    ins.then_inc(S["b_final"], 1)

            run(pe, stream_a, stream_b, prepare)


_INS = ['x', 'adj', 'L0_gnn_Wp', 'L0_gnn_bp', 'L0_gnn_a_src', 'L0_gnn_a_dst', 'L0_gnn_gat_g', 'L0_gnn_gat_b',
        'L0_gnn_eps', 'L0_gnn_W1', 'L0_gnn_b1', 'L0_gnn_mlp_g', 'L0_gnn_mlp_b', 'L0_gnn_W2', 'L0_gnn_b2', 'L1_gnn_W',
        'L1_gnn_e', 'L1_gnn_bias', 'L2_gnn_weight', 'L2_gnn_bias', 'L3_gnn_others_weight', 'L3_gnn_self_weight',
        'L3_gnn_att_weight']


def kernel(**inputs):
    import numpy as _np
    import concourse.bacc as _bacc
    from concourse import mybir as _mybir
    from concourse.bass_utils import run_bass_kernel_spmd as _run

    nc = _bacc.Bacc("TRN2", target_bir_lowering=False, num_devices=1)
    arrays, args = {}, []
    for name in _INS:
        a = _np.ascontiguousarray(inputs[name])
        arrays[f"in_{name}_dram"] = a
        args.append(nc.dram_tensor(f"in_{name}_dram", a.shape, _mybir.dt.from_np(a.dtype), kind="ExternalInput").ap())
    shape = inputs["x"].shape
    args.append(nc.dram_tensor("out_dram", shape, _mybir.dt.float32, kind="ExternalOutput").ap())
    build(nc, *args)
    r = _run(nc, [arrays], core_ids=[0])
    return r.results[0]["out_dram"]
```

```python
from contextlib import ExitStack

import concourse.bass as bass
from concourse import mybir

P = 128
ALU = mybir.AluOpType
ACT = mybir.ActivationFunctionType
F32 = mybir.dt.float32
F16 = mybir.dt.float16
AX_X = mybir.AxisListType.X

FLOAT_MIN = -3.4028234663852886e38
NEG_BIG = -9.0e15
LN_EPS = 1e-5
WS = 64.0


def build(nc, x, adj, Wp, bp, a_src, a_dst, gat_g, gat_b, eps, W1, b1, mlp_g, mlp_b, W2, b2,
          L1_W, L1_e, L1_bias, L2_weight, L2_bias, L3_others, L3_self, L3_att, out):
    B, N, D = x.shape
    T = N // P
    H = N // 2
    TH = T // 2
    assert D == P and N == 512 and L1_e.shape[1] == P

    WP, WZ, WO2, L1A, L1B, L2A, L2B, L2C, L3O, L3S = range(10)
    (R_BP, R_ASRC, R_ADST, R_GG, R_GB, R_B1, R_MG, R_MB, R_B2, R_L1, R_L2, R_A1, R_A2) = range(13)

    with ExitStack() as ctx:
        def sb(name, shape, dt=F32):
            return ctx.enter_context(nc.sbuf_tensor(name, shape, dt))

        def ps(name, shape=(P, 512), dt=F32):
            return ctx.enter_context(nc.psum_tensor(name, list(shape), dt))

        x_all = sb("x_all", [P, B, T, P])
        adj_n = sb("adj_n", [P, T, N])
        adj_t = sb("adj_t", [P, T, N])
        gat_mask = sb("gat_mask", [P, T, N])
        pair_mask = sb("pair_mask", [P, T, H])
        late_mask = sb("late_mask", [P, T, H], F16)
        late_neg = sb("late_neg", [P, T])
        late_cnt = sb("late_cnt", [P, T])
        gin_t = sb("gin_t", [P, 2, T, N], F16)
        att_t = sb("att_t", [P, 2, T, N], F16)
        att_d = sb("att_d", [P, 2, T, P], F16)
        lap_t = sb("lap_t", [P, 2, T, N], F16)
        cheb_t = sb("cheb_t", [P, 2, T, N], F16)
        w_raw = sb("w_raw", [P, 10, P])
        w_hl = sb("w_hl", [P, 2, 10, P], F16)
        rows = sb("rows", [P, 13, P])
        e_col = sb("e_col", [P, 1])
        mlp_col = sb("mlp_col", [P, 2])
        e_last = sb("e_last", [P, 1])
        eps1 = sb("eps1", [P, 1])
        ident = sb("ident", [P, P])
        ident16 = sb("ident16", [P, P], F16)
        ones = sb("ones", [P, P])
        ones16 = sb("ones16", [P, P], F16)
        bias_hl = sb("bias_hl", [P, 5, T, P], F16)
        mhalf = sb("mhalf", [P, T])
        score_w = sb("score_w", [P, 6])
        col_hl = sb("col_hl", [P, 2, 4], F16)
        dst_hl = sb("dst_hl", [P, 2, P], F16)
        pair_hl = sb("pair_hl", [P, 2, P], F16)
        work = sb("work", [P, 3 * T * N])

        def area(at, per_part, inner):
            return work[:, at:at + per_part * inner].rearrange("p (a b) -> p a b", b=inner)

        wk1, wk2, wk3 = (area(k * T * N, T, N) for k in range(3))
        m_t, p_g, p_g2 = (area(k * T * P, T, P) for k in range(3))
        p_te, p_e = (area(3 * T * P + k * T * H, T, H) for k in range(2))
        rest = 3 * T * P + 2 * T * H
        p_lv = area(rest, 2, H)
        p_h, p_g2hl = (work[:, rest + k * T * P:rest + (k + 1) * T * P].bitcast(F16)
                       .rearrange("p (h t d) -> p h t d", h=2, t=T) for k in (1, 2))
        p_hT = work[:, rest + 3 * T * P:rest + 4 * T * P].bitcast(F16).rearrange("p (h n) -> p h n", h=2)
        assert rest + 4 * T * P <= 3 * T * N
        tri = sb("tri", [P, P])
        kcol = sb("kcol", [P, 1])
        krow = sb("krow", [P, P])
        small = sb("small", [P, 16, T])
        pick_t = sb("pick_t", [P, T, P], F16)
        q16 = sb("q16", [P, T, N], F16)

        norms = {"s": 1, "g": 1, "f": 1, "m": 2, "p": 1}
        stats = {k: sb(f"{k}_stats", [P, T, 6]) for k in norms}
        mv = {k: sb(f"{k}_mv", [P, T, 2]) for k in norms}
        rstd = {k: sb(f"{k}_rstd", [P, 4, T]) for k in norms}
        y = {k: sb(f"{k}_y", [P, T, P]) for k in norms}
        s_fT = sb("s_fT", [P, 2, N], F16)
        s_h1 = sb("s_h1", [P, T, P])
        s_s = sb("s_s", [P, 6, T])
        s_t = sb("s_t", [P, T, N])
        s_e = sb("s_e", [P, T, N])
        g_s = sb("g_s", [P, 2, T])
        g_pt = sb("g_pt", [P, T, N])
        g_y2 = sb("g_y2", [P, T, P])
        g_hg = sb("g_hg", [P, T, P])
        g_hghl = sb("g_hghl", [P, 2, T, P], F16)
        g_fT = sb("g_fT", [P, 2, N], F16)
        g_z = sb("g_z", [P, T, P])
        m_h = sb("m_h", [P, 2, T, P], F16)
        m_hT = sb("m_hT", [P, 2, N], F16)
        m_1 = sb("m_1", [P, 2, N], F16)
        m_2 = sb("m_2", [P, 2, N], F16)
        p_lw = sb("p_lw", [P, 2])
        p_s = sb("p_s", [P, 12, T])

        bank = [ps(f"bank{i}") for i in range(8)]

        def halves(b):
            return b[:, :].bitcast(F16).rearrange("p (h n) -> p h n", h=2)

        pair_view = bank[7][:].rearrange("p (i c) -> p c i", c=2)

        names = """adj_loaded w_loaded rows_loaded x0_loaded x_loaded consts waits_passed
            pool_chain dve_chain adj_turned w_hi score_weights biases row_counts row_starts pick_ready picked
            edge_values spread edge_max edge_exp att_rows att_turned degrees degree_roots d_diag d_spread
            lap_rows lap_turned lap_cols lap_squared prepared
            s_turned s_hi s_lo s_rows s_src s_proj s_h1 s_max s_step s_negmax s_relu s_lrelu s_exp
            g_turned g_weighed g_recip g_recip2 g_heads g_v1 g_v2 g_gain g_shift g_hg g_hghi g_hglo
            g_sum g_hi g_lo g_z g_zturned g_zr g_zhi g_zlo g_out g_t x1_done
            m_hi m_lo m_off m_off_hi m_off_lo m_own m_own_hi m_own_lo m_mix x2_done
            m_lap m_lap_hi m_lap_lo m_cheb m_cheb_hi m_cheb_lo m_turned m_hT m_mix3 m_relu x3_done
            p_hi p_lo p_turned p_hT p_vec p_tenth p_lv p_vcol p_wtenth p_lw p_g p_max p_step p_negmax
            p_late p_exp p_recip p_gs p_g2 p_g2hi p_g2lo p_out x4_done out_stored""".split()
        for k in norms:
            names += [f"{k}_stats", f"{k}_mv", f"{k}_var", f"{k}_rstd", f"{k}_y"]
        S = {n: ctx.enter_context(nc.semaphore(n)) for n in names}

        block = ctx.enter_context(nc.Block())

        def flat(ap):
            return ap.rearrange("p t d -> p (t d)")

        def row4(r):
            return rows[:, r:r + 1, :].broadcast_to([P, T, P])

        def node_view(dram):
            return dram.rearrange("(t p) d -> p t d", p=P)

        def since(eng, sem, q, per, k):
            if isinstance(q, int) and per * q + k <= 0:
                return
            eng.wait_ge(sem, per * q + k)

        def since_apart(eng, sem, q, per, k):
            since(eng, sem, q, per, k)
            if not isinstance(q, int):
                eng.sem_inc(S["waits_passed"], 1)

        def normed(eng, stage, what, q, k):
            since(eng, S[f"{stage}_{what}"], q, norms[stage], k + 1)

        AHEAD = {n: k for k, names_ in (
            (4, "x_stats x_apply x_turn x_low score_rows score_src project scores negmax exp"),
            (3, "weigh weigh2 heads heads_stats heads_apply"),
            (2, "gat_out gat_low gin gin_low mlp_in mlp_stats mlp_apply mlp_turn mlp_low mlp_out"),
            (1, "l2_stats l2_apply l2_high l2_low off off_low own own_low l2_out l3_stats l3_apply l3_high l3_low "
                "lap lap_low cheb cheb_low l3_turn l3_out l3_add"),
            (0, "l4_stats l4_apply l4_high l4_low l4_turn pair_rows pair_lrelu pair_feats pair_cols pair_mask pair_max "
                "pair_exp pair_sums pair_scale late_high late_low l4_out")) for n in names_.split()}
        ORDER = {
            "pool": """l2_stats x_stats gat_out l4_stats gat_low l3_stats scores mlp_stats late_high late_low
                  heads_stats mlp_low l3_add""".split(),
            "act": """l2_high own x_turn gat_out l4_high off l4_turn pair_rows scores pair_cols gin l3_high project
                  pair_exp lap late_high mlp_turn cheb l3_turn exp l3_out""".split(),
            "dve": """l2_stats x_stats weigh l2_apply l4_stats l2_low x_apply weigh2 own_low l4_apply x_low l4_low
                  score_src off_low scores l2_out pair_lrelu l3_stats pair_mask l3_apply gin_low pair_max l3_low
                  mlp_stats pair_sums pair_scale mlp_apply lap_low heads_stats negmax cheb_low heads_apply l4_out
                  mlp_out""".split(),
            "pe": """weigh weigh2 own x_turn off score_rows l4_turn project l2_out pair_rows gin pair_cols heads
                  pair_feats mlp_in lap cheb mlp_turn l3_turn l4_out mlp_out l3_out""".split(),
        }
        LAST = 4
        GAP = AHEAD["x_turn"] - AHEAD["gin"]

        def run(eng, order, step, prepare):
            for i in range(-LAST, 0):
                for k in range(4):
                    prepare(4 * (i + LAST) + k) if i < 2 - LAST and k < 1 else None
                for name in order:
                    if i + AHEAD[name] >= 0:
                        step(name, i + AHEAD[name])
                for k in range(1, 4):
                    prepare(4 * (i + LAST) + k) if i < 2 - LAST else None
            with eng.Fori(0, B - LAST) as i:
                for name in order:
                    step(name, i + AHEAD[name])
            for i in range(B - LAST, B):
                for name in order:
                    if i + AHEAD[name] < B:
                        step(name, i + AHEAD[name])

        @block.sync
        def _(sp):
            sp.dma_start(adj_n[:], adj.rearrange("(t p) n -> p t n", p=P)).then_inc(S["adj_loaded"], 16)
            sp.dma_start(x_all[:, 0], node_view(x[0])).then_inc(S["x0_loaded"], 16)
            for k, w in enumerate((Wp, W1, W2, L1_W[0], L1_W[1], L2_weight[0, 0], L2_weight[1, 0],
                                   L2_weight[2, 0], L3_others, L3_self)):
                sp.dma_start(w_raw[:, k, :], w).then_inc(S["w_loaded"], 16)
            sp.dma_start(x_all[:, 1:B].rearrange("p b t d -> p (b t) d"),
                         x[1:B].rearrange("b (t p) d -> p (b t) d", p=P)).then_inc(S["x_loaded"], 16)
            out_v = out.rearrange("b (t p) d -> b p t d", p=P)
            with sp.Fori(0, B) as q:
                sp.wait_ge(S["x4_done"], q + 1)
                sp.dma_start(out_v[q], x_all[:, q]).then_inc(S["out_stored"], 16)
            sp.wait_ge(S["out_stored"], 16 * B)

        @block.gpsimd
        def _(pool):
            def bcast(v):
                return v.rearrange("(o d) -> o d", o=1).broadcast_to([P, v.shape[0]])

            att_flat = L3_att.rearrange("k o -> (k o)")
            vecs = [bp, a_src, a_dst, gat_g, gat_b, b1, mlp_g, mlp_b, b2, L1_bias,
                    L2_bias.rearrange("a b d -> (a b d)"), att_flat[0:P], att_flat[P:2 * P]]
            for k, v in enumerate(vecs):
                pool.dma_start(rows[:, k, :], bcast(v)).then_inc(S["rows_loaded"], 16)
            pool.dma_start(e_col[:], L1_e.rearrange("o k -> k o")).then_inc(S["rows_loaded"], 16)
            pool.dma_start(mlp_col[:, 0:1], mlp_g.rearrange("(d o) -> d o", o=1)).then_inc(S["rows_loaded"], 16)
            pool.dma_start(mlp_col[:, 1:2], mlp_b.rearrange("(d o) -> d o", o=1)).then_inc(S["rows_loaded"], 16)
            pool.dma_start(e_last[:], L1_e[0:1, P - 1:P].broadcast_to([P, 1])).then_inc(S["rows_loaded"], 16)
            pool.dma_start(eps1[:], eps.rearrange("(o d) -> o d", o=1).broadcast_to([P, 1])).then_inc(
                S["rows_loaded"], 16)

            n = 0

            def link(ins):
                nonlocal n
                n += 1
                ins.then_inc(S["pool_chain"], 1)
                pool.wait_ge(S["pool_chain"], n)

            link(pool.memset(ones[:], 1.0))
            pool.memset(mhalf[:], -0.5)
            pool.memset(ones16[:], 1.0)
            link(pool.affine_select(out=ident[:], in_=ones[:], pattern=[[-1, P]], compare_op=ALU.is_equal,
                                    fill=0.0, base=0, channel_multiplier=1))
            pool.affine_select(out=tri[:], in_=ones[:], pattern=[[1, P]], compare_op=ALU.is_gt,
                               fill=0.0, base=0, channel_multiplier=-1)
            pool.iota(kcol[:], pattern=[[0, 1]], base=0, channel_multiplier=1,
                      allow_small_or_imprecise_dtypes=True)
            pool.iota(krow[:], pattern=[[1, P]], base=0, channel_multiplier=0,
                      allow_small_or_imprecise_dtypes=True)
            pool.tensor_copy(ident16[:], ident[:]).then_inc(S["consts"], 1)

            def root(q, stage, k, eps_=LN_EPS):
                normed(pool, stage, "mv", q, k)
                if not isinstance(q, int):
                    pool.sem_inc(S["waits_passed"], 1)
                pool.tensor_scalar(rstd[stage][:, 0], mv[stage][:, :, 1], eps_, None, ALU.add).then_inc(
                    S[f"{stage}_var"], 1)
                normed(pool, stage, "var", q, k)
                pool.tensor_tensor(rstd[stage][:, 1], rstd[stage][:, 0], mhalf[:], ALU.pow).then_inc(
                    S[f"{stage}_rstd"], 1)

            def step(name, q):
                if name == "x_stats":
                    root(q, "s", 0)
                elif name == "scores":
                    for t in range(T):
                        since(pool, S["s_relu"], q, T, t + 1)
                        pool.tensor_tensor(s_e[:, t], s_e[:, t], s_t[:, t], ALU.add).then_inc(S["s_lrelu"], 1)
                elif name == "heads_stats":
                    since(pool, S["g_recip"], q, 1, 1)
                    pool.tensor_tensor(g_s[:, 1], g_s[:, 0], g_s[:, 0], ALU.mult).then_inc(S["g_recip2"], 1)
                    since(pool, S["g_recip2"], q, 1, 1)
                    normed(pool, "g", "mv", q, 0)
                    pool.tensor_tensor(rstd["g"][:, 2], mv["g"][:, :, 1], g_s[:, 1], ALU.mult).then_inc(S["g_v1"], 1)
                    since_apart(pool, S["g_v1"], q, 1, 1)
                    pool.tensor_scalar(rstd["g"][:, 0], rstd["g"][:, 2], LN_EPS, None, ALU.add).then_inc(
                        S["g_var"], 1)
                    normed(pool, "g", "var", q, 0)
                    pool.tensor_tensor(rstd["g"][:, 3], rstd["g"][:, 0], mhalf[:], ALU.pow).then_inc(S["g_v2"], 1)
                    since(pool, S["g_v2"], q, 1, 1)
                    pool.tensor_tensor(rstd["g"][:, 1], rstd["g"][:, 3], g_s[:, 0], ALU.mult).then_inc(
                        S["g_rstd"], 1)
                elif name == "gat_out":
                    normed(pool, "g", "y", q, 0)
                    pool.tensor_tensor(g_y2[:], y["g"][:], row4(R_GG), ALU.mult).then_inc(S["g_gain"], 1)
                    since(pool, S["g_gain"], q, 1, 1)
                    pool.tensor_tensor(g_y2[:], g_y2[:], row4(R_GB), ALU.add).then_inc(S["g_shift"], 1)
                elif name == "gat_low":
                    since(pool, S["g_hghi"], q, 1, 1)
                    pool.tensor_tensor(g_hghl[:, 1], g_hg[:], g_hghl[:, 0], ALU.subtract).then_inc(S["g_hglo"], 1)
                elif name == "mlp_stats":
                    root(q, "f", 0, LN_EPS * WS * WS)
                elif name == "mlp_low":
                    since(pool, S["g_zhi"], q, 1, 1)
                    pool.tensor_tensor(g_fT[:, 1], flat(g_z[:]), g_fT[:, 0], ALU.subtract).then_inc(S["g_zlo"], 1)
                elif name == "l2_stats":
                    root(q, "m", 0)
                elif name == "l3_stats":
                    root(q, "m", 1)
                elif name == "l3_add":
                    since_apart(pool, S["m_relu"], q, 1, 1)
                    pool.tensor_tensor(x_all[:, q], m_t, x_all[:, q], ALU.add).then_inc(S["x3_done"], 1)
                elif name == "l4_stats":
                    root(q, "p", 0)
                elif name == "late_high":
                    since(pool, S["p_gs"], q, 1, 1)
                    pool.tensor_tensor(p_g2, p_g, p_s[:, 5].unsqueeze(2).broadcast_to([P, T, P]),
                                       ALU.mult).then_inc(S["p_g2"], 1)
                elif name == "late_low":
                    since(pool, S["p_g2hi"], q, 1, 1)
                    pool.tensor_tensor(p_g2hl[:, 1], p_g2, p_g2hl[:, 0], ALU.subtract).then_inc(S["p_g2lo"], 1)

            run(pool, ORDER["pool"], step, lambda i: None)

        @block.scalar
        def _(act):
            act.wait_ge(S["w_loaded"], 160)
            act.activation(w_hl[:, 0], w_raw[:], ACT.Copy, scale=WS).then_inc(S["w_hi"], 1)

            def prepare(i):
                if i == 3:
                    act.wait_ge(S["edge_max"], 1)
                    for t in range(T):
                        ins = act.activation(wk1[:, t], wk2[:, t], ACT.Exp, bias=small[:, 6, t:t + 1],
                                             accum_out=small[:, 7, t:t + 1])
                    ins.then_inc(S["edge_exp"], 1)
                if i == 5:
                    act.wait_ge(S["degrees"], 1)
                    act.activation(small[:, 1], small[:, 0], ACT.Sqrt).then_inc(S["degree_roots"], 1)

            def step(name, q):
                if name == "x_turn":
                    since(act, S["s_turned"], q, 1, 1)
                    act.activation(s_fT[:, 0], bank[0][:], ACT.Relu).then_inc(S["s_hi"], 1)
                elif name == "project":
                    since(act, S["s_proj"], q, 1, 1)
                    since(act, S["g_heads"], q, 1, 0)
                    act.activation(flat(s_h1[:]), bank[0][:], ACT.Copy, scale=1.0 / WS).then_inc(S["s_h1"], 1)
                elif name == "scores":
                    since(act, S["g_turned"], q, T, 0)
                    since(act, S["g_recip"], q, 1, 0)
                    since(act, S["s_src"], q, 1, 1)
                    for t in range(T):
                        since(act, S["s_max"], q, T, t + 1)
                        act.activation(s_e[:, t], s_t[:, t], ACT.Relu, bias=s_s[:, 0, t:t + 1],
                                       scale=4.0).then_inc(S["s_relu"], 1)
                elif name == "exp":
                    since(act, S["s_negmax"], q, 1, 1)
                    for t in range(T):
                        since(act, S["s_lrelu"], q, T, t + 1)
                        act.activation(s_e[:, t], s_e[:, t], ACT.Exp, bias=s_s[:, 4, t:t + 1],
                                       accum_out=s_s[:, 5, t:t + 1]).then_inc(S["s_exp"], 1)
                elif name == "gat_out":
                    since(act, S["g_shift"], q, 1, 1)
                    since(act, S["g_t"], q, 1, 0)
                    since(act, S["g_sum"], q, 1, 0)
                    act.activation(g_hg[:], g_y2[:], ACT.Relu).then_inc(S["g_hg"], 1)
                    act.activation(g_hghl[:, 0], g_y2[:], ACT.Relu).then_inc(S["g_hghi"], 1)
                elif name == "gin":
                    since(act, S["g_sum"], q, 1, 1)
                    act.activation(g_fT[:, 0], bank[1][:], ACT.Copy).then_inc(S["g_hi"], 1)
                elif name == "mlp_turn":
                    since(act, S["g_zturned"], q, 1, 1)
                    act.activation(flat(g_z[:]), bank[1][:], ACT.Relu, bias=mlp_col[:, 1:2],
                                   scale=mlp_col[:, 0:1]).then_inc(S["g_zr"], 1)
                    since(act, S["g_zr"], q, 1, 1)
                    act.activation(g_fT[:, 0], flat(g_z[:]), ACT.Copy).then_inc(S["g_zhi"], 1)
                elif name in ("l2_high", "l3_high"):
                    k = 0 if name == "l2_high" else 1
                    normed(act, "m", "y", q, k)
                    act.activation(m_h[:, 0], y["m"][:], ACT.Relu).then_inc(S["m_hi"], 1)
                elif name == "off":
                    since(act, S["m_off"], q, 1, 1)
                    act.activation(m_1[:, 0], bank[4][:], ACT.Copy).then_inc(S["m_off_hi"], 1)
                elif name == "own":
                    since(act, S["m_own"], q, 1, 1)
                    act.activation(m_2[:, 0], bank[5][:], ACT.Copy).then_inc(S["m_own_hi"], 1)
                elif name == "lap":
                    since(act, S["m_lap"], q, 1, 1)
                    act.activation(m_1[:, 0], bank[4][:], ACT.Copy).then_inc(S["m_lap_hi"], 1)
                elif name == "cheb":
                    since(act, S["m_cheb"], q, 1, 1)
                    act.activation(m_2[:, 0], bank[5][:], ACT.Copy).then_inc(S["m_cheb_hi"], 1)
                elif name == "l3_turn":
                    since(act, S["m_turned"], q, 1, 1)
                    act.activation(m_hT[:], halves(bank[4]), ACT.Copy).then_inc(S["m_hT"], 1)
                elif name == "l3_out":
                    since(act, S["m_mix3"], q, 1, 1)
                    act.activation(flat(m_t), bank[5][:], ACT.Relu, scale=1.0 / WS).then_inc(S["m_relu"], 1)
                elif name == "l4_high":
                    normed(act, "p", "y", q, 0)
                    act.activation(p_h[:, 0], y["p"][:], ACT.Relu).then_inc(S["p_hi"], 1)
                elif name == "l4_turn":
                    since(act, S["p_turned"], q, 1, 1)
                    act.activation(p_hT, halves(bank[6]), ACT.Copy).then_inc(S["p_hT"], 1)
                elif name == "pair_rows":
                    since(act, S["p_vec"], q, 1, 1)
                    act.activation(p_lv, pair_view, ACT.Copy, scale=0.1).then_inc(S["p_tenth"], 1)
                elif name == "pair_cols":
                    since(act, S["p_vcol"], q, 1, 1)
                    act.activation(p_lw[:], bank[7][:, 0:2], ACT.Copy, scale=0.1).then_inc(S["p_wtenth"], 1)
                elif name == "pair_exp":
                    since(act, S["p_negmax"], q, 1, 1)
                    act.activation(p_s[:, 5], p_s[:, 4], ACT.Exp).then_inc(S["p_late"], 1)
                    for t in range(T):
                        ins = act.activation(p_e[:, t], p_te[:, t], ACT.Exp, bias=p_s[:, 3, t:t + 1],
                                             accum_out=p_s[:, 7, t:t + 1])
                    ins.then_inc(S["p_exp"], 1)
                elif name == "late_high":
                    since(act, S["p_g2"], q, 1, 1)
                    act.activation(p_g2hl[:, 0], p_g2, ACT.Copy).then_inc(S["p_g2hi"], 1)

            run(act, ORDER["act"], step, prepare)

        @block.vector
        def _(dve):
            n = 0

            def link(ins, named=None):
                nonlocal n
                if named:
                    ins.then_inc(S[named], 1)
                    dve.wait_ge(S[named], 1)
                else:
                    n += 1
                    ins.then_inc(S["dve_chain"], 1)
                    dve.wait_ge(S["dve_chain"], n)

            dve.wait_ge(S["consts"], 1)
            for t in range(T):
                dve.wait_ge(S["adj_turned"], t + 1)
                ins = dve.tensor_copy(adj_t[:, t], bank[t][:])
            link(ins)
            link(dve.tensor_scalar(gat_mask[:], adj_n[:], 0.0, FLOAT_MIN, ALU.is_le, ALU.mult))
            dve.wait_ge(S["w_hi"], 1)
            dve.wait_ge(S["rows_loaded"], 16 * 18)
            link(dve.scalar_tensor_tensor(out=w_hl[:, 1].rearrange("p a b -> p (a b)"),
                                          in0=w_raw[:].rearrange("p a b -> p (a b)"), scalar=WS,
                                          in1=w_hl[:, 0].rearrange("p a b -> p (a b)"),
                                          op0=ALU.mult, op1=ALU.subtract))
            for k, (w, r) in enumerate(((WP, R_ASRC), (WP, R_ADST), (L3O, R_A1), (L3O, R_A2))):
                link(dve.tensor_tensor_reduce(out=wk2[:, 0, 0:P], in0=w_raw[:, w], in1=rows[:, r], scale=1.0,
                                              scalar=0.0, op0=ALU.mult, op1=ALU.add,
                                              accum_out=score_w[:, k:k + 1]))
            link(dve.tensor_tensor(score_w[:, 4:5], score_w[:, 2:3], score_w[:, 3:4], ALU.add))
            link(dve.tensor_tensor(wk2[:, 1, 0:P], rows[:, R_ASRC], rows[:, R_ADST], ALU.add))
            link(dve.tensor_tensor_reduce(out=wk2[:, 0, 0:P], in0=wk2[:, 1, 0:P], in1=rows[:, R_BP], scale=1.0,
                                          scalar=0.0, op0=ALU.mult, op1=ALU.add, accum_out=score_w[:, 5:6]))
            link(dve.tensor_copy(col_hl[:, 0], score_w[:, 0:4]))
            link(dve.tensor_tensor(col_hl[:, 1], score_w[:, 0:4], col_hl[:, 0], ALU.subtract))
            for o, k in ((dst_hl, 1), (pair_hl, 4)):
                link(dve.tensor_scalar(wk2[:, 0, 0:P], ones[:], score_w[:, k:k + 1], None, ALU.mult))
                link(dve.tensor_copy(o[:, 0], wk2[:, 0, 0:P]))
                link(dve.tensor_tensor(o[:, 1], wk2[:, 0, 0:P], o[:, 0], ALU.subtract))
            link(dve.memset(small[:, 14], 0.0), "score_weights")

            for k, r in enumerate((R_BP, R_B1, R_B2, R_L1, R_L2)):
                b_hi, b_lo = bias_hl[:, k], wk1[:, 0].rearrange("p (t d) -> p t d", t=T)
                link(dve.tensor_scalar(b_hi, row4(r), WS, None, ALU.mult))
                link(dve.scalar_tensor_tensor(out=b_lo, in0=row4(r), scalar=WS, in1=b_hi, op0=ALU.mult,
                                              op1=ALU.subtract))
                link(dve.tensor_scalar(b_lo, b_lo, ident[:, 1:2], None, ALU.mult))
                link(dve.scalar_tensor_tensor(out=b_hi, in0=b_hi, scalar=ident[:, 0:1], in1=b_lo, op0=ALU.mult,
                                              op1=ALU.add), "biases" if k == 4 else None)

            def split(o, src):
                link(dve.tensor_copy(o[:, 0], src))
                link(dve.tensor_tensor(o[:, 1], src, o[:, 0], ALU.subtract))

            def diag_block(m, t):
                return m[:, t, t * P:(t + 1) * P]

            def prepare(i):
                if i == 0:
                    link(dve.tensor_scalar(eps1[:], eps1[:], 1.0, None, ALU.add))
                    link(dve.tensor_copy(wk3, adj_t[:]))
                    for t in range(T):
                        dg = diag_block(wk3, t)
                        ins = dve.scalar_tensor_tensor(out=dg, in0=ident[:], scalar=eps1[:], in1=dg,
                                                       op0=ALU.mult, op1=ALU.add)
                    link(ins)
                    split(gin_t, wk3)
                    link(dve.tensor_scalar(pair_mask[:], adj_t[:, :, 0:H], 0.0, NEG_BIG, ALU.is_le, ALU.mult))
                    link(dve.tensor_scalar(wk1, adj_t[:], 0.0, None, ALU.is_gt))
                    link(dve.tensor_reduce(small[:, 8], wk1, AX_X, ALU.add))
                    link(dve.tensor_reduce(small[:, 9], wk1[:, :, H:N], AX_X, ALU.add))
                    link(dve.tensor_scalar(small[:, 10], small[:, 8], 0.0, None, ALU.is_equal))
                    link(dve.tensor_scalar(late_neg[:], small[:, 9], 0.0, NEG_BIG, ALU.is_equal, ALU.mult))
                    link(dve.scalar_tensor_tensor(out=late_cnt[:], in0=small[:, 10], scalar=float(H),
                                                  in1=small[:, 9], op0=ALU.mult, op1=ALU.add))
                    link(dve.tensor_tensor(late_mask[:], wk1[:, :, H:N],
                                           small[:, 10].unsqueeze(2).broadcast_to([P, T, H]), ALU.add))
                if i == 1:
                    for t in range(T):
                        link(dve.tensor_scalar(wk1[:, t], adj_n[:, t], 0.0, None, ALU.is_gt))
                        link(dve.tensor_tensor_scan(wk2[:, t], wk1[:, t], wk1[:, t], 0.0, ALU.add, ALU.max))
                    link(dve.tensor_copy(small[:, 2], wk2[:, :, N - 1]), "row_counts")
                if i == 2:
                    dve.wait_ge(S["row_starts"], 1)
                    link(dve.tensor_copy(small[:, 3], bank[4][:, 0:T]))
                    link(dve.tensor_tensor(small[:, 4], small[:, 3], small[:, 2], ALU.add))
                    for t in range(T):
                        link(dve.tensor_scalar(wk3[:, t, 0:P], krow[:], small[:, 3, t:t + 1], None, ALU.is_ge))
                        link(dve.scalar_tensor_tensor(out=pick_t[:, t], in0=krow[:], scalar=small[:, 4, t:t + 1],
                                                      in1=wk3[:, t, 0:P], op0=ALU.is_lt, op1=ALU.mult))
                        link(dve.scalar_tensor_tensor(out=wk2[:, t], in0=wk2[:, t], scalar=small[:, 3, t:t + 1],
                                                      in1=wk1[:, t], op0=ALU.add, op1=ALU.mult))
                    link(dve.tensor_scalar(q16[:], wk2, float(N), None, ALU.min), "pick_ready")
                    for t in range(T):
                        link(dve.tensor_scalar(wk1[:, t], wk2[:, t], float(P), e_last[:], ALU.is_gt, ALU.mult))
                    link(dve.tensor_scalar(small[:, 5, 0:1], kcol[:], 1.0, None, ALU.add))
                    dve.wait_ge(S["picked"], 1)
                    link(dve.tensor_scalar(wk3[:, 0], bank[5][:], small[:, 5, 0:1], None, ALU.is_equal))
                    link(dve.tensor_scalar(wk3[:, 1], bank[6][:], e_col[:], None, ALU.mult), "edge_values")
                if i == 3:
                    for t in range(T):
                        dve.wait_ge(S["spread"], t + 1)
                        link(dve.tensor_tensor(wk1[:, t], wk1[:, t], bank[4 + t][:], ALU.add))
                    link(dve.tensor_scalar(wk2, adj_n[:], 0.0, NEG_BIG, ALU.is_le, ALU.mult))
                    link(dve.tensor_tensor(wk2, wk2, wk1, ALU.add))
                    link(dve.tensor_reduce(small[:, 6], wk2, AX_X, ALU.max, negate=True), "edge_max")
                if i == 4:
                    dve.wait_ge(S["edge_exp"], 1)
                    link(dve.reciprocal(small[:, 11], small[:, 7]))
                    for t in range(T):
                        ins = dve.tensor_scalar(wk2[:, t], wk1[:, t], small[:, 11, t:t + 1], None, ALU.mult)
                    link(ins, "att_rows")
                    for t in range(T):
                        dve.wait_ge(S["att_turned"], t + 1)
                        link(dve.tensor_copy(wk1[:, t], bank[4 + t][:]))
                        dg, own = diag_block(wk1, t), wk3[:, 0, t * P:(t + 1) * P]
                        link(dve.tensor_tensor(own, dg, ident[:], ALU.mult))
                        link(dve.tensor_tensor(dg, dg, own, ALU.subtract))
                    split(att_d, wk3[:, 0].rearrange("p (t n) -> p t n", t=T))
                    split(att_t, wk1)
                if i == 5:
                    link(dve.tensor_reduce(small[:, 0], adj_n[:], AX_X, ALU.add), "degrees")
                    dve.wait_ge(S["degree_roots"], 1)
                    link(dve.reciprocal(small[:, 12], small[:, 1]))
                    for t in range(T):
                        ins = dve.tensor_scalar(wk3[:, 1, t * P:(t + 1) * P], ident[:], small[:, 12, t:t + 1], None,
                                                ALU.mult)
                    link(ins, "d_diag")
                    dve.wait_ge(S["d_spread"], 1)
                    for t in range(T):
                        ins = dve.scalar_tensor_tensor(out=wk1[:, t], in0=adj_n[:, t], scalar=small[:, 12, t:t + 1],
                                                       in1=bank[4][:], op0=ALU.mult, op1=ALU.mult)
                    link(ins)
                    link(dve.tensor_scalar(wk1, wk1, -1.0, None, ALU.mult))
                    for t in range(T):
                        ins = dve.tensor_tensor(diag_block(wk1, t), diag_block(wk1, t), ident[:], ALU.add)
                    link(ins, "lap_rows")
                if i == 6:
                    for t in range(T):
                        dve.wait_ge(S["lap_turned"], t + 1)
                        ins = dve.tensor_copy(wk2[:, t], bank[4 + t][:])
                    link(ins, "lap_cols")
                    split(lap_t, wk2)
                if i == 7:
                    for t in range(T):
                        dve.wait_ge(S["lap_squared"], t + 1)
                        link(dve.tensor_scalar(wk3[:, t], bank[4 + t][:], 2.0, None, ALU.mult))
                        link(dve.tensor_tensor(diag_block(wk3, t), diag_block(wk3, t), ident[:], ALU.subtract))
                    split(cheb_t, wk3)
                    link(dve.memset(small[:, 15], 0.0), "prepared")

            def measure(q, stage, k, src):
                for t in range(T):
                    ins = dve.bn_stats(stats[stage][:, t], src(t))
                ins.then_inc(S[f"{stage}_stats"], 1)
                since_apart(dve, S[f"{stage}_stats"], q, norms[stage], k + 1)
                for t in range(T):
                    ins = dve.bn_aggr(mv[stage][:, t], stats[stage][:, t])
                ins.then_inc(S[f"{stage}_mv"], 1)

            def apply(q, stage, k, src):
                normed(dve, stage, "rstd", q, k)
                for t in range(T):
                    ins = dve.tensor_scalar(y[stage][:, t], src(t), mv[stage][:, t, 0:1],
                                            rstd[stage][:, 1, t:t + 1], ALU.subtract, ALU.mult)
                ins.then_inc(S[f"{stage}_y"], 1)

            def low(out_, src, hi, floor=None):
                op = ALU.max if floor is not None else ALU.mult
                return dve.scalar_tensor_tensor(out=out_, in0=src, scalar=0.0 if floor is not None else 1.0,
                                                in1=hi, op0=op, op1=ALU.subtract)

            def step(name, q):
                if name == "x_stats":
                    dve.wait_ge(S["x0_loaded" if isinstance(q, int) and q == 0 else "x_loaded"], 16)
                    measure(q, "s", 0, lambda t: x_all[:, q, t])
                elif name == "x_apply":
                    apply(q, "s", 0, lambda t: x_all[:, q, t])
                elif name == "x_low":
                    since(dve, S["s_hi"], q, 1, 1)
                    low(s_fT[:, 1], bank[0][:], s_fT[:, 0], 0.0).then_inc(S["s_lo"], 1)
                elif name == "score_src":
                    since(dve, S["s_rows"], q, 1, 1)
                    dve.tensor_scalar(s_s[:, 0], bank[0][:, 0:T], score_w[:, 5:6], 0.8, ALU.add,
                                      ALU.mult).then_inc(S["s_src"], 1)
                elif name == "scores":
                    since_apart(dve, S["s_rows"], q, 1, 1)
                    for t in range(T):
                        dve.tensor_tensor_reduce(out=s_t[:, t], in0=bank[1][:], in1=gat_mask[:, t], scale=0.2,
                                                 scalar=FLOAT_MIN, op0=ALU.add, op1=ALU.max,
                                                 accum_out=s_s[:, 1, t:t + 1]).then_inc(S["s_max"], 1)
                elif name == "negmax":
                    since(dve, S["s_src"], q, 1, 1)
                    since(dve, S["s_max"], q, T, T)
                    dve.scalar_tensor_tensor(out=s_s[:, 2], in0=s_s[:, 1], scalar=4.0, in1=s_s[:, 0],
                                             op0=ALU.mult, op1=ALU.add).then_inc(S["s_step"], 1)
                    since(dve, S["s_step"], q, 2, 1)
                    dve.scalar_tensor_tensor(out=s_s[:, 3], in0=s_s[:, 2], scalar=0.0, in1=s_s[:, 1],
                                             op0=ALU.max, op1=ALU.add).then_inc(S["s_step"], 1)
                    since(dve, S["s_step"], q, 2, 2)
                    dve.tensor_scalar(s_s[:, 4], s_s[:, 3], -1.0, None, ALU.mult).then_inc(S["s_negmax"], 1)
                elif name in ("weigh", "weigh2"):
                    for t in (range(TH) if name == "weigh" else range(TH, T)):
                        since(dve, S["g_turned"], q, T, t + 1)
                        dve.tensor_tensor(g_pt[:, :, t * P:(t + 1) * P],
                                          bank[2 + t % 2][:].rearrange("p (j m) -> p j m", j=T),
                                          adj_t[:, :, t * P:(t + 1) * P], ALU.mult).then_inc(S["g_weighed"], 1)
                    if name == "weigh":
                        since(dve, S["s_exp"], q, T, T)
                        dve.reciprocal(g_s[:, 0], s_s[:, 5]).then_inc(S["g_recip"], 1)
                elif name == "heads_stats":
                    since(dve, S["g_heads"], q, 1, 1)
                    measure(q, "g", 0, lambda t: bank[2][:, t * P:(t + 1) * P])
                elif name == "heads_apply":
                    since(dve, S["g_gain"], q, 1, 0)
                    apply(q, "g", 0, lambda t: bank[2][:, t * P:(t + 1) * P])
                elif name == "gin_low":
                    since(dve, S["g_hi"], q, 1, 1)
                    low(g_fT[:, 1], bank[1][:], g_fT[:, 0]).then_inc(S["g_lo"], 1)
                elif name == "mlp_stats":
                    since(dve, S["g_z"], q, 1, 1)
                    measure(q, "f", 0, lambda t: bank[0][:, t * P:(t + 1) * P])
                elif name == "mlp_apply":
                    apply(q, "f", 0, lambda t: bank[0][:, t * P:(t + 1) * P])
                elif name == "mlp_out":
                    since(dve, S["g_out"], q, 1, 1)
                    dve.scalar_tensor_tensor(out=flat(g_z[:]), in0=bank[0][:], scalar=1.0 / WS, in1=flat(g_hg[:]),
                                             op0=ALU.mult, op1=ALU.add).then_inc(S["g_t"], 1)
                    since(dve, S["g_t"], q, 1, 1)
                    dve.scalar_tensor_tensor(out=x_all[:, q], in0=g_z[:], scalar=0.0, in1=x_all[:, q],
                                             op0=ALU.max, op1=ALU.add).then_inc(S["x1_done"], 1)
                elif name in ("l2_stats", "l3_stats"):
                    k = 0 if name == "l2_stats" else 1
                    since_apart(dve, S["x1_done" if k == 0 else "x2_done"], q, 1, 1)
                    measure(q, "m", k, lambda t: x_all[:, q, t])
                elif name in ("l2_apply", "l3_apply"):
                    apply(q, "m", 0 if name == "l2_apply" else 1, lambda t: x_all[:, q, t])
                elif name in ("l2_low", "l3_low"):
                    since(dve, S["m_hi"], q, 2, 1 if name == "l2_low" else 2)
                    low(flat(m_h[:, 1]), flat(y["m"][:]), flat(m_h[:, 0]), 0.0).then_inc(S["m_lo"], 1)
                elif name == "off_low":
                    since(dve, S["m_off_hi"], q, 1, 1)
                    low(m_1[:, 1], bank[4][:], m_1[:, 0]).then_inc(S["m_off_lo"], 1)
                elif name == "own_low":
                    since(dve, S["m_own_hi"], q, 1, 1)
                    low(m_2[:, 1], bank[5][:], m_2[:, 0]).then_inc(S["m_own_lo"], 1)
                elif name == "l2_out":
                    since(dve, S["m_mix"], q, 1, 1)
                    dve.scalar_tensor_tensor(out=x_all[:, q], in0=bank[4][:].rearrange("p (t d) -> p t d", t=T),
                                             scalar=1.0 / WS, in1=x_all[:, q], op0=ALU.mult,
                                             op1=ALU.add).then_inc(S["x2_done"], 1)
                elif name == "lap_low":
                    since(dve, S["m_lap_hi"], q, 1, 1)
                    low(m_1[:, 1], bank[4][:], m_1[:, 0]).then_inc(S["m_lap_lo"], 1)
                elif name == "cheb_low":
                    since(dve, S["m_cheb_hi"], q, 1, 1)
                    low(m_2[:, 1], bank[5][:], m_2[:, 0]).then_inc(S["m_cheb_lo"], 1)
                elif name == "l4_stats":
                    since_apart(dve, S["x3_done"], q, 1, 1)
                    measure(q, "p", 0, lambda t: x_all[:, q, t])
                elif name == "l4_apply":
                    apply(q, "p", 0, lambda t: x_all[:, q, t])
                elif name == "l4_low":
                    since(dve, S["p_hi"], q, 1, 1)
                    low(flat(p_h[:, 1]), flat(y["p"][:]), flat(p_h[:, 0]), 0.0).then_inc(S["p_lo"], 1)
                elif name == "pair_lrelu":
                    since(dve, S["p_tenth"], q, 1, 1)
                    dve.tensor_tensor(p_lv, p_lv, pair_view, ALU.max).then_inc(S["p_lv"], 1)
                elif name == "pair_mask":
                    since_apart(dve, S["p_lv"], q, 1, 1)
                    for t in range(T):
                        dve.tensor_tensor_reduce(out=p_te[:, t], in0=p_lv[:, t // TH], in1=pair_mask[:, t],
                                                 scale=1.0, scalar=FLOAT_MIN, op0=ALU.add, op1=ALU.max,
                                                 accum_out=p_s[:, 0, t:t + 1]).then_inc(S["p_max"], 1)
                elif name == "pair_max":
                    since(dve, S["p_wtenth"], q, 1, 1)
                    dve.tensor_tensor(p_lw[:], p_lw[:], bank[7][:, 0:2], ALU.max).then_inc(S["p_lw"], 1)
                    since(dve, S["p_lw"], q, 1, 1)
                    dve.tensor_tensor(p_s[:, 1].rearrange("p (r c) -> p r c", c=2),
                                      p_lw[:].unsqueeze(1).broadcast_to([P, T // 2, 2]),
                                      late_neg[:].rearrange("p (r c) -> p r c", c=2),
                                      ALU.add).then_inc(S["p_step"], 1)
                    since(dve, S["p_step"], q, 4, 1)
                    since(dve, S["p_max"], q, T, T)
                    dve.tensor_tensor(p_s[:, 2], p_s[:, 0], p_s[:, 1], ALU.max).then_inc(S["p_step"], 1)
                    since(dve, S["p_step"], q, 4, 2)
                    dve.tensor_scalar(p_s[:, 3], p_s[:, 2], -1.0, None, ALU.mult)
                    dve.tensor_tensor(p_s[:, 4], p_s[:, 1], p_s[:, 2], ALU.subtract).then_inc(S["p_negmax"], 1)
                elif name == "pair_sums":
                    since(dve, S["p_late"], q, 1, 1)
                    dve.tensor_tensor(p_s[:, 8], p_s[:, 5], late_cnt[:], ALU.mult).then_inc(S["p_step"], 1)
                    since(dve, S["p_exp"], q, 1, 1)
                    since(dve, S["p_step"], q, 4, 3)
                    dve.tensor_tensor(p_s[:, 9], p_s[:, 8], p_s[:, 7], ALU.add).then_inc(S["p_step"], 1)
                    since(dve, S["p_step"], q, 4, 4)
                    dve.reciprocal(p_s[:, 10], p_s[:, 9]).then_inc(S["p_recip"], 1)
                elif name == "pair_scale":
                    since(dve, S["p_recip"], q, 1, 1)
                    since(dve, S["p_g"], q, 1, 1)
                    dve.tensor_tensor(p_g, bank[6][:].rearrange("p (t d) -> p t d", t=T),
                                      p_s[:, 10].unsqueeze(2).broadcast_to([P, T, P]),
                                      ALU.mult).then_inc(S["p_gs"], 1)
                elif name == "l4_out":
                    since(dve, S["p_out"], q, 1, 1)
                    dve.scalar_tensor_tensor(out=x_all[:, q], in0=bank[7][:].rearrange("p (t d) -> p t d", t=T),
                                             scalar=1.0 / WS, in1=x_all[:, q], op0=ALU.mult,
                                             op1=ALU.add).then_inc(S["x4_done"], 1)

            run(dve, ORDER["dve"], step, prepare)

        @block.tensor
        def _(pe):
            def turn_all(banks, src, sem):
                for j in range(T):
                    for t in range(T):
                        ins = pe.transpose(banks[j][:, t * P:(t + 1) * P], src[:, t, j * P:(j + 1) * P], ident[:])
                    ins.then_inc(sem, 1)

            pe.wait_ge(S["consts"], 1)
            pe.wait_ge(S["adj_loaded"], 16)
            turn_all(bank[0:4], adj_n, S["adj_turned"])

            def prepare(i):
                if i == 1:
                    pe.wait_ge(S["row_counts"], 1)
                    for t in range(T):
                        for k in range(t):
                            pe.matmul(bank[4][:, t:t + 1], ones[:], small[:, 2, k:k + 1], start=(k == 0), stop=False)
                        ins = pe.matmul(bank[4][:, t:t + 1], tri[:], small[:, 2, t:t + 1], start=(t == 0), stop=True)
                    ins.then_inc(S["row_starts"], 1)
                if i == 2:
                    pe.wait_ge(S["pick_ready"], 1)
                    for t in range(T):
                        pe.matmul(bank[5][:], pick_t[:, t], q16[:, t], start=(t == 0), stop=(t == T - 1))
                    for t in range(T):
                        ins = pe.matmul(bank[6][:, t * P:(t + 1) * P], pick_t[:, t], ident16[:], start=True, stop=True)
                    ins.then_inc(S["picked"], 1)
                    pe.wait_ge(S["edge_values"], 1)
                    for t in range(T):
                        pe.matmul(bank[4 + t][:], wk3[:, 1, t * P:(t + 1) * P], wk3[:, 0], start=True,
                                  stop=True).then_inc(S["spread"], 1)
                if i == 4:
                    pe.wait_ge(S["att_rows"], 1)
                    turn_all(bank[4:8], wk2, S["att_turned"])
                if i == 5:
                    pe.wait_ge(S["d_diag"], 1)
                    pe.matmul(bank[4][:], ones[:], wk3[:, 1], start=True, stop=True).then_inc(S["d_spread"], 1)
                if i == 6:
                    pe.wait_ge(S["lap_rows"], 1)
                    turn_all(bank[4:8], wk1, S["lap_turned"])
                if i == 7:
                    pe.wait_ge(S["lap_cols"], 1)
                    for j in range(T):
                        for k in range(T):
                            ins = pe.matmul(bank[4 + j][:], wk1[:, k, j * P:(j + 1) * P], wk2[:, k], start=(k == 0),
                                            stop=(k == T - 1))
                        ins.then_inc(S["lap_squared"], 1)
                    pe.wait_ge(S["prepared"], 1)

            def mm3(o, lh, ll, rh, rl, first, last):
                pe.matmul(o, lh, rh, start=first, stop=False)
                pe.matmul(o, lh, rl, start=False, stop=False)
                return pe.matmul(o, ll, rh, start=False, stop=last)

            def by_weight(b, parts, bias=None):
                if bias is not None:
                    pe.matmul(b[:], ones16[:], bias_hl[:, bias].rearrange("p t d -> p (t d)"), start=True,
                              stop=False)
                for t in range(T):
                    c = slice(t * P, (t + 1) * P)
                    for n, (f, w) in enumerate(parts):
                        last = n == len(parts) - 1 and (bias is None or t == T - 1)
                        ins = mm3(b[:, c], f[:, 0, c], f[:, 1, c], w_hl[:, 0, w], w_hl[:, 1, w],
                                  n == 0 and bias is None, last)
                return ins

            def over_nodes(b, h, m):
                for t in range(T):
                    ins = mm3(b[:], h[:, 0, t], h[:, 1, t], m[:, 0, t], m[:, 1, t], t == 0, t == T - 1)
                return ins

            def turn_parts(b, h):
                for part in range(2):
                    for t in range(T):
                        ins = pe.transpose(halves(b)[:, part, t * P:(t + 1) * P], h[:, part, t], ident16[:])
                return ins

            def passed_scores(sem, q, per):
                if not isinstance(q, int) or q + GAP < B:
                    since(pe, sem, q + GAP, per, per)

            def step(name, q):
                if name == "x_turn":
                    normed(pe, "s", "y", q, 0)
                    since(pe, S["x1_done"], q - GAP, 1, 0)
                    for t in range(T):
                        ins = pe.transpose(bank[0][:, t * P:(t + 1) * P], y["s"][:, t], ident[:])
                    ins.then_inc(S["s_turned"], 1)
                elif name == "score_rows":
                    since(pe, S["s_lo"], q, 1, 1)
                    since(pe, S["g_zr"], q - GAP, 1, 0)
                    mm3(bank[1][:], dst_hl[:, 0], dst_hl[:, 1], s_fT[:, 0], s_fT[:, 1], True, True)
                    for t in range(T):
                        c = slice(t * P, (t + 1) * P)
                        ins = mm3(bank[0][:, t:t + 1], s_fT[:, 0, c], s_fT[:, 1, c], col_hl[:, 0, 0:1],
                                  col_hl[:, 1, 0:1], True, True)
                    ins.then_inc(S["s_rows"], 1)
                elif name == "project":
                    since(pe, S["s_src"], q, 1, 1)
                    by_weight(bank[0], [(s_fT, WP)], 0).then_inc(S["s_proj"], 1)
                elif name in ("weigh", "weigh2"):
                    for t in (range(TH) if name == "weigh" else range(TH, T)):
                        since(pe, S["s_exp"], q, T, t + 1)
                        if t == 0:
                            normed(pe, "g", "y", q - 1, 0)
                        elif t == 1:
                            since(pe, S["g_weighed"], q, T, 0)
                        else:
                            since(pe, S["g_weighed"], q, T, t - 1)
                        for j in range(T):
                            ins = pe.transpose(bank[2 + t % 2][:, j * P:(j + 1) * P], s_e[:, t, j * P:(j + 1) * P],
                                               ident[:])
                        ins.then_inc(S["g_turned"], 1)
                elif name == "heads":
                    since(pe, S["g_weighed"], q, T, T)
                    since(pe, S["s_h1"], q, 1, 1)
                    for t in range(T):
                        for j in range(T):
                            ins = pe.matmul(bank[2][:, t * P:(t + 1) * P], g_pt[:, j, t * P:(t + 1) * P], s_h1[:, j],
                                            start=(j == 0), stop=(j == T - 1))
                    ins.then_inc(S["g_heads"], 1)
                elif name == "gin":
                    since(pe, S["g_hglo"], q, 1, 1)
                    passed_scores(S["s_max"], q, T)
                    over_nodes(bank[1], g_hghl, gin_t).then_inc(S["g_sum"], 1)
                elif name == "mlp_in":
                    since(pe, S["g_lo"], q, 1, 1)
                    passed_scores(S["s_h1"], q, 1)
                    by_weight(bank[0], [(g_fT, WZ)], 1).then_inc(S["g_z"], 1)
                elif name == "mlp_turn":
                    normed(pe, "f", "y", q, 0)
                    for t in range(T):
                        ins = pe.transpose(bank[1][:, t * P:(t + 1) * P], y["f"][:, t], ident[:])
                    ins.then_inc(S["g_zturned"], 1)
                elif name == "mlp_out":
                    since(pe, S["g_zlo"], q, 1, 1)
                    by_weight(bank[0], [(g_fT, WO2)], 2).then_inc(S["g_out"], 1)
                elif name == "off":
                    since(pe, S["m_lo"], q, 2, 1)
                    over_nodes(bank[4], m_h, att_t).then_inc(S["m_off"], 1)
                elif name == "own":
                    since(pe, S["m_lo"], q, 2, 1)
                    since(pe, S["m_relu"], q, 1, 0)
                    for t in range(T):
                        ins = mm3(bank[5][:, t * P:(t + 1) * P], m_h[:, 0, t], m_h[:, 1, t], att_d[:, 0, t],
                                  att_d[:, 1, t], True, True)
                    ins.then_inc(S["m_own"], 1)
                elif name == "l2_out":
                    since(pe, S["m_off_lo"], q, 1, 1)
                    since(pe, S["m_own_lo"], q, 1, 1)
                    by_weight(bank[4], [(m_2, L1A), (m_1, L1B)], 3).then_inc(S["m_mix"], 1)
                elif name == "lap":
                    since(pe, S["m_lo"], q, 2, 2)
                    over_nodes(bank[4], m_h, lap_t).then_inc(S["m_lap"], 1)
                elif name == "cheb":
                    since(pe, S["m_lo"], q, 2, 2)
                    over_nodes(bank[5], m_h, cheb_t).then_inc(S["m_cheb"], 1)
                elif name == "l3_turn":
                    since(pe, S["m_lap_lo"], q, 1, 1)
                    turn_parts(bank[4], m_h).then_inc(S["m_turned"], 1)
                elif name == "l3_out":
                    since(pe, S["m_hT"], q, 1, 1)
                    since(pe, S["m_cheb_lo"], q, 1, 1)
                    by_weight(bank[5], [(m_hT, L2A), (m_1, L2B), (m_2, L2C)], 4).then_inc(S["m_mix3"], 1)
                elif name == "l4_turn":
                    since(pe, S["p_lo"], q, 1, 1)
                    turn_parts(bank[6], p_h).then_inc(S["p_turned"], 1)
                elif name == "pair_rows":
                    since(pe, S["p_hT"], q, 1, 1)
                    mm3(bank[7][:], pair_hl[:, 0], pair_hl[:, 1], p_hT[:, 0], p_hT[:, 1], True,
                        True).then_inc(S["p_vec"], 1)
                elif name == "pair_feats":
                    since(pe, S["p_hT"], q, 1, 1)
                    by_weight(bank[6], [(p_hT, L3O)]).then_inc(S["p_g"], 1)
                elif name == "pair_cols":
                    since(pe, S["p_lv"], q, 1, 1)
                    for c in range(2):
                        ev = slice(c * H, (c + 1) * H, 2)
                        od = slice(c * H + 1, (c + 1) * H, 2)
                        mm3(bank[7][:, c:c + 1], p_hT[:, 0, ev], p_hT[:, 1, ev], col_hl[:, 0, 2:3],
                            col_hl[:, 1, 2:3], True, False)
                        ins = mm3(bank[7][:, c:c + 1], p_hT[:, 0, od], p_hT[:, 1, od], col_hl[:, 0, 3:4],
                                  col_hl[:, 1, 3:4], False, True)
                    ins.then_inc(S["p_vcol"], 1)
                elif name == "l4_out":
                    since(pe, S["p_lw"], q, 1, 1)
                    since(pe, S["p_exp"], q, 1, 1)
                    since(pe, S["p_gs"], q, 1, 1)
                    since(pe, S["p_g2lo"], q, 1, 1)
                    for t in range(T):
                        c = slice(t * P, (t + 1) * P)
                        mm3(bank[7][:, c], p_hT[:, 0, c], p_hT[:, 1, c], w_hl[:, 0, L3S], w_hl[:, 1, L3S], True,
                            False)
                        for j in range(T):
                            if t < TH:
                                ins = pe.matmul(bank[7][:, c], p_e[:, j, c], p_g[:, j], start=False,
                                                stop=(j == T - 1))
                            else:
                                r = slice((t - TH) * P, (t - TH + 1) * P)
                                pe.matmul(bank[7][:, c], late_mask[:, j, r], p_g2hl[:, 0, j], start=False, stop=False)
                                ins = pe.matmul(bank[7][:, c], late_mask[:, j, r], p_g2hl[:, 1, j], start=False,
                                                stop=(j == T - 1))
                    ins.then_inc(S["p_out"], 1)

            run(pe, ORDER["pe"], step, prepare)


_INS = ['x', 'adj', 'L0_gnn_Wp', 'L0_gnn_bp', 'L0_gnn_a_src', 'L0_gnn_a_dst', 'L0_gnn_gat_g', 'L0_gnn_gat_b',
        'L0_gnn_eps', 'L0_gnn_W1', 'L0_gnn_b1', 'L0_gnn_mlp_g', 'L0_gnn_mlp_b', 'L0_gnn_W2', 'L0_gnn_b2', 'L1_gnn_W',
        'L1_gnn_e', 'L1_gnn_bias', 'L2_gnn_weight', 'L2_gnn_bias', 'L3_gnn_others_weight', 'L3_gnn_self_weight',
        'L3_gnn_att_weight']


def kernel(**inputs):
    import numpy as _np
    import concourse.bacc as _bacc
    from concourse import mybir as _mybir
    from concourse.bass_utils import run_bass_kernel_spmd as _run

    nc = _bacc.Bacc("TRN2", target_bir_lowering=False, num_devices=1)
    arrays, args = {}, []
    for name in _INS:
        a = _np.ascontiguousarray(inputs[name])
        arrays[f"in_{name}_dram"] = a
        args.append(nc.dram_tensor(f"in_{name}_dram", a.shape, _mybir.dt.from_np(a.dtype), kind="ExternalInput").ap())
    shape = inputs["x"].shape
    args.append(nc.dram_tensor("out_dram", shape, _mybir.dt.float32, kind="ExternalOutput").ap())
    build(nc, *args)
    r = _run(nc, [arrays], core_ids=[0])
    return r.results[0]["out_dram"]
```

```python
from contextlib import ExitStack

import concourse.bass as bass
from concourse import mybir

P = 128
ALU = mybir.AluOpType
ACT = mybir.ActivationFunctionType
F32 = mybir.dt.float32
F16 = mybir.dt.float16
AX_X = mybir.AxisListType.X

FLOAT_MIN = -3.4028234663852886e38
NEG_BIG = -9.0e15
LN_EPS = 1e-5
WS = 64.0


def build(nc, x, adj, Wp, bp, a_src, a_dst, gat_g, gat_b, eps, W1, b1, mlp_g, mlp_b, W2, b2,
          L1_W, L1_e, L1_bias, L2_weight, L2_bias, L3_others, L3_self, L3_att, out):
    B, N, D = x.shape
    T = N // P
    H = N // 2
    TH = T // 2
    assert D == P and N == 512 and L1_e.shape[1] == P

    WP, WZ, WO2, L1A, L1B, L2A, L2B, L2C, L3O, L3S = range(10)
    (R_BP, R_B1, R_B2, R_L1, R_L2, R_ASRC, R_ADST, R_GG, R_GB, R_A1, R_A2) = range(11)
    BIASES = 5

    with ExitStack() as ctx:
        def sb(name, shape, dt=F32):
            return ctx.enter_context(nc.sbuf_tensor(name, shape, dt))

        def ps(name, shape=(P, 512), dt=F32):
            return ctx.enter_context(nc.psum_tensor(name, list(shape), dt))

        x_all = sb("x_all", [P, B, T, P])
        adj_n = sb("adj_n", [P, T, N])
        adj_t = sb("adj_t", [P, T, N])
        gat_mask = sb("gat_mask", [P, T, N])
        pair_mask = sb("pair_mask", [P, T, H])
        late_mask = sb("late_mask", [P, T, H], F16)
        late_neg = sb("late_neg", [P, T])
        late_cnt = sb("late_cnt", [P, T])
        gin_t = sb("gin_t", [P, 2, T, N], F16)
        att_t = sb("att_t", [P, 2, T, N], F16)
        att_d = sb("att_d", [P, 2, T, P], F16)
        lap_t = sb("lap_t", [P, 2, T, N], F16)
        cheb_t = sb("cheb_t", [P, 2, T, N], F16)
        w_raw = sb("w_raw", [P, 10, P])
        w_hl = sb("w_hl", [P, 2, 10, P], F16)
        rows = sb("rows", [P, 11, P])
        e_col = sb("e_col", [P, 1])
        mlp_col = sb("mlp_col", [P, 2])
        e_last = sb("e_last", [P, 1])
        eps1 = sb("eps1", [P, 1])
        ident = sb("ident", [P, P])
        ident16 = sb("ident16", [P, P], F16)
        ones = sb("ones", [P, P])
        ones16 = sb("ones16", [P, P], F16)
        bias_hl = sb("bias_hl", [P, BIASES, P], F16)
        mhalf = sb("mhalf", [P, T])
        score_w = sb("score_w", [P, 6])
        col_hl = sb("col_hl", [P, 2, 4], F16)
        dst_hl = sb("dst_hl", [P, 2, P], F16)
        pair_hl = sb("pair_hl", [P, 2, P], F16)
        work = sb("work", [P, 3 * T * N])

        def area(at, per_part, inner):
            return work[:, at:at + per_part * inner].rearrange("p (a b) -> p a b", b=inner)

        wk1, wk2, wk3 = (area(k * T * N, T, N) for k in range(3))
        m_t, p_g, p_g2 = (area(k * T * P, T, P) for k in range(3))
        p_te, p_e = (area(3 * T * P + k * T * H, T, H) for k in range(2))
        rest = 3 * T * P + 2 * T * H
        p_lv = area(rest, 2, H)
        p_h, p_g2hl = (work[:, rest + k * T * P:rest + (k + 1) * T * P].bitcast(F16)
                       .rearrange("p (h t d) -> p h t d", h=2, t=T) for k in (1, 2))
        p_hT = work[:, rest + 3 * T * P:rest + 4 * T * P].bitcast(F16).rearrange("p (h n) -> p h n", h=2)
        assert rest + 4 * T * P <= 3 * T * N
        tri = sb("tri", [P, P])
        kcol = sb("kcol", [P, 1])
        krow = sb("krow", [P, P])
        small = sb("small", [P, 16, T])
        pick_t = sb("pick_t", [P, T, P], F16)
        q16 = sb("q16", [P, T, N], F16)

        stages = "sgfmnp"
        stats = {k: sb(f"{k}_stats", [P, T, 6]) for k in stages}
        mv = {k: sb(f"{k}_mv", [P, T, 2]) for k in stages}
        rstd = {k: sb(f"{k}_rstd", [P, 4, T]) for k in stages}
        y = {k: sb(f"{k}_y", [P, T, P]) for k in stages if k != "n"}
        y["n"] = adj_n[:, 0].rearrange("p (t d) -> p t d", t=T)
        n_h = adj_n[:, 1].bitcast(F16).rearrange("p (h t d) -> p h t d", h=2, t=T)
        n_1, n_2 = (adj_n[:, k].bitcast(F16).rearrange("p (h n) -> p h n", h=2) for k in (2, 3))
        s_fT = sb("s_fT", [P, 2, N], F16)
        s_h1 = sb("s_h1", [P, T, P])
        s_s = sb("s_s", [P, 6, T])
        s_t = sb("s_t", [P, T, N])
        s_e = sb("s_e", [P, T, N])
        g_s = sb("g_s", [P, 2, T])
        g_pt = sb("g_pt", [P, T, N])
        g_y2 = sb("g_y2", [P, T, P])
        g_hg = sb("g_hg", [P, T, P])
        g_hghl = sb("g_hghl", [P, 2, T, P], F16)
        g_fT = sb("g_fT", [P, 2, N], F16)
        g_z = sb("g_z", [P, T, P])
        m_h = sb("m_h", [P, 2, T, P], F16)
        n_hT = sb("n_hT", [P, 2, N], F16)
        m_1 = sb("m_1", [P, 2, N], F16)
        m_2 = sb("m_2", [P, 2, N], F16)
        p_lw = sb("p_lw", [P, 2])
        p_s = sb("p_s", [P, 12, T])

        bank = [ps(f"bank{i}") for i in range(8)]

        def halves(b):
            return b[:, :].bitcast(F16).rearrange("p (h n) -> p h n", h=2)

        pair_view = bank[7][:].rearrange("p (i c) -> p c i", c=2)

        names = """adj_loaded w_loaded rows_loaded more_loaded x0_loaded x_loaded consts waits_passed
            pool_chain dve_chain adj_turned adj_copied w_hi score_weights biases gin_copy parts_summed parts_high
            parts_ready row_counts row_starts pick_ready picked edge_values spread spread_added edge_max edge_exp att_rows
            att_turned att_copied diag_ready degrees degree_roots d_diag d_spread
            lap_rows lap_turned lap_copied lap_squared cheb_copied
            s_turned s_hi s_lo s_rows s_src s_proj s_h1 s_max s_step s_negmax s_relu s_lrelu s_exp
            g_turned g_weighed g_recip g_recip2 g_heads g_v1 g_v2 g_gain g_shift g_hg g_hghi g_hglo
            g_sum g_hi g_lo g_z g_zturned g_zr g_zhi g_zlo g_out g_t x1_done
            m_hi m_lo m_off m_off_hi m_off_lo m_own m_own_hi m_own_lo m_mix x2_done
            n_hi n_lo n_lap n_lap_hi n_lap_lo n_cheb n_cheb_hi n_cheb_lo n_turned n_hT n_mix n_relu x3_done
            p_hi p_lo p_turned p_hT p_vec p_tenth p_lv p_vcol p_wtenth p_lw p_g p_max p_step p_negmax
            p_late p_exp p_recip p_gs p_g2 p_g2hi p_g2lo p_out x4_done out_stored""".split()
        for k in stages:
            names += [f"{k}_stats", f"{k}_mv", f"{k}_var", f"{k}_rstd", f"{k}_y"]
        S = {n: ctx.enter_context(nc.semaphore(n)) for n in names}

        GIN, ATT, LAP, CHEB = range(1, 5)
        W_LOADS = 7
        LOADS, ON_ACT = 16, 8
        block = ctx.enter_context(nc.Block())

        def flat(ap):
            return ap.rearrange("p t d -> p (t d)")

        def row4(r):
            return rows[:, r:r + 1, :].broadcast_to([P, T, P])

        def node_view(dram):
            return dram.rearrange("(t p) d -> p t d", p=P)

        def since(eng, sem, q, per, k):
            if isinstance(q, int) and per * q + k <= 0:
                return
            eng.wait_ge(sem, per * q + k)

        def since_apart(eng, sem, q, per, k):
            since(eng, sem, q, per, k)
            if not isinstance(q, int):
                eng.sem_inc(S["waits_passed"], 1)

        def normed(eng, stage, what, q, k=1):
            since(eng, S[f"{stage}_{what}"], q, 1, k)

        AHEAD = {n: k for k, names_ in (
            (5, "x_stats x_apply x_turn x_low score_rows score_src project scores negmax exp"),
            (4, "weigh weigh2 heads heads_stats heads_apply"),
            (3, "gat_out gat_low gin gin_low mlp_in mlp_stats mlp_apply mlp_turn mlp_low mlp_out"),
            (2, "l2_stats l2_apply l2_high l2_low off off_low own own_low l2_out"),
            (1, "l3_stats l3_apply l3_high l3_low lap lap_low cheb cheb_low l3_turn l3_out l3_add"),
            (0, "l4_stats l4_apply l4_high l4_low l4_turn pair_rows pair_lrelu pair_feats pair_cols pair_mask pair_max "
                "pair_exp pair_sums pair_scale late_high late_low l4_out")) for n in names_.split()}
        ORDER = {
            "pool": """
                l2_stats x_stats l4_stats gat_out l3_stats gat_low heads_stats scores mlp_stats late_high late_low
                mlp_low l3_add""".split(),
            "act": """
                l2_high l4_high gat_out x_turn l4_turn l3_high own off pair_rows scores gin pair_cols project
                pair_exp lap late_high cheb mlp_turn l3_turn exp l3_out""".split(),
            "dve": """
                x_stats weigh l2_stats weigh2 l4_stats l2_apply x_apply l2_low l4_apply l3_stats heads_stats x_low
                l4_low l3_apply score_src scores l3_low off_low pair_lrelu own_low pair_mask gin_low pair_max l2_out
                mlp_stats pair_sums pair_scale mlp_apply lap_low negmax cheb_low heads_apply l4_out mlp_out""".split(),
            "pe": """
                weigh weigh2 heads x_turn off score_rows l4_turn own project pair_rows gin pair_cols l2_out
                pair_feats mlp_in lap cheb l3_turn mlp_turn l4_out mlp_out l3_out""".split(),
        }
        LAST = max(AHEAD.values())
        GAP = AHEAD["x_turn"] - AHEAD["gin"]
        GAP3 = AHEAD["off"] - AHEAD["lap"]
        FILL = {
            "pool": """
                x_stats.0 scores.0 gin_low x_stats.1 heads_stats.0 scores.1 x_stats.2 gat_out.0 gat_low.0 att_low
                scores.2 mlp_stats.0 x_stats.3 mlp_low.0 heads_stats.1 gat_out.1 lap_low gat_low.1 l2_stats.0
                scores.3 heads_stats.2 mlp_stats.1 x_stats.4 mlp_low.1 gat_out.2 l2_stats.1 gat_low.2 l3_stats.0
                cheb_low scores.4 heads_stats.3 mlp_stats.2 mlp_low.2 l3_add.0""".split(),
            "act": """
                turn x_turn.0 weights gin scores.0 gin_high exp.0 project.0 x_turn.1 edge_exp scores.1 att_turn
                project.1 exp.1 x_turn.2 att_high gat_out.0 degree_roots scores.2 gin.0 project.2 lap_turn lap_high
                mlp_turn.0 cheb_turn exp.2 x_turn.3 gat_out.1 scores.3 l2_high.0 cheb_high gin.1 project.3 exp.3
                own.0 off.0 mlp_turn.1 gat_out.2 l2_high.1 x_turn.4 own.1 scores.4 off.1 l3_high.0 gin.2 project.4
                lap.0 mlp_turn.2 cheb.0 l3_turn.0 exp.4 l3_out.0""".split(),
            "dve": """
                x_stats.0 mask turn x_apply.0 score_weights x_low.0 weights biases scores.0 score_src.0 gin negmax.0
                late count weigh.0 pick x_stats.1 edge_values weigh2.0 x_apply.1 edges x_low.1 heads_stats.0
                score_src.1 scores.1 negmax.1 att x_stats.2 heads_apply.0 x_apply.2 att_parts weigh.1 x_low.2
                weigh2.1 degrees scores.2 score_src.2 lap gin_low.0 mlp_stats.0 heads_stats.1 mlp_apply.0 negmax.2
                x_stats.3 heads_apply.1 x_apply.3 mlp_out.0 weigh.2 x_low.3 weigh2.2 l2_stats.0 score_src.3 scores.3
                negmax.3 cheb_parts l2_apply.0 heads_stats.2 x_stats.4 l2_low.0 gin_low.1 heads_apply.2 mlp_stats.1
                weigh.3 mlp_apply.1 own_low.0 off_low.0 weigh2.3 x_apply.4 l2_out.0 mlp_out.1 l2_stats.1 l3_stats.0
                l2_apply.1 l2_low.1 x_low.4 heads_stats.3 score_src.4 scores.4 l3_apply.0 off_low.1 own_low.1
                l3_low.0 gin_low.2 l2_out.1 mlp_stats.2 mlp_apply.2 negmax.4 lap_low.0 heads_apply.3 cheb_low.0
                mlp_out.2""".split(),
            "pe": """
                turn x_turn.0 score_rows.0 weigh.0 row_starts weigh2.0 project.0 picked spread x_turn.1 heads.0
                score_rows.1 project.1 att_turn weigh.1 x_turn.2 weigh2.1 score_rows.2 heads.1 d_spread gin.0
                project.2 mlp_in.0 lap_turn mlp_turn.0 lap_square mlp_out.0 weigh.2 x_turn.3 weigh2.2 score_rows.3
                heads.2 gin.1 project.3 own.0 mlp_in.1 weigh.3 off.0 mlp_turn.1 weigh2.3 l2_out.0 mlp_out.1 heads.3
                x_turn.4 own.1 score_rows.4 off.1 project.4 gin.2 l2_out.1 mlp_in.2 lap.0 mlp_turn.2 cheb.0
                l3_turn.0 mlp_out.2 l3_out.0""".split(),
        }
        DRAIN = {
            "pool": """
                gat_out.14 l4_stats.11 l3_stats.12 gat_low.14 l2_stats.13 heads_stats.15 mlp_stats.14 late_high.11
                mlp_low.14 late_low.11 gat_out.15 l2_stats.14 gat_low.15 l3_add.12 l3_stats.13 l4_stats.12
                mlp_stats.15 mlp_low.15 late_high.12 late_low.12 l2_stats.15 l3_add.13 l3_stats.14 l4_stats.13
                late_high.13 late_low.13 l3_add.14 l3_stats.15 l4_stats.14 late_high.14 late_low.14 l3_add.15
                l4_stats.15 late_high.15 late_low.15""".split(),
            "act": """
                gat_out.14 l4_high.11 l4_turn.11 l3_high.12 l2_high.13 gin.14 pair_rows.11 own.13 off.13
                pair_cols.11 pair_exp.11 mlp_turn.14 cheb.12 late_high.11 lap.12 l3_turn.12 gat_out.15 l3_out.12
                l2_high.14 own.14 gin.15 l3_high.13 l4_high.12 off.14 l4_turn.12 pair_rows.12 lap.13 pair_cols.12
                mlp_turn.15 pair_exp.12 cheb.13 l3_turn.13 late_high.12 l3_out.13 l2_high.15 l3_high.14 off.15
                l4_high.13 own.15 l4_turn.13 pair_rows.13 pair_cols.13 lap.14 pair_exp.13 cheb.14 l3_turn.14
                late_high.13 l3_out.14 l3_high.15 l4_high.14 lap.15 l4_turn.14 pair_rows.14 pair_cols.14 l3_turn.15
                pair_exp.14 cheb.15 late_high.14 l3_out.15 l4_high.15 l4_turn.15 pair_rows.15 pair_cols.15
                pair_exp.15 late_high.15""".split(),
            "dve": """
                l3_stats.12 weigh.15 weigh2.15 l4_stats.11 l2_stats.13 l4_apply.11 l4_low.11 l3_apply.12 l2_apply.13
                heads_stats.15 l2_low.13 gin_low.14 l3_low.12 pair_lrelu.11 own_low.13 pair_mask.11 off_low.13
                mlp_stats.14 pair_max.11 l2_out.13 mlp_apply.14 pair_sums.11 pair_scale.11 heads_apply.15 lap_low.12
                mlp_out.14 cheb_low.12 l2_stats.14 l3_stats.13 l4_out.11 l2_apply.14 l2_low.14 l4_stats.12
                l3_apply.13 own_low.14 l4_apply.12 gin_low.15 l4_low.12 off_low.14 mlp_stats.15 l3_low.13 l2_out.14
                mlp_apply.15 pair_lrelu.12 pair_mask.12 pair_max.12 lap_low.13 pair_sums.12 pair_scale.12
                cheb_low.13 mlp_out.15 l2_stats.15 l3_stats.14 l2_apply.15 l4_out.12 l2_low.15 l4_stats.13
                l3_apply.14 l4_apply.13 off_low.15 l4_low.13 own_low.15 l3_low.14 l2_out.15 pair_lrelu.13
                pair_mask.13 pair_max.13 lap_low.14 pair_sums.13 cheb_low.14 pair_scale.13 l3_stats.15 l3_apply.15
                l4_out.13 l4_stats.14 l3_low.15 l4_apply.14 l4_low.14 lap_low.15 pair_lrelu.14 pair_mask.14
                pair_max.14 pair_sums.14 pair_scale.14 cheb_low.15 l4_out.14 l4_stats.15 l4_apply.15 l4_low.15
                pair_lrelu.15 pair_mask.15 pair_max.15 pair_sums.15 pair_scale.15 l4_out.15""".split(),
            "pe": """
                weigh.15 weigh2.15 heads.15 l4_turn.11 gin.14 pair_rows.11 own.13 off.13 pair_cols.11 mlp_in.14
                pair_feats.11 l2_out.13 cheb.12 mlp_turn.14 lap.12 mlp_out.14 l3_turn.12 l4_out.11 l3_out.12 gin.15
                own.14 off.14 mlp_in.15 l4_turn.12 l2_out.14 pair_rows.12 lap.13 pair_cols.12 mlp_turn.15 cheb.13
                l3_turn.13 pair_feats.12 mlp_out.15 l3_out.13 l4_out.12 off.15 own.15 l4_turn.13 l2_out.15
                pair_rows.13 lap.14 pair_cols.13 cheb.14 l3_turn.14 pair_feats.13 l3_out.14 l4_out.13 lap.15
                l4_turn.14 l3_turn.15 pair_rows.14 pair_cols.14 pair_feats.14 cheb.15 l3_out.15 l4_out.14 l4_turn.15
                pair_rows.15 pair_feats.15 pair_cols.15 l4_out.15""".split(),
        }

        def run(eng, key, step, prepare):
            def straight(items):
                for item in items:
                    name, _, q = item.partition(".")
                    if q:
                        step(name, int(q))
                    else:
                        prepare(name)

            straight(FILL[key])
            with eng.Fori(0, B - LAST) as i:
                for name in ORDER[key]:
                    step(name, i + AHEAD[name])
            straight(DRAIN[key])

        def load_vectors(eng, lo, hi, sem):
            att_flat = L3_att.rearrange("k o -> (k o)")
            vecs = [bp, b1, b2, L1_bias, L2_bias.rearrange("a b d -> (a b d)"), a_src, a_dst, gat_g, gat_b,
                    att_flat[0:P], att_flat[P:2 * P]]
            loads = [(rows[:, k, :], v.rearrange("(o d) -> o d", o=1).broadcast_to([P, P]))
                     for k, v in enumerate(vecs)]
            loads += [(e_col[:], L1_e.rearrange("o k -> k o")),
                      (mlp_col[:, 0:1], mlp_g.rearrange("(d o) -> d o", o=1)),
                      (mlp_col[:, 1:2], mlp_b.rearrange("(d o) -> d o", o=1)),
                      (e_last[:], L1_e[0:1, P - 1:P].broadcast_to([P, 1])),
                      (eps1[:], eps.rearrange("(o d) -> o d", o=1).broadcast_to([P, 1]))]
            assert len(loads) == LOADS
            for to, what in loads[lo:hi]:
                eng.dma_start(to, what).then_inc(S[sem], 16)

        @block.sync
        def _(sp):
            sp.dma_start(adj_n[:], adj.rearrange("(t p) n -> p t n", p=P)).then_inc(S["adj_loaded"], 16)
            sp.dma_start(x_all[:, 0], node_view(x[0])).then_inc(S["x0_loaded"], 16)
            at = 0
            for w in (Wp, W1, W2, L1_W, L2_weight.rearrange("k o a b -> (k o) a b"), L3_others, L3_self):
                n = w.shape[0] if len(w.shape) == 3 else 1
                sp.dma_start(w_raw[:, at:at + n, :], w.rearrange("k a b -> a k b") if n > 1 else w).then_inc(
                    S["w_loaded"], 16)
                at += n
            sp.wait_ge(S["more_loaded"], 16 * (LOADS - ON_ACT))
            sp.dma_start(x_all[:, 1:B].rearrange("p b t d -> p (b t) d"),
                         x[1:B].rearrange("b (t p) d -> p (b t) d", p=P)).then_inc(S["x_loaded"], 16)
            out_v = out.rearrange("b (t p) d -> b p t d", p=P)
            with sp.Fori(0, B) as q:
                sp.wait_ge(S["x4_done"], q + 1)
                sp.dma_start(out_v[q], x_all[:, q]).then_inc(S["out_stored"], 16)
            sp.wait_ge(S["out_stored"], 16 * B)

        @block.gpsimd
        def _(pool):
            n = 0

            def link(ins):
                nonlocal n
                n += 1
                ins.then_inc(S["pool_chain"], 1)
                pool.wait_ge(S["pool_chain"], n)

            link(pool.memset(ones[:], 1.0))
            pool.memset(mhalf[:], -0.5)
            pool.memset(ones16[:], 1.0)
            link(pool.affine_select(out=ident[:], in_=ones[:], pattern=[[-1, P]], compare_op=ALU.is_equal,
                                    fill=0.0, base=0, channel_multiplier=1))
            pool.affine_select(out=tri[:], in_=ones[:], pattern=[[1, P]], compare_op=ALU.is_gt,
                               fill=0.0, base=0, channel_multiplier=-1)
            pool.iota(kcol[:], pattern=[[0, 1]], base=0, channel_multiplier=1,
                      allow_small_or_imprecise_dtypes=True)
            pool.iota(krow[:], pattern=[[1, P]], base=0, channel_multiplier=0,
                      allow_small_or_imprecise_dtypes=True)
            pool.tensor_copy(ident16[:], ident[:]).then_inc(S["consts"], 1)
            load_vectors(pool, ON_ACT, LOADS, "more_loaded")

            def prepare(name):
                if name == "gin_low":
                    pool.wait_ge(S["parts_high"], GIN)
                    pool.tensor_tensor(gin_t[:, 1], wk3, gin_t[:, 0], ALU.subtract).then_inc(S["parts_ready"], 1)
                elif name == "att_low":
                    pool.wait_ge(S["parts_high"], ATT)
                    pool.tensor_tensor(att_t[:, 1], wk1, att_t[:, 0], ALU.subtract).then_inc(S["parts_ready"], 1)
                elif name == "lap_low":
                    pool.wait_ge(S["parts_high"], LAP)
                    pool.tensor_tensor(lap_t[:, 1], wk2, lap_t[:, 0], ALU.subtract).then_inc(S["parts_ready"], 1)
                elif name == "cheb_low":
                    pool.wait_ge(S["parts_high"], CHEB)
                    pool.tensor_tensor(cheb_t[:, 1], wk3, cheb_t[:, 0], ALU.subtract).then_inc(S["parts_ready"], 1)

            def root(q, stage, eps_=LN_EPS):
                normed(pool, stage, "mv", q)
                if not isinstance(q, int):
                    pool.sem_inc(S["waits_passed"], 1)
                pool.tensor_scalar(rstd[stage][:, 0], mv[stage][:, :, 1], eps_, None, ALU.add).then_inc(
                    S[f"{stage}_var"], 1)
                normed(pool, stage, "var", q)
                pool.tensor_tensor(rstd[stage][:, 1], rstd[stage][:, 0], mhalf[:], ALU.pow).then_inc(
                    S[f"{stage}_rstd"], 1)

            def step(name, q):
                if name == "x_stats":
                    root(q, "s")
                elif name == "scores":
                    for t in range(T):
                        since(pool, S["s_relu"], q, T, t + 1)
                        pool.tensor_tensor(s_e[:, t], s_e[:, t], s_t[:, t], ALU.add).then_inc(S["s_lrelu"], 1)
                elif name == "heads_stats":
                    since(pool, S["g_recip"], q, 1, 1)
                    pool.tensor_tensor(g_s[:, 1], g_s[:, 0], g_s[:, 0], ALU.mult).then_inc(S["g_recip2"], 1)
                    since(pool, S["g_recip2"], q, 1, 1)
                    normed(pool, "g", "mv", q)
                    pool.tensor_tensor(rstd["g"][:, 2], mv["g"][:, :, 1], g_s[:, 1], ALU.mult).then_inc(S["g_v1"], 1)
                    since_apart(pool, S["g_v1"], q, 1, 1)
                    pool.tensor_scalar(rstd["g"][:, 0], rstd["g"][:, 2], LN_EPS, None, ALU.add).then_inc(
                        S["g_var"], 1)
                    normed(pool, "g", "var", q)
                    pool.tensor_tensor(rstd["g"][:, 3], rstd["g"][:, 0], mhalf[:], ALU.pow).then_inc(S["g_v2"], 1)
                    since(pool, S["g_v2"], q, 1, 1)
                    pool.tensor_tensor(rstd["g"][:, 1], rstd["g"][:, 3], g_s[:, 0], ALU.mult).then_inc(
                        S["g_rstd"], 1)
                elif name == "gat_out":
                    normed(pool, "g", "y", q)
                    pool.tensor_tensor(g_y2[:], y["g"][:], row4(R_GG), ALU.mult).then_inc(S["g_gain"], 1)
                    since(pool, S["g_gain"], q, 1, 1)
                    pool.tensor_tensor(g_y2[:], g_y2[:], row4(R_GB), ALU.add).then_inc(S["g_shift"], 1)
                elif name == "gat_low":
                    since(pool, S["g_hghi"], q, 1, 1)
                    pool.tensor_tensor(g_hghl[:, 1], g_hg[:], g_hghl[:, 0], ALU.subtract).then_inc(S["g_hglo"], 1)
                elif name == "mlp_stats":
                    root(q, "f", LN_EPS * WS * WS)
                elif name == "mlp_low":
                    since(pool, S["g_zhi"], q, 1, 1)
                    pool.tensor_tensor(g_fT[:, 1], flat(g_z[:]), g_fT[:, 0], ALU.subtract).then_inc(S["g_zlo"], 1)
                elif name == "l2_stats":
                    root(q, "m")
                elif name == "l3_stats":
                    root(q, "n")
                elif name == "l3_add":
                    since_apart(pool, S["n_relu"], q, 1, 1)
                    pool.tensor_tensor(x_all[:, q], m_t, x_all[:, q], ALU.add).then_inc(S["x3_done"], 1)
                elif name == "l4_stats":
                    root(q, "p")
                elif name == "late_high":
                    since(pool, S["p_gs"], q, 1, 1)
                    pool.tensor_tensor(p_g2, p_g, p_s[:, 5].unsqueeze(2).broadcast_to([P, T, P]),
                                       ALU.mult).then_inc(S["p_g2"], 1)
                elif name == "late_low":
                    since(pool, S["p_g2hi"], q, 1, 1)
                    pool.tensor_tensor(p_g2hl[:, 1], p_g2, p_g2hl[:, 0], ALU.subtract).then_inc(S["p_g2lo"], 1)

            run(pool, "pool", step, prepare)

        @block.scalar
        def _(act):
            load_vectors(act, 0, ON_ACT, "rows_loaded")

            def prepare(name):
                if name == "turn":
                    for t in range(TH):
                        act.wait_ge(S["adj_turned"], t + 1)
                        ins = act.activation(adj_t[:, t], bank[t][:], ACT.Copy)
                    ins.then_inc(S["adj_copied"], 1)
                elif name == "weights":
                    act.wait_ge(S["w_loaded"], 16 * W_LOADS)
                    act.activation(w_hl[:, 0], w_raw[:], ACT.Copy, scale=WS).then_inc(S["w_hi"], 1)
                elif name == "gin":
                    act.wait_ge(S["adj_copied"], 2)
                    act.activation(wk3, adj_t[:], ACT.Copy).then_inc(S["gin_copy"], 1)
                elif name == "gin_high":
                    act.wait_ge(S["parts_summed"], 1)
                    act.activation(gin_t[:, 0], wk3, ACT.Copy).then_inc(S["parts_high"], 1)
                elif name == "edge_exp":
                    act.wait_ge(S["edge_max"], 1)
                    for t in range(T):
                        ins = act.activation(wk1[:, t], wk2[:, t], ACT.Exp, bias=small[:, 6, t:t + 1],
                                             accum_out=small[:, 7, t:t + 1])
                    ins.then_inc(S["edge_exp"], 1)
                elif name == "att_turn":
                    for t in range(T):
                        act.wait_ge(S["att_turned"], t + 1)
                        act.activation(wk1[:, t], bank[6 + t % 2][:], ACT.Copy).then_inc(S["att_copied"], 1)
                elif name == "att_high":
                    act.wait_ge(S["parts_summed"], 2)
                    act.activation(att_t[:, 0], wk1, ACT.Copy).then_inc(S["parts_high"], 1)
                elif name == "degree_roots":
                    act.wait_ge(S["degrees"], 1)
                    act.activation(small[:, 1], small[:, 0], ACT.Sqrt).then_inc(S["degree_roots"], 1)
                elif name == "lap_turn":
                    for t in range(T):
                        act.wait_ge(S["lap_turned"], t + 1)
                        act.activation(wk2[:, t], bank[6 + t % 2][:], ACT.Copy).then_inc(S["lap_copied"], 1)
                elif name == "lap_high":
                    act.wait_ge(S["lap_copied"], T)
                    act.activation(lap_t[:, 0], wk2, ACT.Copy).then_inc(S["parts_high"], 1)
                elif name == "cheb_turn":
                    for t in range(T):
                        act.wait_ge(S["lap_squared"], t + 1)
                        act.activation(wk3[:, t], bank[6 + t % 2][:], ACT.Copy, scale=2.0).then_inc(
                            S["cheb_copied"], 1)
                elif name == "cheb_high":
                    act.wait_ge(S["parts_summed"], 3)
                    act.activation(cheb_t[:, 0], wk3, ACT.Copy).then_inc(S["parts_high"], 1)

            def step(name, q):
                if name == "x_turn":
                    since(act, S["s_turned"], q, 1, 1)
                    act.activation(s_fT[:, 0], bank[0][:], ACT.Relu).then_inc(S["s_hi"], 1)
                elif name == "project":
                    since(act, S["s_proj"], q, 1, 1)
                    since(act, S["g_heads"], q, 1, 0)
                    act.activation(flat(s_h1[:]), bank[0][:], ACT.Copy, scale=1.0 / WS).then_inc(S["s_h1"], 1)
                elif name == "scores":
                    since(act, S["g_turned"], q, T, 0)
                    since(act, S["g_recip"], q, 1, 0)
                    since(act, S["s_src"], q, 1, 1)
                    for t in range(T):
                        since(act, S["s_max"], q, T, t + 1)
                        act.activation(s_e[:, t], s_t[:, t], ACT.Relu, bias=s_s[:, 0, t:t + 1],
                                       scale=4.0).then_inc(S["s_relu"], 1)
                elif name == "exp":
                    since(act, S["s_negmax"], q, 1, 1)
                    for t in range(T):
                        since(act, S["s_lrelu"], q, T, t + 1)
                        act.activation(s_e[:, t], s_e[:, t], ACT.Exp, bias=s_s[:, 4, t:t + 1],
                                       accum_out=s_s[:, 5, t:t + 1]).then_inc(S["s_exp"], 1)
                elif name == "gat_out":
                    since(act, S["g_shift"], q, 1, 1)
                    since(act, S["g_t"], q, 1, 0)
                    since(act, S["g_sum"], q, 1, 0)
                    act.activation(g_hg[:], g_y2[:], ACT.Relu).then_inc(S["g_hg"], 1)
                    act.activation(g_hghl[:, 0], g_y2[:], ACT.Relu).then_inc(S["g_hghi"], 1)
                elif name == "gin":
                    since(act, S["g_sum"], q, 1, 1)
                    act.activation(g_fT[:, 0], bank[1][:], ACT.Copy).then_inc(S["g_hi"], 1)
                elif name == "mlp_turn":
                    since(act, S["g_zturned"], q, 1, 1)
                    act.activation(flat(g_z[:]), bank[1][:], ACT.Relu, bias=mlp_col[:, 1:2],
                                   scale=mlp_col[:, 0:1]).then_inc(S["g_zr"], 1)
                    since(act, S["g_zr"], q, 1, 1)
                    act.activation(g_fT[:, 0], flat(g_z[:]), ACT.Copy).then_inc(S["g_zhi"], 1)
                elif name == "l2_high":
                    normed(act, "m", "y", q)
                    since(act, S["m_off"], q, 1, 0)
                    since(act, S["m_own"], q, 1, 0)
                    act.activation(m_h[:, 0], y["m"][:], ACT.Relu).then_inc(S["m_hi"], 1)
                elif name == "off":
                    since(act, S["m_off"], q, 1, 1)
                    since(act, S["m_mix"], q, 1, 0)
                    act.activation(m_1[:, 0], bank[4][:], ACT.Copy).then_inc(S["m_off_hi"], 1)
                elif name == "own":
                    since(act, S["m_own"], q, 1, 1)
                    since(act, S["m_mix"], q, 1, 0)
                    act.activation(m_2[:, 0], bank[5][:], ACT.Copy).then_inc(S["m_own_hi"], 1)
                elif name == "l3_high":
                    normed(act, "n", "y", q)
                    since(act, S["n_turned"], q, 1, 0)
                    act.activation(n_h[:, 0], y["n"], ACT.Relu).then_inc(S["n_hi"], 1)
                elif name == "lap":
                    since(act, S["n_lap"], q, 1, 1)
                    since(act, S["n_mix"], q, 1, 0)
                    act.activation(n_1[:, 0], bank[4][:], ACT.Copy).then_inc(S["n_lap_hi"], 1)
                elif name == "cheb":
                    since(act, S["n_cheb"], q, 1, 1)
                    since(act, S["n_mix"], q, 1, 0)
                    act.activation(n_2[:, 0], bank[5][:], ACT.Copy).then_inc(S["n_cheb_hi"], 1)
                elif name == "l3_turn":
                    since(act, S["n_turned"], q, 1, 1)
                    act.activation(n_hT[:], halves(bank[4]), ACT.Copy).then_inc(S["n_hT"], 1)
                elif name == "l3_out":
                    since(act, S["n_mix"], q, 1, 1)
                    since(act, S["x3_done"], q, 1, 0)
                    act.activation(flat(m_t), bank[5][:], ACT.Relu, scale=1.0 / WS).then_inc(S["n_relu"], 1)
                elif name == "l4_high":
                    normed(act, "p", "y", q)
                    act.activation(p_h[:, 0], y["p"][:], ACT.Relu).then_inc(S["p_hi"], 1)
                elif name == "l4_turn":
                    since(act, S["p_turned"], q, 1, 1)
                    act.activation(p_hT, halves(bank[6]), ACT.Copy).then_inc(S["p_hT"], 1)
                elif name == "pair_rows":
                    since(act, S["p_vec"], q, 1, 1)
                    act.activation(p_lv, pair_view, ACT.Copy, scale=0.1).then_inc(S["p_tenth"], 1)
                elif name == "pair_cols":
                    since(act, S["p_vcol"], q, 1, 1)
                    act.activation(p_lw[:], bank[7][:, 0:2], ACT.Copy, scale=0.1).then_inc(S["p_wtenth"], 1)
                elif name == "pair_exp":
                    since(act, S["p_negmax"], q, 1, 1)
                    act.activation(p_s[:, 5], p_s[:, 4], ACT.Exp).then_inc(S["p_late"], 1)
                    for t in range(T):
                        ins = act.activation(p_e[:, t], p_te[:, t], ACT.Exp, bias=p_s[:, 3, t:t + 1],
                                             accum_out=p_s[:, 7, t:t + 1])
                    ins.then_inc(S["p_exp"], 1)
                elif name == "late_high":
                    since(act, S["p_g2"], q, 1, 1)
                    act.activation(p_g2hl[:, 0], p_g2, ACT.Copy).then_inc(S["p_g2hi"], 1)

            run(act, "act", step, prepare)

        @block.vector
        def _(dve):
            n = 0

            def link(ins, named=None):
                nonlocal n
                if named:
                    ins.then_inc(S[named], 1)
                    dve.wait_ge(S[named], 1)
                else:
                    n += 1
                    ins.then_inc(S["dve_chain"], 1)
                    dve.wait_ge(S["dve_chain"], n)

            def split(o, src, named=None):
                link(dve.tensor_copy(o[:, 0], src))
                link(dve.tensor_tensor(o[:, 1], src, o[:, 0], ALU.subtract), named)

            def diag_block(m, t):
                return m[:, t, t * P:(t + 1) * P]

            scratch_a, scratch_b = wk2[:, 0, 0:P], wk2[:, 1, 0:P]

            def prepare(name):
                if name == "mask":
                    dve.wait_ge(S["adj_loaded"], 16)
                    link(dve.tensor_scalar(gat_mask[:], adj_n[:], 0.0, FLOAT_MIN, ALU.is_le, ALU.mult))
                elif name == "turn":
                    for t in range(TH, T):
                        dve.wait_ge(S["adj_turned"], t + 1)
                        ins = dve.tensor_copy(adj_t[:, t], bank[t][:])
                    ins.then_inc(S["adj_copied"], 1)
                    dve.wait_ge(S["adj_copied"], 2)
                elif name == "weights":
                    dve.wait_ge(S["w_hi"], 1)
                    link(dve.scalar_tensor_tensor(out=w_hl[:, 1].rearrange("p a b -> p (a b)"),
                                                  in0=w_raw[:].rearrange("p a b -> p (a b)"), scalar=WS,
                                                  in1=w_hl[:, 0].rearrange("p a b -> p (a b)"),
                                                  op0=ALU.mult, op1=ALU.subtract))
                elif name == "score_weights":
                    dve.wait_ge(S["w_loaded"], 16 * W_LOADS)
                    dve.wait_ge(S["rows_loaded"], 16 * ON_ACT)
                    dve.wait_ge(S["more_loaded"], 16 * (LOADS - ON_ACT))
                    dve.wait_ge(S["consts"], 1)
                    for k, (w, r) in enumerate(((WP, R_ASRC), (WP, R_ADST), (L3O, R_A1), (L3O, R_A2))):
                        link(dve.tensor_tensor_reduce(out=scratch_a, in0=w_raw[:, w], in1=rows[:, r], scale=1.0,
                                                      scalar=0.0, op0=ALU.mult, op1=ALU.add,
                                                      accum_out=score_w[:, k:k + 1]))
                    link(dve.tensor_tensor(score_w[:, 4:5], score_w[:, 2:3], score_w[:, 3:4], ALU.add))
                    link(dve.tensor_tensor(scratch_b, rows[:, R_ASRC], rows[:, R_ADST], ALU.add))
                    link(dve.tensor_tensor_reduce(out=scratch_a, in0=scratch_b, in1=rows[:, R_BP], scale=1.0,
                                                  scalar=0.0, op0=ALU.mult, op1=ALU.add, accum_out=score_w[:, 5:6]))
                    link(dve.tensor_copy(col_hl[:, 0], score_w[:, 0:4]))
                    link(dve.tensor_tensor(col_hl[:, 1], score_w[:, 0:4], col_hl[:, 0], ALU.subtract))
                    for o, k in ((dst_hl, 1), (pair_hl, 4)):
                        link(dve.tensor_scalar(scratch_a, ones[:], score_w[:, k:k + 1], None, ALU.mult))
                        link(dve.tensor_copy(o[:, 0], scratch_a))
                        link(dve.tensor_tensor(o[:, 1], scratch_a, o[:, 0], ALU.subtract))
                    link(dve.memset(small[:, 14], 0.0), "score_weights")

                elif name == "biases":
                    b_lo = wk2[:, 0:2].rearrange("p t n -> p (t n)")[:, 0:BIASES * P].rearrange(
                        "p (k d) -> p k d", d=P)
                    link(dve.tensor_scalar(bias_hl[:], rows[:, 0:BIASES], WS, None, ALU.mult))
                    link(dve.scalar_tensor_tensor(out=b_lo, in0=rows[:, 0:BIASES], scalar=WS, in1=bias_hl[:],
                                                  op0=ALU.mult, op1=ALU.subtract))
                    link(dve.tensor_scalar(b_lo, b_lo, ident[:, 1:2], None, ALU.mult))
                    link(dve.scalar_tensor_tensor(out=bias_hl[:], in0=bias_hl[:], scalar=ident[:, 0:1], in1=b_lo,
                                                  op0=ALU.mult, op1=ALU.add), "biases")
                elif name == "gin":
                    link(dve.tensor_scalar(eps1[:], eps1[:], 1.0, None, ALU.add))
                    dve.wait_ge(S["gin_copy"], 1)
                    for t in range(T):
                        dg = diag_block(wk3, t)
                        ins = dve.scalar_tensor_tensor(out=dg, in0=ident[:], scalar=eps1[:], in1=dg,
                                                       op0=ALU.mult, op1=ALU.add)
                    ins.then_inc(S["parts_summed"], 1)
                elif name == "late":
                    link(dve.tensor_scalar(pair_mask[:], adj_t[:, :, 0:H], 0.0, NEG_BIG, ALU.is_le, ALU.mult))
                    link(dve.tensor_scalar(wk1, adj_t[:], 0.0, None, ALU.is_gt))
                    link(dve.tensor_reduce(small[:, 8], wk1, AX_X, ALU.add))
                    link(dve.tensor_reduce(small[:, 9], wk1[:, :, H:N], AX_X, ALU.add))
                    link(dve.tensor_scalar(small[:, 10], small[:, 8], 0.0, None, ALU.is_equal))
                    link(dve.tensor_scalar(late_neg[:], small[:, 9], 0.0, NEG_BIG, ALU.is_equal, ALU.mult))
                    link(dve.scalar_tensor_tensor(out=late_cnt[:], in0=small[:, 10], scalar=float(H),
                                                  in1=small[:, 9], op0=ALU.mult, op1=ALU.add))
                    link(dve.tensor_tensor(late_mask[:], wk1[:, :, H:N],
                                           small[:, 10].unsqueeze(2).broadcast_to([P, T, H]), ALU.add))
                elif name == "count":
                    link(dve.tensor_scalar(wk1, adj_n[:], 0.0, None, ALU.is_gt))
                    for t in range(T):
                        ins = dve.tensor_tensor_scan(wk2[:, t], wk1[:, t], wk1[:, t], 0.0, ALU.add, ALU.max)
                    link(ins)
                    link(dve.tensor_copy(small[:, 2], wk2[:, :, N - 1]), "row_counts")
                elif name == "pick":
                    dve.wait_ge(S["row_starts"], 1)
                    dve.wait_ge(S["parts_ready"], GIN)
                    link(dve.tensor_copy(small[:, 3], bank[6][:, 0:T]))
                    link(dve.tensor_tensor(small[:, 4], small[:, 3], small[:, 2], ALU.add))
                    for t in range(T):
                        ins = dve.tensor_scalar(wk3[:, t, 0:P], krow[:], small[:, 3, t:t + 1], None, ALU.is_ge)
                    link(ins)
                    for t in range(T):
                        dve.scalar_tensor_tensor(out=pick_t[:, t], in0=krow[:], scalar=small[:, 4, t:t + 1],
                                                 in1=wk3[:, t, 0:P], op0=ALU.is_lt, op1=ALU.mult)
                        ins = dve.scalar_tensor_tensor(out=wk2[:, t], in0=wk2[:, t], scalar=small[:, 3, t:t + 1],
                                                       in1=wk1[:, t], op0=ALU.add, op1=ALU.mult)
                    link(ins)
                    link(dve.tensor_scalar(q16[:], wk2, float(N), None, ALU.min), "pick_ready")
                    for t in range(T):
                        ins = dve.tensor_scalar(wk1[:, t], wk2[:, t], float(P), e_last[:], ALU.is_gt, ALU.mult)
                    link(ins)
                    link(dve.tensor_scalar(small[:, 5, 0:1], kcol[:], 1.0, None, ALU.add))
                elif name == "edge_values":
                    dve.wait_ge(S["picked"], 1)
                    link(dve.tensor_scalar(wk3[:, 0], bank[6][:], small[:, 5, 0:1], None, ALU.is_equal))
                    link(dve.tensor_scalar(wk3[:, 1], bank[7][:], e_col[:], None, ALU.mult), "edge_values")
                elif name == "edges":
                    for t in range(T):
                        dve.wait_ge(S["spread"], t + 1)
                        dve.tensor_tensor(wk1[:, t], wk1[:, t], bank[6 + t % 2][:], ALU.add).then_inc(
                            S["spread_added"], 1)
                    dve.wait_ge(S["spread_added"], T)
                    link(dve.tensor_scalar(wk2, adj_n[:], 0.0, NEG_BIG, ALU.is_le, ALU.mult))
                    link(dve.tensor_tensor(wk2, wk2, wk1, ALU.add))
                    link(dve.tensor_reduce(small[:, 6], wk2, AX_X, ALU.max, negate=True), "edge_max")
                elif name == "att":
                    dve.wait_ge(S["edge_exp"], 1)
                    link(dve.reciprocal(small[:, 11], small[:, 7]))
                    for t in range(T):
                        ins = dve.tensor_scalar(wk2[:, t], wk1[:, t], small[:, 11, t:t + 1], None, ALU.mult)
                    link(ins, "att_rows")
                elif name == "att_parts":
                    owns = [wk3[:, 0, t * P:(t + 1) * P] for t in range(T)]
                    for t in range(T):
                        dve.wait_ge(S["att_copied"], t + 1)
                        ins = dve.tensor_tensor(owns[t], diag_block(wk1, t), ident[:], ALU.mult)
                    link(ins)
                    for t in range(T):
                        ins = dve.tensor_tensor(diag_block(wk1, t), diag_block(wk1, t), owns[t], ALU.subtract)
                    ins.then_inc(S["parts_summed"], 1)
                    split(att_d, wk3[:, 0].rearrange("p (t n) -> p t n", t=T), "diag_ready")
                elif name == "degrees":
                    dve.wait_ge(S["adj_loaded"], 16)
                    link(dve.tensor_reduce(small[:, 0], adj_n[:], AX_X, ALU.add), "degrees")
                elif name == "lap":
                    dve.wait_ge(S["degree_roots"], 1)
                    link(dve.reciprocal(small[:, 12], small[:, 1]))
                    for t in range(T):
                        ins = dve.tensor_scalar(wk3[:, 1, t * P:(t + 1) * P], ident[:], small[:, 12, t:t + 1], None,
                                                ALU.mult)
                    link(ins, "d_diag")
                    link(dve.tensor_scalar(small[:, 13], small[:, 12], -1.0, None, ALU.mult))
                    dve.wait_ge(S["parts_ready"], ATT)
                    dve.wait_ge(S["d_spread"], 1)
                    for t in range(T):
                        ins = dve.scalar_tensor_tensor(out=wk1[:, t], in0=adj_n[:, t], scalar=small[:, 13, t:t + 1],
                                                       in1=bank[6][:], op0=ALU.mult, op1=ALU.mult)
                    link(ins)
                    for t in range(T):
                        ins = dve.tensor_tensor(diag_block(wk1, t), diag_block(wk1, t), ident[:], ALU.add)
                    link(ins, "lap_rows")
                elif name == "cheb_parts":
                    for t in range(T):
                        dve.wait_ge(S["cheb_copied"], t + 1)
                        ins = dve.tensor_tensor(diag_block(wk3, t), diag_block(wk3, t), ident[:], ALU.subtract)
                    ins.then_inc(S["parts_summed"], 1)

            def measure(q, stage, src):
                for t in range(T):
                    ins = dve.bn_stats(stats[stage][:, t], src(t))
                ins.then_inc(S[f"{stage}_stats"], 1)
                since_apart(dve, S[f"{stage}_stats"], q, 1, 1)
                for t in range(T):
                    ins = dve.bn_aggr(mv[stage][:, t], stats[stage][:, t])
                ins.then_inc(S[f"{stage}_mv"], 1)

            def apply(q, stage, src):
                normed(dve, stage, "rstd", q)
                for t in range(T):
                    ins = dve.tensor_scalar(y[stage][:, t], src(t), mv[stage][:, t, 0:1],
                                            rstd[stage][:, 1, t:t + 1], ALU.subtract, ALU.mult)
                ins.then_inc(S[f"{stage}_y"], 1)

            def low(out_, src, hi, floor=None):
                op = ALU.max if floor is not None else ALU.mult
                return dve.scalar_tensor_tensor(out=out_, in0=src, scalar=0.0 if floor is not None else 1.0,
                                                in1=hi, op0=op, op1=ALU.subtract)

            def step(name, q):
                if name == "x_stats":
                    dve.wait_ge(S["x0_loaded" if isinstance(q, int) and q == 0 else "x_loaded"], 16)
                    measure(q, "s", lambda t: x_all[:, q, t])
                elif name == "x_apply":
                    apply(q, "s", lambda t: x_all[:, q, t])
                elif name == "x_low":
                    since(dve, S["s_hi"], q, 1, 1)
                    low(s_fT[:, 1], bank[0][:], s_fT[:, 0], 0.0).then_inc(S["s_lo"], 1)
                elif name == "score_src":
                    since(dve, S["s_rows"], q, 1, 1)
                    dve.tensor_scalar(s_s[:, 0], bank[0][:, 0:T], score_w[:, 5:6], 0.8, ALU.add,
                                      ALU.mult).then_inc(S["s_src"], 1)
                elif name == "scores":
                    since_apart(dve, S["s_rows"], q, 1, 1)
                    for t in range(T):
                        dve.tensor_tensor_reduce(out=s_t[:, t], in0=bank[1][:], in1=gat_mask[:, t], scale=0.2,
                                                 scalar=FLOAT_MIN, op0=ALU.add, op1=ALU.max,
                                                 accum_out=s_s[:, 1, t:t + 1]).then_inc(S["s_max"], 1)
                elif name == "negmax":
                    since(dve, S["s_src"], q, 1, 1)
                    since(dve, S["s_max"], q, T, T)
                    dve.scalar_tensor_tensor(out=s_s[:, 2], in0=s_s[:, 1], scalar=4.0, in1=s_s[:, 0],
                                             op0=ALU.mult, op1=ALU.add).then_inc(S["s_step"], 1)
                    since(dve, S["s_step"], q, 2, 1)
                    dve.scalar_tensor_tensor(out=s_s[:, 3], in0=s_s[:, 2], scalar=0.0, in1=s_s[:, 1],
                                             op0=ALU.max, op1=ALU.add).then_inc(S["s_step"], 1)
                    since(dve, S["s_step"], q, 2, 2)
                    dve.tensor_scalar(s_s[:, 4], s_s[:, 3], -1.0, None, ALU.mult).then_inc(S["s_negmax"], 1)
                elif name in ("weigh", "weigh2"):
                    for t in (range(TH) if name == "weigh" else range(TH, T)):
                        since(dve, S["g_turned"], q, T, t + 1)
                        dve.tensor_tensor(g_pt[:, :, t * P:(t + 1) * P],
                                          bank[2 + t % 2][:].rearrange("p (j m) -> p j m", j=T),
                                          adj_t[:, :, t * P:(t + 1) * P], ALU.mult).then_inc(S["g_weighed"], 1)
                    if name == "weigh":
                        since(dve, S["s_exp"], q, T, T)
                        dve.reciprocal(g_s[:, 0], s_s[:, 5]).then_inc(S["g_recip"], 1)
                elif name == "heads_stats":
                    since(dve, S["g_heads"], q, 1, 1)
                    measure(q, "g", lambda t: bank[2][:, t * P:(t + 1) * P])
                elif name == "heads_apply":
                    since(dve, S["g_gain"], q, 1, 0)
                    apply(q, "g", lambda t: bank[2][:, t * P:(t + 1) * P])
                elif name == "gin_low":
                    since(dve, S["g_hi"], q, 1, 1)
                    low(g_fT[:, 1], bank[1][:], g_fT[:, 0]).then_inc(S["g_lo"], 1)
                elif name == "mlp_stats":
                    since(dve, S["g_z"], q, 1, 1)
                    measure(q, "f", lambda t: bank[0][:, t * P:(t + 1) * P])
                elif name == "mlp_apply":
                    apply(q, "f", lambda t: bank[0][:, t * P:(t + 1) * P])
                elif name == "mlp_out":
                    since(dve, S["g_out"], q, 1, 1)
                    dve.scalar_tensor_tensor(out=flat(g_z[:]), in0=bank[0][:], scalar=1.0 / WS, in1=flat(g_hg[:]),
                                             op0=ALU.mult, op1=ALU.add).then_inc(S["g_t"], 1)
                    since(dve, S["g_t"], q, 1, 1)
                    dve.scalar_tensor_tensor(out=x_all[:, q], in0=g_z[:], scalar=0.0, in1=x_all[:, q],
                                             op0=ALU.max, op1=ALU.add).then_inc(S["x1_done"], 1)
                elif name == "l2_stats":
                    since_apart(dve, S["x1_done"], q, 1, 1)
                    measure(q, "m", lambda t: x_all[:, q, t])
                elif name == "l2_apply":
                    apply(q, "m", lambda t: x_all[:, q, t])
                elif name == "l2_low":
                    since(dve, S["m_hi"], q, 1, 1)
                    low(flat(m_h[:, 1]), flat(y["m"][:]), flat(m_h[:, 0]), 0.0).then_inc(S["m_lo"], 1)
                elif name == "l3_stats":
                    since_apart(dve, S["x2_done"], q, 1, 1)
                    measure(q, "n", lambda t: x_all[:, q, t])
                elif name == "l3_apply":
                    if isinstance(q, int) and q == 0:
                        dve.wait_ge(S["lap_rows"], 1)
                    apply(q, "n", lambda t: x_all[:, q, t])
                elif name == "l3_low":
                    since(dve, S["n_hi"], q, 1, 1)
                    low(flat(n_h[:, 1]), flat(y["n"]), flat(n_h[:, 0]), 0.0).then_inc(S["n_lo"], 1)
                elif name == "off_low":
                    since(dve, S["m_off_hi"], q, 1, 1)
                    low(m_1[:, 1], bank[4][:], m_1[:, 0]).then_inc(S["m_off_lo"], 1)
                elif name == "own_low":
                    since(dve, S["m_own_hi"], q, 1, 1)
                    low(m_2[:, 1], bank[5][:], m_2[:, 0]).then_inc(S["m_own_lo"], 1)
                elif name == "l2_out":
                    since(dve, S["m_mix"], q, 1, 1)
                    dve.scalar_tensor_tensor(out=x_all[:, q], in0=bank[4][:].rearrange("p (t d) -> p t d", t=T),
                                             scalar=1.0 / WS, in1=x_all[:, q], op0=ALU.mult,
                                             op1=ALU.add).then_inc(S["x2_done"], 1)
                elif name == "lap_low":
                    since(dve, S["n_lap_hi"], q, 1, 1)
                    low(n_1[:, 1], bank[4][:], n_1[:, 0]).then_inc(S["n_lap_lo"], 1)
                elif name == "cheb_low":
                    since(dve, S["n_cheb_hi"], q, 1, 1)
                    low(n_2[:, 1], bank[5][:], n_2[:, 0]).then_inc(S["n_cheb_lo"], 1)
                elif name == "l4_stats":
                    since_apart(dve, S["x3_done"], q, 1, 1)
                    measure(q, "p", lambda t: x_all[:, q, t])
                elif name == "l4_apply":
                    apply(q, "p", lambda t: x_all[:, q, t])
                elif name == "l4_low":
                    since(dve, S["p_hi"], q, 1, 1)
                    low(flat(p_h[:, 1]), flat(y["p"][:]), flat(p_h[:, 0]), 0.0).then_inc(S["p_lo"], 1)
                elif name == "pair_lrelu":
                    since(dve, S["p_tenth"], q, 1, 1)
                    dve.tensor_tensor(p_lv, p_lv, pair_view, ALU.max).then_inc(S["p_lv"], 1)
                elif name == "pair_mask":
                    since_apart(dve, S["p_lv"], q, 1, 1)
                    for t in range(T):
                        dve.tensor_tensor_reduce(out=p_te[:, t], in0=p_lv[:, t // TH], in1=pair_mask[:, t],
                                                 scale=1.0, scalar=FLOAT_MIN, op0=ALU.add, op1=ALU.max,
                                                 accum_out=p_s[:, 0, t:t + 1]).then_inc(S["p_max"], 1)
                elif name == "pair_max":
                    since(dve, S["p_wtenth"], q, 1, 1)
                    dve.tensor_tensor(p_lw[:], p_lw[:], bank[7][:, 0:2], ALU.max).then_inc(S["p_lw"], 1)
                    since(dve, S["p_lw"], q, 1, 1)
                    dve.tensor_tensor(p_s[:, 1].rearrange("p (r c) -> p r c", c=2),
                                      p_lw[:].unsqueeze(1).broadcast_to([P, T // 2, 2]),
                                      late_neg[:].rearrange("p (r c) -> p r c", c=2),
                                      ALU.add).then_inc(S["p_step"], 1)
                    since(dve, S["p_step"], q, 4, 1)
                    since(dve, S["p_max"], q, T, T)
                    dve.tensor_tensor(p_s[:, 2], p_s[:, 0], p_s[:, 1], ALU.max).then_inc(S["p_step"], 1)
                    since(dve, S["p_step"], q, 4, 2)
                    dve.tensor_scalar(p_s[:, 3], p_s[:, 2], -1.0, None, ALU.mult)
                    dve.tensor_tensor(p_s[:, 4], p_s[:, 1], p_s[:, 2], ALU.subtract).then_inc(S["p_negmax"], 1)
                elif name == "pair_sums":
                    since(dve, S["p_late"], q, 1, 1)
                    dve.tensor_tensor(p_s[:, 8], p_s[:, 5], late_cnt[:], ALU.mult).then_inc(S["p_step"], 1)
                    since(dve, S["p_exp"], q, 1, 1)
                    since(dve, S["p_step"], q, 4, 3)
                    dve.tensor_tensor(p_s[:, 9], p_s[:, 8], p_s[:, 7], ALU.add).then_inc(S["p_step"], 1)
                    since(dve, S["p_step"], q, 4, 4)
                    dve.reciprocal(p_s[:, 10], p_s[:, 9]).then_inc(S["p_recip"], 1)
                elif name == "pair_scale":
                    since(dve, S["p_recip"], q, 1, 1)
                    since(dve, S["p_g"], q, 1, 1)
                    dve.tensor_tensor(p_g, bank[6][:].rearrange("p (t d) -> p t d", t=T),
                                      p_s[:, 10].unsqueeze(2).broadcast_to([P, T, P]),
                                      ALU.mult).then_inc(S["p_gs"], 1)
                elif name == "l4_out":
                    since(dve, S["p_out"], q, 1, 1)
                    dve.scalar_tensor_tensor(out=x_all[:, q], in0=bank[7][:].rearrange("p (t d) -> p t d", t=T),
                                             scalar=1.0 / WS, in1=x_all[:, q], op0=ALU.mult,
                                             op1=ALU.add).then_inc(S["x4_done"], 1)

            run(dve, "dve", step, prepare)

        @block.tensor
        def _(pe):
            def turn_all(banks, src, sem, copied=None):
                for j in range(T):
                    if j >= len(banks):
                        pe.wait_ge(S[copied], j + 1 - len(banks))
                    for t in range(T):
                        ins = pe.transpose(banks[j % len(banks)][:, t * P:(t + 1) * P], src[:, t, j * P:(j + 1) * P],
                                           ident[:])
                    ins.then_inc(S[sem], 1)

            def prepare(name):
                if name == "turn":
                    pe.wait_ge(S["consts"], 1)
                    pe.wait_ge(S["adj_loaded"], 16)
                    turn_all(bank[0:4], adj_n, "adj_turned")
                elif name == "row_starts":
                    pe.wait_ge(S["row_counts"], 1)
                    for t in range(T):
                        for k in range(t):
                            pe.matmul(bank[6][:, t:t + 1], ones[:], small[:, 2, k:k + 1], start=(k == 0), stop=False)
                        ins = pe.matmul(bank[6][:, t:t + 1], tri[:], small[:, 2, t:t + 1], start=(t == 0), stop=True)
                    ins.then_inc(S["row_starts"], 1)
                elif name == "picked":
                    pe.wait_ge(S["pick_ready"], 1)
                    for t in range(T):
                        pe.matmul(bank[6][:], pick_t[:, t], q16[:, t], start=(t == 0), stop=(t == T - 1))
                    for t in range(T):
                        ins = pe.matmul(bank[7][:, t * P:(t + 1) * P], pick_t[:, t], ident16[:], start=True, stop=True)
                    ins.then_inc(S["picked"], 1)
                elif name == "spread":
                    pe.wait_ge(S["edge_values"], 1)
                    for t in range(T):
                        if t >= 2:
                            pe.wait_ge(S["spread_added"], t - 1)
                        pe.matmul(bank[6 + t % 2][:], wk3[:, 1, t * P:(t + 1) * P], wk3[:, 0], start=True,
                                  stop=True).then_inc(S["spread"], 1)
                elif name == "att_turn":
                    pe.wait_ge(S["att_rows"], 1)
                    turn_all(bank[6:8], wk2, "att_turned", "att_copied")
                elif name == "d_spread":
                    pe.wait_ge(S["d_diag"], 1)
                    pe.wait_ge(S["att_copied"], T)
                    pe.matmul(bank[6][:], ones[:], wk3[:, 1], start=True, stop=True).then_inc(S["d_spread"], 1)
                elif name == "lap_turn":
                    pe.wait_ge(S["lap_rows"], 1)
                    turn_all(bank[6:8], wk1, "lap_turned", "lap_copied")
                elif name == "lap_square":
                    pe.wait_ge(S["lap_copied"], T)
                    for j in range(T):
                        if j >= 2:
                            pe.wait_ge(S["cheb_copied"], j - 1)
                        for k in range(T):
                            ins = pe.matmul(bank[6 + j % 2][:], wk1[:, k, j * P:(j + 1) * P], wk2[:, k],
                                            start=(k == 0), stop=(k == T - 1))
                        ins.then_inc(S["lap_squared"], 1)

            def first(q, sem, count=1):
                if isinstance(q, int) and q == 0:
                    pe.wait_ge(S[sem], count)

            def mm3(o, lh, ll, rh, rl, first, last):
                pe.matmul(o, lh, rh, start=first, stop=False)
                pe.matmul(o, lh, rl, start=False, stop=False)
                return pe.matmul(o, ll, rh, start=False, stop=last)

            def by_weight(b, parts, bias=None):
                if bias is not None:
                    pe.matmul(b[:], ones16[:], bias_hl[:, bias:bias + 1].broadcast_to([P, T, P]), start=True,
                              stop=False)
                for t in range(T):
                    c = slice(t * P, (t + 1) * P)
                    for n, (f, w) in enumerate(parts):
                        last = n == len(parts) - 1 and (bias is None or t == T - 1)
                        ins = mm3(b[:, c], f[:, 0, c], f[:, 1, c], w_hl[:, 0, w], w_hl[:, 1, w],
                                  n == 0 and bias is None, last)
                return ins

            def over_nodes(b, h, m):
                for t in range(T):
                    ins = mm3(b[:], h[:, 0, t], h[:, 1, t], m[:, 0, t], m[:, 1, t], t == 0, t == T - 1)
                return ins

            def turn_parts(b, h):
                for part in range(2):
                    for t in range(T):
                        ins = pe.transpose(halves(b)[:, part, t * P:(t + 1) * P], h[:, part, t], ident16[:])
                return ins

            def passed(gap, sem, q, per):
                if not isinstance(q, int) or q + gap < B:
                    since(pe, sem, q + gap, per, per)

            def step(name, q):
                if name == "x_turn":
                    first(q, "adj_copied", 2)
                    normed(pe, "s", "y", q)
                    since(pe, S["x1_done"], q - GAP, 1, 0)
                    if isinstance(q, int) and q <= GAP:
                        since(pe, S["s_h1"], q, 1, 0)
                    for t in range(T):
                        ins = pe.transpose(bank[0][:, t * P:(t + 1) * P], y["s"][:, t], ident[:])
                    ins.then_inc(S["s_turned"], 1)
                elif name == "score_rows":
                    first(q, "score_weights")
                    since(pe, S["s_lo"], q, 1, 1)
                    since(pe, S["g_zr"], q - GAP, 1, 0)
                    if isinstance(q, int) and q <= GAP:
                        since(pe, S["s_max"], q, T, 0)
                    mm3(bank[1][:], dst_hl[:, 0], dst_hl[:, 1], s_fT[:, 0], s_fT[:, 1], True, True)
                    for t in range(T):
                        c = slice(t * P, (t + 1) * P)
                        ins = mm3(bank[0][:, t:t + 1], s_fT[:, 0, c], s_fT[:, 1, c], col_hl[:, 0, 0:1],
                                  col_hl[:, 1, 0:1], True, True)
                    ins.then_inc(S["s_rows"], 1)
                elif name == "project":
                    first(q, "biases")
                    since(pe, S["s_src"], q, 1, 1)
                    by_weight(bank[0], [(s_fT, WP)], 0).then_inc(S["s_proj"], 1)
                elif name in ("weigh", "weigh2"):
                    for t in (range(TH) if name == "weigh" else range(TH, T)):
                        since(pe, S["s_exp"], q, T, t + 1)
                        if t == 0:
                            normed(pe, "g", "y", q - 1)
                        elif t == 1:
                            since(pe, S["g_weighed"], q, T, 0)
                        else:
                            since(pe, S["g_weighed"], q, T, t - 1)
                        for j in range(T):
                            ins = pe.transpose(bank[2 + t % 2][:, j * P:(j + 1) * P], s_e[:, t, j * P:(j + 1) * P],
                                               ident[:])
                        ins.then_inc(S["g_turned"], 1)
                elif name == "heads":
                    since(pe, S["g_weighed"], q, T, T)
                    since(pe, S["s_h1"], q, 1, 1)
                    for t in range(T):
                        for j in range(T):
                            ins = pe.matmul(bank[2][:, t * P:(t + 1) * P], g_pt[:, j, t * P:(t + 1) * P], s_h1[:, j],
                                            start=(j == 0), stop=(j == T - 1))
                    ins.then_inc(S["g_heads"], 1)
                elif name == "gin":
                    first(q, "parts_ready", GIN)
                    since(pe, S["g_hglo"], q, 1, 1)
                    passed(GAP, S["s_max"], q, T)
                    over_nodes(bank[1], g_hghl, gin_t).then_inc(S["g_sum"], 1)
                elif name == "mlp_in":
                    since(pe, S["g_lo"], q, 1, 1)
                    passed(GAP, S["s_h1"], q, 1)
                    by_weight(bank[0], [(g_fT, WZ)], 1).then_inc(S["g_z"], 1)
                elif name == "mlp_turn":
                    normed(pe, "f", "y", q)
                    for t in range(T):
                        ins = pe.transpose(bank[1][:, t * P:(t + 1) * P], y["f"][:, t], ident[:])
                    ins.then_inc(S["g_zturned"], 1)
                elif name == "mlp_out":
                    since(pe, S["g_zlo"], q, 1, 1)
                    by_weight(bank[0], [(g_fT, WO2)], 2).then_inc(S["g_out"], 1)
                elif name == "off":
                    first(q, "parts_ready", ATT)
                    since(pe, S["m_lo"], q, 1, 1)
                    since(pe, S["n_hT"], q - GAP3, 1, 0)
                    if isinstance(q, int) and q <= GAP3:
                        since(pe, S["x2_done"], q, 1, 0)
                    over_nodes(bank[4], m_h, att_t).then_inc(S["m_off"], 1)
                elif name == "own":
                    first(q, "diag_ready")
                    since(pe, S["m_lo"], q, 1, 1)
                    since(pe, S["n_relu"], q - GAP3, 1, 0)
                    if isinstance(q, int) and q <= GAP3:
                        since(pe, S["m_own_lo"], q, 1, 0)
                    for t in range(T):
                        ins = mm3(bank[5][:, t * P:(t + 1) * P], m_h[:, 0, t], m_h[:, 1, t], att_d[:, 0, t],
                                  att_d[:, 1, t], True, True)
                    ins.then_inc(S["m_own"], 1)
                elif name == "l2_out":
                    since(pe, S["m_off_lo"], q, 1, 1)
                    since(pe, S["m_own_lo"], q, 1, 1)
                    by_weight(bank[4], [(m_2, L1A), (m_1, L1B)], 3).then_inc(S["m_mix"], 1)
                elif name == "lap":
                    first(q, "parts_ready", LAP)
                    since(pe, S["n_lo"], q, 1, 1)
                    passed(GAP3, S["x2_done"], q, 1)
                    over_nodes(bank[4], n_h, lap_t).then_inc(S["n_lap"], 1)
                elif name == "cheb":
                    first(q, "parts_ready", CHEB)
                    since(pe, S["n_lo"], q, 1, 1)
                    passed(GAP3, S["m_own_lo"], q, 1)
                    over_nodes(bank[5], n_h, cheb_t).then_inc(S["n_cheb"], 1)
                elif name == "l3_turn":
                    since(pe, S["n_lap_lo"], q, 1, 1)
                    turn_parts(bank[4], n_h).then_inc(S["n_turned"], 1)
                elif name == "l3_out":
                    since(pe, S["n_hT"], q, 1, 1)
                    since(pe, S["n_cheb_lo"], q, 1, 1)
                    by_weight(bank[5], [(n_hT, L2A), (n_1, L2B), (n_2, L2C)], 4).then_inc(S["n_mix"], 1)
                elif name == "l4_turn":
                    since(pe, S["p_lo"], q, 1, 1)
                    turn_parts(bank[6], p_h).then_inc(S["p_turned"], 1)
                elif name == "pair_rows":
                    since(pe, S["p_hT"], q, 1, 1)
                    mm3(bank[7][:], pair_hl[:, 0], pair_hl[:, 1], p_hT[:, 0], p_hT[:, 1], True,
                        True).then_inc(S["p_vec"], 1)
                elif name == "pair_feats":
                    since(pe, S["p_hT"], q, 1, 1)
                    by_weight(bank[6], [(p_hT, L3O)]).then_inc(S["p_g"], 1)
                elif name == "pair_cols":
                    since(pe, S["p_lv"], q, 1, 1)
                    for c in range(2):
                        ev = slice(c * H, (c + 1) * H, 2)
                        od = slice(c * H + 1, (c + 1) * H, 2)
                        mm3(bank[7][:, c:c + 1], p_hT[:, 0, ev], p_hT[:, 1, ev], col_hl[:, 0, 2:3],
                            col_hl[:, 1, 2:3], True, False)
                        ins = mm3(bank[7][:, c:c + 1], p_hT[:, 0, od], p_hT[:, 1, od], col_hl[:, 0, 3:4],
                                  col_hl[:, 1, 3:4], False, True)
                    ins.then_inc(S["p_vcol"], 1)
                elif name == "l4_out":
                    since(pe, S["p_lw"], q, 1, 1)
                    since(pe, S["p_exp"], q, 1, 1)
                    since(pe, S["p_gs"], q, 1, 1)
                    since(pe, S["p_g2lo"], q, 1, 1)
                    for t in range(T):
                        c = slice(t * P, (t + 1) * P)
                        mm3(bank[7][:, c], p_hT[:, 0, c], p_hT[:, 1, c], w_hl[:, 0, L3S], w_hl[:, 1, L3S], True,
                            False)
                        for j in range(T):
                            if t < TH:
                                ins = pe.matmul(bank[7][:, c], p_e[:, j, c], p_g[:, j], start=False,
                                                stop=(j == T - 1))
                            else:
                                r = slice((t - TH) * P, (t - TH + 1) * P)
                                pe.matmul(bank[7][:, c], late_mask[:, j, r], p_g2hl[:, 0, j], start=False, stop=False)
                                ins = pe.matmul(bank[7][:, c], late_mask[:, j, r], p_g2hl[:, 1, j], start=False,
                                                stop=(j == T - 1))
                    ins.then_inc(S["p_out"], 1)

            run(pe, "pe", step, prepare)


_INS = ['x', 'adj', 'L0_gnn_Wp', 'L0_gnn_bp', 'L0_gnn_a_src', 'L0_gnn_a_dst', 'L0_gnn_gat_g', 'L0_gnn_gat_b',
        'L0_gnn_eps', 'L0_gnn_W1', 'L0_gnn_b1', 'L0_gnn_mlp_g', 'L0_gnn_mlp_b', 'L0_gnn_W2', 'L0_gnn_b2', 'L1_gnn_W',
        'L1_gnn_e', 'L1_gnn_bias', 'L2_gnn_weight', 'L2_gnn_bias', 'L3_gnn_others_weight', 'L3_gnn_self_weight',
        'L3_gnn_att_weight']


def kernel(**inputs):
    import numpy as _np
    import concourse.bacc as _bacc
    from concourse import mybir as _mybir
    from concourse.bass_utils import run_bass_kernel_spmd as _run

    nc = _bacc.Bacc("TRN2", target_bir_lowering=False, num_devices=1)
    arrays, args = {}, []
    for name in _INS:
        a = _np.ascontiguousarray(inputs[name])
        arrays[f"in_{name}_dram"] = a
        args.append(nc.dram_tensor(f"in_{name}_dram", a.shape, _mybir.dt.from_np(a.dtype), kind="ExternalInput").ap())
    shape = inputs["x"].shape
    args.append(nc.dram_tensor("out_dram", shape, _mybir.dt.float32, kind="ExternalOutput").ap())
    build(nc, *args)
    r = _run(nc, [arrays], core_ids=[0])
    return r.results[0]["out_dram"]
```
